# Optimizing a Trainium2 kernel written in Bass

```python
import numpy as np
import jax
import jax.numpy as jnp

def _softmax(x, axis=-1):
    return jax.nn.softmax(x, axis=axis)

def _gelu(x):
    return jax.nn.gelu(x, approximate=True)

def _silu(x):
    return jax.nn.silu(x)

def _sigmoid(x):
    return jax.nn.sigmoid(x)

def _layernorm(x, axis=-1, eps=1e-05):
    m = jnp.mean(x, axis=axis, keepdims=True)
    v = jnp.var(x, axis=axis, keepdims=True)
    return (x - m) / jnp.sqrt(v + eps)

def _scatter_add(tgt, idx, src, axis=0):
    return tgt.at[idx].add(src)

def _segment_sum(src, seg, n):
    return jax.ops.segment_sum(src, seg, n)
kernel_name = 'mk_gnn_preln_d2_gnn_r8_310ea3'

def setup_inputs(seed: int=0):
    np.random.seed(seed)
    _w = jnp.asarray

    def _rec_inputs():
        import jax
        import jax.numpy as jnp
        _gk = jax.random.key(seed)
        x = -0.0005121 + 1.001 * jax.random.normal(jax.random.fold_in(_gk, 1), (6250, 64), jnp.float32)
        _s = jax.random.randint(jax.random.fold_in(_gk, 2), (100000,), 0, 6250, jnp.int32)
        _d = jax.random.randint(jax.random.fold_in(_gk, 3), (100000,), 0, 6250, jnp.int32)
        _loop = jnp.arange(6250, dtype=jnp.int32)
        src = jnp.concatenate([_s, _d, _loop])
        dst = jnp.concatenate([_d, _s, _loop])
        _o = jnp.argsort(dst, stable=True)
        src = src[_o]
        dst = dst[_o]
        return (x, src, dst)
    x, src, dst = _rec_inputs()

    def _L0_gnn_setup():
        import jax, jax.numpy as jnp
        import numpy as np
        N = 6250
        E = 100000
        IN_C, HID_C, OUT_C = (64, 128, 64)

        def _gin_conv(x, src, dst, Wa, ba, Wb, bb):
            agg = jax.ops.segment_sum(x[src], dst, num_segments=N)
            h = x + agg
            h = jax.nn.relu(h @ Wa + ba)
            return h @ Wb + bb
        key = jax.random.key(seed)
        ks = jax.random.split(key, 10)
        x = jax.random.normal(ks[0], (N, IN_C), dtype=jnp.float32)
        edge_index = jax.random.randint(ks[1], (2, E), 0, N, dtype=jnp.int64)
        s1 = 1.0 / np.sqrt(IN_C)
        s2 = 1.0 / np.sqrt(HID_C)
        W1 = jax.random.uniform(ks[2], (IN_C, HID_C), jnp.float32, -s1, s1)
        b1 = jax.random.uniform(ks[3], (HID_C,), jnp.float32, -s1, s1)
        W2 = jax.random.uniform(ks[4], (HID_C, HID_C), jnp.float32, -s2, s2)
        b2 = jax.random.uniform(ks[5], (HID_C,), jnp.float32, -s2, s2)
        W3 = jax.random.uniform(ks[6], (HID_C, HID_C), jnp.float32, -s2, s2)
        b3 = jax.random.uniform(ks[7], (HID_C,), jnp.float32, -s2, s2)
        W4 = jax.random.uniform(ks[8], (HID_C, OUT_C), jnp.float32, -s2, s2)
        b4 = jax.random.uniform(ks[9], (OUT_C,), jnp.float32, -s2, s2)
        return {'x': x, 'edge_index': edge_index, 'W1': W1, 'b1': b1, 'W2': W2, 'b2': b2, 'W3': W3, 'b3': b3, 'W4': W4, 'b4': b4}
    _L0_gnn_all = _L0_gnn_setup()
    _L0_gnn_in = {k: v for k, v in _L0_gnn_all.items() if k in ('W1', 'b1', 'W2', 'b2', 'W3', 'b3', 'W4', 'b4')}
    del _L0_gnn_all

    def _L1_gnn_setup():
        import jax, jax.numpy as jnp
        import numpy as np
        N, E = (12500, 200000)
        D_NODE, D_HID_M, D_OUT_M = (64, 128, 64)
        D_HID_U, D_OUT_U = (128, 64)

        def _glorot(key, shape):
            fan_in, fan_out = shape
            lim = (6.0 / (fan_in + fan_out)) ** 0.5
            return jax.random.uniform(key, shape, jnp.float32, -lim, lim)

        def _mlp3(x, W1, b1, W2, b2, W3, b3):
            h = jax.nn.relu(x @ W1 + b1)
            h = jax.nn.relu(h @ W2 + b2)
            return h @ W3 + b3
        key = jax.random.key(seed)
        ks = jax.random.split(key, 16)
        node_features = jax.random.normal(ks[0], (N, D_NODE), jnp.float32)
        edge_index = jax.random.randint(ks[1], (2, E), 0, N, jnp.int64)
        d_in_U = D_NODE + D_OUT_M
        return {'node_features': node_features, 'edge_index': edge_index, 'WM1': _glorot(ks[2], (D_NODE, D_HID_M)), 'bM1': jnp.zeros((D_HID_M,), jnp.float32), 'WM2': _glorot(ks[3], (D_HID_M, D_HID_M)), 'bM2': jnp.zeros((D_HID_M,), jnp.float32), 'WM3': _glorot(ks[4], (D_HID_M, D_OUT_M)), 'bM3': jnp.zeros((D_OUT_M,), jnp.float32), 'WU1': _glorot(ks[5], (d_in_U, D_HID_U)), 'bU1': jnp.zeros((D_HID_U,), jnp.float32), 'WU2': _glorot(ks[6], (D_HID_U, D_HID_U)), 'bU2': jnp.zeros((D_HID_U,), jnp.float32), 'WU3': _glorot(ks[7], (D_HID_U, D_OUT_U)), 'bU3': jnp.zeros((D_OUT_U,), jnp.float32)}
    _L1_gnn_all = _L1_gnn_setup()
    _L1_gnn_in = {k: v for k, v in _L1_gnn_all.items() if k in ('WM1', 'bM1', 'WM2', 'bM2', 'WM3', 'bM3', 'WU1', 'bU1', 'WU2', 'bU2', 'WU3', 'bU3')}
    del _L1_gnn_all
    return {'x': x, 'src': src, 'dst': dst, 'L0_gnn_W1': _L0_gnn_in['W1'], 'L0_gnn_b1': _L0_gnn_in['b1'], 'L0_gnn_W2': _L0_gnn_in['W2'], 'L0_gnn_b2': _L0_gnn_in['b2'], 'L0_gnn_W3': _L0_gnn_in['W3'], 'L0_gnn_b3': _L0_gnn_in['b3'], 'L0_gnn_W4': _L0_gnn_in['W4'], 'L0_gnn_b4': _L0_gnn_in['b4'], 'L1_gnn_WM1': _L1_gnn_in['WM1'], 'L1_gnn_bM1': _L1_gnn_in['bM1'], 'L1_gnn_WM2': _L1_gnn_in['WM2'], 'L1_gnn_bM2': _L1_gnn_in['bM2'], 'L1_gnn_WM3': _L1_gnn_in['WM3'], 'L1_gnn_bM3': _L1_gnn_in['bM3'], 'L1_gnn_WU1': _L1_gnn_in['WU1'], 'L1_gnn_bU1': _L1_gnn_in['bU1'], 'L1_gnn_WU2': _L1_gnn_in['WU2'], 'L1_gnn_bU2': _L1_gnn_in['bU2'], 'L1_gnn_WU3': _L1_gnn_in['WU3'], 'L1_gnn_bU3': _L1_gnn_in['bU3']}

def reference(x, src, dst, L0_gnn_W1, L0_gnn_b1, L0_gnn_W2, L0_gnn_b2, L0_gnn_W3, L0_gnn_b3, L0_gnn_W4, L0_gnn_b4, L1_gnn_WM1, L1_gnn_bM1, L1_gnn_WM2, L1_gnn_bM2, L1_gnn_WM3, L1_gnn_bM3, L1_gnn_WU1, L1_gnn_bU1, L1_gnn_WU2, L1_gnn_bU2, L1_gnn_WU3, L1_gnn_bU3):
    import jax
    import jax.numpy as jnp

    def _L0_gnn_ref(x, edge_index, W1, b1, W2, b2, W3, b3, W4, b4):
        import jax, jax.numpy as jnp
        import numpy as np
        N = 6250
        E = 100000
        IN_C, HID_C, OUT_C = (64, 128, 64)

        def _gin_conv(x, src, dst, Wa, ba, Wb, bb):
            agg = jax.ops.segment_sum(x[src], dst, num_segments=N)
            h = x + agg
            h = jax.nn.relu(h @ Wa + ba)
            return h @ Wb + bb
        src, dst = (edge_index[0], edge_index[1])
        h = jax.nn.relu(_gin_conv(x, src, dst, W1, b1, W2, b2))
        out = _gin_conv(h, src, dst, W3, b3, W4, b4)
        return out

    def _L1_gnn_ref(node_features, edge_index, WM1, bM1, WM2, bM2, WM3, bM3, WU1, bU1, WU2, bU2, WU3, bU3):
        import jax, jax.numpy as jnp
        import numpy as np
        N, E = (12500, 200000)
        D_NODE, D_HID_M, D_OUT_M = (64, 128, 64)
        D_HID_U, D_OUT_U = (128, 64)

        def _glorot(key, shape):
            fan_in, fan_out = shape
            lim = (6.0 / (fan_in + fan_out)) ** 0.5
            return jax.random.uniform(key, shape, jnp.float32, -lim, lim)

        def _mlp3(x, W1, b1, W2, b2, W3, b3):
            h = jax.nn.relu(x @ W1 + b1)
            h = jax.nn.relu(h @ W2 + b2)
            return h @ W3 + b3
        source, destination = (edge_index[0], edge_index[1])
        message = node_features[source]
        y = _mlp3(message, WM1, bM1, WM2, bM2, WM3, bM3)
        z = jax.ops.segment_sum(y, destination, num_segments=node_features.shape[0])
        return _mlp3(jnp.concatenate([node_features, z], axis=-1), WU1, bU1, WU2, bU2, WU3, bU3)
    edge_index = jnp.stack([src, dst])
    h = jnp.maximum(_layernorm(x, axis=-1), 0.0)
    x = x + _L0_gnn_ref(h, edge_index, L0_gnn_W1, L0_gnn_b1, L0_gnn_W2, L0_gnn_b2, L0_gnn_W3, L0_gnn_b3, L0_gnn_W4, L0_gnn_b4)
    h = jnp.maximum(_layernorm(x, axis=-1), 0.0)
    x = x + _L1_gnn_ref(h, edge_index, L1_gnn_WM1, L1_gnn_bM1, L1_gnn_WM2, L1_gnn_bM2, L1_gnn_WM3, L1_gnn_bM3, L1_gnn_WU1, L1_gnn_bU1, L1_gnn_WU2, L1_gnn_bU2, L1_gnn_WU3, L1_gnn_bU3)
    return x

_drawn_inputs = setup_inputs


def setup_inputs(seed=0):
    import zlib

    import numpy as np

    out = dict(_drawn_inputs(seed))
    spreads = {'L1_gnn_bM1': (0.0, 0.1),
     'L1_gnn_bM2': (0.0, 0.1),
     'L1_gnn_bM3': (0.0, 0.1),
     'L1_gnn_bU1': (0.0, 2.0),
     'L1_gnn_bU2': (0.0, 2.0),
     'L1_gnn_bU3': (0.0, 0.8)}
    factors = {'L0_gnn_b1': 6.666, 'L0_gnn_b2': 4.618, 'L0_gnn_b3': 58.192, 'L0_gnn_b4': 22.467}
    for name, (base, spread) in spreads.items():
        noise = np.random.default_rng([zlib.crc32(name.encode()), seed]).standard_normal(out[name].shape)
        drawn = base * np.exp(spread * noise) if base else spread * noise
        out[name] = jnp.asarray(drawn.astype(out[name].dtype))
    for name, factor in factors.items():
        out[name] = (out[name] * factor).astype(out[name].dtype)
    return out
```

```python
import numpy as np
import concourse.bass as bass
from concourse import mybir
from contextlib import ExitStack

FP32 = mybir.dt.float32
BF16 = mybir.dt.bfloat16
I32 = mybir.dt.int32
ALU = mybir.AluOpType
ACT = mybir.ActivationFunctionType
AX = mybir.AxisListType

P = 128
N = 6250
E = 206250
F = 64
H = 128
NW = -(-N // P)
NWP = -(-NW // 4) * 4
NB4 = NWP // 4
NT = -(-E // (P * P))
NCH = -(-E // P)
J = 38
COLS = NT * P + 40
XM = J - 1
SLOTS = -(-(NW + XM) // 4) * 4
XS = SLOTS - NW
MAIN_BLOCKS = -(-(NW + 3) // 4)
RANK_STEPS = 19
ROWS_DONE = 10
ENDS_DONE = 15
GMAX = NW * -(-NCH // J) + 3
RB = 8192
FAR = 64 * P
SKIP = NT * P
assert J * P < RB and NW <= 64


def group_pairs(eng, row):
    return eng.value_load(row[0:1, 2 * NW:2 * NW + 1], min_val=NW // 2 - 2, max_val=GMAX // 2 - 2) + 2


def sort_edges(nc, src, dst, lists_dram, meta_dram, window_dram, row):
    ctx = ExitStack()
    with ctx:
        def sb(name, shape, dt):
            return ctx.enter_context(nc.sbuf_tensor(name, shape, dt))

        def pb(name, shape, dt=FP32):
            return ctx.enter_context(nc.psum_tensor(name, shape, dt))

        def sem(name):
            return ctx.enter_context(nc.semaphore(name))

        key = sb("key", [P, COLS], FP32)
        tile_of = sb("tile_of", [P, COLS], BF16)
        low = sb("low", [P, 2, COLS], BF16)
        ident = sb("ident", [P, P], FP32)
        tri = sb("tri", [P, P], BF16)
        ones = sb("ones", [P, P], BF16)
        free = sb("free", [P, P], FP32)
        part = sb("part", [P, 1], FP32)
        part_k = sb("part_k", [P, 1], FP32)
        window_no = sb("window_no", [P, NW], FP32)
        minus64w = sb("minus64w", [P, NW], FP32)

        with ExitStack() as pro:
            def tmp(name, shape, dt):
                return pro.enter_context(nc.sbuf_tensor(name, shape, dt))

            srow = tmp("srow", [P, NT, P], I32)
            drow = tmp("drow", [P, NT, P], I32)
            bits = tmp("bits", [P, NT, P], I32)
            hi = tmp("hi", [P, NT, P], I32)
            rows = [tmp(n, [P, NT, P], FP32) for n in ("key_row", "tile_row", "slow_row", "dlow_row")]
            dhi = tmp("dhi", [P, NT, P], FP32)
            dmax = tmp("dmax", [P, NT], FP32)
            dmin = tmp("dmin", [P, NT], FP32)
            cid1 = tmp("cid1", [P, NT], FP32)
            wgrid = tmp("wgrid", [P, NW, NT], FP32)
            hit = tmp("hit", [P, 2, NW, NT], FP32)
            ends = tmp("ends", [P, 2, NW], FP32)
            span = tmp("span", [NW, 4], FP32)
            span_i = tmp("span_i", [NW, 2], I32)
            steps = tmp("steps", [NW, NCH // J + 1], FP32)
            stepped = tmp("stepped", [NW, NCH // J + 1], FP32)
            onesf = tmp("onesf", [NW, P], FP32)
            pairs_i = tmp("pairs_i", [1, 1], I32)
            pairs_f = tmp("pairs_f", [1, 1], FP32)
            pt = [pro.enter_context(nc.psum_tensor(f"pt{i}", [P, 4, P], FP32)) for i in range(4)]
            pe_ends = pro.enter_context(nc.psum_tensor("pe_ends", [NW, 2, P], FP32))
            pe_tot = pro.enter_context(nc.psum_tensor("pe_tot", [P, 1], FP32))

            loaded = pro.enter_context(nc.semaphore("edges_loaded"))
            padded = pro.enter_context(nc.semaphore("padding_set"))
            consts = pro.enter_context(nc.semaphore("constants_ready"))
            step = pro.enter_context(nc.semaphore("vector_steps"))
            turned = pro.enter_context(nc.semaphore("columns_turned"))
            copied = pro.enter_context(nc.semaphore("columns_copied"))
            ends_turned = pro.enter_context(nc.semaphore("ends_turned"))
            counted = pro.enter_context(nc.semaphore("groups_counted"))
            summed = pro.enter_context(nc.semaphore("groups_summed"))
            table_out = pro.enter_context(nc.semaphore("table_written"))
            table_in = pro.enter_context(nc.semaphore("table_read"))
            table_done = pro.enter_context(nc.semaphore("table_ready"))

            full = E // P
            in_last = full - (NT - 1) * P
            rest = E - full * P

            with nc.Block() as block:
                @block.sync
                def _(sp):
                    sp.wait_ge(padded, 2)
                    for edges, to in ((dst, drow), (src, srow)):
                        sp.dma_start(to[:, 0:NT - 1, :],
                                     edges[0:(NT - 1) * P * P].rearrange("(t c e) -> c t e", c=P, e=P)
                                     ).then_inc(loaded, 16)
                        sp.dma_start(to[0:in_last, NT - 1, :],
                                     edges[(NT - 1) * P * P:full * P].rearrange("(c e) -> c e", e=P)
                                     ).then_inc(loaded, 16)
                        if rest:
                            sp.dma_start(to[in_last:in_last + 1, NT - 1, 0:rest],
                                         edges[full * P:E].rearrange("(c e) -> c e", c=1)
                                         ).then_inc(loaded, 16)
                    sp.wait_ge(table_done, 2)
                    sp.dma_start(window_dram[0:2 * NW].rearrange("(w k) -> w k", k=2),
                                 span_i[:, :]).then_inc(table_out, 16)
                    sp.dma_start(window_dram[2 * NW:2 * NW + 1].rearrange("(w k) -> w k", k=1),
                                 pairs_i[:, :]).then_inc(table_out, 16)
                    sp.wait_ge(table_out, 32)
                    sp.dma_start(row[:, :], window_dram[:].rearrange("(o k) -> o k", o=1)
                                 ).then_inc(table_in, 16)
                    sp.wait_ge(table_in, 16)

                @block.gpsimd
                def _(pool):
                    nc.gpsimd.memset(drow[:, NT - 1, :], FAR).then_inc(padded, 1)
                    nc.gpsimd.memset(srow[:, NT - 1, :], 0).then_inc(padded, 1)
                    kw = dict(allow_small_or_imprecise_dtypes=True)
                    nc.gpsimd.iota(free[:, :], [[1, P]], 0, 0, **kw).then_inc(consts, 1)
                    nc.gpsimd.iota(part[:, :], [[0, 1]], 0, 1, **kw).then_inc(consts, 1)
                    nc.gpsimd.iota(window_no[:, :], [[1, NW]], 0, 0, **kw).then_inc(consts, 1)
                    nc.gpsimd.iota(minus64w[:, :], [[-64, NW]], 0, 0, **kw).then_inc(consts, 1)
                    nc.gpsimd.iota(cid1[:, :], [[P, NT]], 1, 1, **kw).then_inc(consts, 1)
                    nc.gpsimd.iota(wgrid[:, :, :], [[1, NW], [0, NT]], 0, 0, **kw).then_inc(consts, 1)
                    nc.gpsimd.iota(steps[:, :], [[J, NCH // J + 1]], 0, 0, **kw).then_inc(consts, 1)
                    nc.gpsimd.memset(ones[:, :], 1.0)
                    nc.gpsimd.memset(onesf[:, :], 1.0)
                    nc.gpsimd.memset(key[:, NT * P:COLS], float(FAR))
                    nc.gpsimd.memset(tile_of[:, NT * P:COLS], 0.0)
                    nc.gpsimd.memset(low[:, :, NT * P:COLS], 0.0).then_inc(consts, 1)

                @block.vector
                def _(dve):
                    done = [0]

                    def link(ins):
                        done[0] += 1
                        ins.then_inc(step, 1)
                        dve.wait_ge(step, done[0])

                    v = nc.vector
                    dve.wait_ge(consts, 8)
                    v.tensor_scalar(ident[:, :], free[:, :], part[:, 0:1], None, ALU.is_equal)
                    link(v.tensor_scalar(tri[:, :], free[:, :], part[:, 0:1], None, ALU.is_gt))
                    key_row, tile_row, slow_row, dlow_row = rows
                    dve.wait_ge(loaded, 96 if rest else 64)
                    link(v.tensor_scalar(hi[:, :, :], drow[:, :, :], 7, 6, ALU.logical_shift_right, ALU.logical_shift_left))
                    v.tensor_scalar(key_row[:, :, :], hi[:, :, :], 1.0, None, ALU.mult)
                    link(v.tensor_scalar(bits[:, :, :], srow[:, :, :], 7, None, ALU.logical_shift_right))
                    link(v.tensor_copy(tile_row[:, :, :], bits[:, :, :]))
                    link(v.tensor_scalar(dhi[:, :, :], hi[:, :, :], 1.0 / 64, None, ALU.mult))
                    link(v.tensor_tensor(key_row[:, :, :], key_row[:, :, :], tile_row[:, :, :], ALU.add))
                    link(v.tensor_scalar(bits[:, :, :], srow[:, :, :], 127, None, ALU.bitwise_and))
                    link(v.tensor_scalar(slow_row[:, :, :], bits[:, :, :], 1.0, None, ALU.add))
                    link(v.tensor_scalar(hi[:, :, :], drow[:, :, :], 127, None, ALU.bitwise_and))
                    link(v.tensor_scalar(dlow_row[:, :, :], hi[:, :, :], 1.0, None, ALU.add))
                    rows_done = done[0]
                    assert rows_done == ROWS_DONE
                    v.tensor_reduce(dmax[:, :], dhi[:, :, :], AX.X, ALU.max)
                    link(v.tensor_reduce(dmin[:, :], dhi[:, :, :], AX.X, ALU.min))
                    wide = [P, NW, NT]
                    v.tensor_tensor(hit[:, 0, :, :], dmax[:, None, :].broadcast_to(wide), wgrid[:, :, :], ALU.is_ge)
                    link(v.tensor_tensor(hit[:, 1, :, :], dmin[:, None, :].broadcast_to(wide), wgrid[:, :, :], ALU.is_le))
                    link(v.tensor_scalar(dmax[:, :], cid1[:, :], float(-1 - NT * P), None, ALU.add))
                    v.tensor_tensor(hit[:, 0, :, :], hit[:, 0, :, :], dmax[:, None, :].broadcast_to(wide), ALU.mult)
                    link(v.tensor_tensor(hit[:, 1, :, :], hit[:, 1, :, :], cid1[:, None, :].broadcast_to(wide), ALU.mult))
                    v.tensor_reduce(ends[:, 0, :], hit[:, 0, :, :], AX.X, ALU.min)
                    link(v.tensor_reduce(ends[:, 1, :], hit[:, 1, :, :], AX.X, ALU.max))
                    assert done[0] == ENDS_DONE
                    for t in range(NT):
                        dve.wait_ge(turned, t + 1)
                        c = slice(t * P, (t + 1) * P)
                        b = pt[t % 4]
                        v.tensor_copy(key[:, c], b[:, 0, :])
                        v.tensor_copy(tile_of[:, c], b[:, 1, :])
                        v.tensor_copy(low[:, :, c], b[:, 2:4, :]).then_inc(copied, 1)
                    dve.wait_ge(ends_turned, 2)
                    v.tensor_reduce(span[:, 0:1], pe_ends[:, 0, :], AX.X, ALU.min)
                    link(v.tensor_reduce(span[:, 1:2], pe_ends[:, 1, :], AX.X, ALU.max))
                    link(v.tensor_scalar(span[:, 0:1], span[:, 0:1], float(NT * P), None, ALU.add))
                    link(v.tensor_tensor(span[:, 2:3], span[:, 1:2], span[:, 0:1], ALU.subtract))
                    link(v.tensor_scalar(stepped[:, :], steps[:, :], span[:, 2:3], None, ALU.is_lt))
                    link(v.tensor_reduce(span[:, 3:4], stepped[:, :], AX.X, ALU.add))
                    link(v.tensor_scalar(span[:, 3:4], span[:, 3:4], 1.0, None, ALU.max))
                    v.tensor_copy(span_i[:, 0:1], span[:, 0:1])
                    v.tensor_copy(span_i[:, 1:2], span[:, 3:4]).then_inc(table_done, 1)
                    v.engine_nop().then_inc(counted, 1)
                    dve.wait_ge(summed, 1)
                    link(v.tensor_scalar(pairs_f[:, :], pe_tot[0:1, :], -3.0, None, ALU.add))
                    link(v.tensor_copy(pairs_i[:, :], pairs_f[:, :]))
                    v.tensor_scalar(pairs_i[:, :], pairs_i[:, :], 1, None, ALU.logical_shift_right).then_inc(table_done, 1)

                @block.tensor
                def _(pe):
                    pe.wait_ge(step, ROWS_DONE)
                    for t in range(NT):
                        if t >= 4:
                            pe.wait_ge(copied, t - 3)
                        for k in range(4):
                            last = nc.tensor.transpose(pt[t % 4][:, k, :], rows[k][:, t, :], ident[:, :])
                        last.then_inc(turned, 1)
                    pe.wait_ge(step, ENDS_DONE)
                    for k in range(2):
                        nc.tensor.transpose(pe_ends[:, k, :], ends[:, k, :], ident[:, :]).then_inc(ends_turned, 1)
                    pe.wait_ge(counted, 1)
                    nc.tensor.matmul(pe_tot[:, :], onesf[:, :], span[:, 3:4], start=True, stop=True).then_inc(summed, 1)

        def pair(name, shape, dt):
            return [sb(f"{name}{i}", shape, dt) for i in range(2)]

        grid_k = sb("grid_k", [P, P, J], BF16)
        grid_a = sb("grid_a", [P, NW, J], BF16)
        grid_x = sb("grid_x", [P, XS, J], BF16)
        st_key = sb("st_key", [P, 2, J], BF16)
        st_tile = sb("st_tile", [P, 2, J], BF16)
        st_low = sb("st_low", [P, 2, 2, J], BF16)
        st_win = sb("st_win", [P, 2, 1], FP32)
        bucket = pair("bucket", [P, NW, J], BF16)
        place = pair("place", [P, P, J], BF16)
        cargo = pair("cargo", [P, 2, SLOTS, J], BF16)
        extra = pair("extra", [P, XS, J], BF16)
        low_main = pair("low_main", [P, 2, J], BF16)
        resets = sb("resets", [P, NW, J], FP32)
        ranks = sb("ranks", [P, NW, J], FP32)
        picked = sb("picked", [P, NW, J], FP32)
        rank = sb("rank", [P, J], FP32)
        iv = sb("iv", [P, 5, J], I32)
        row_of = sb("row_of", [P, J], BF16)
        is_main = sb("is_main", [P, J], BF16)
        is_extra = sb("is_extra", [P, J], BF16)
        xslot = sb("xslot", [P, J], FP32)
        xslot_b = sb("xslot_b", [P, J], BF16)
        cnt = sb("cnt", [P, 6, NW], FP32)
        cnt_i = sb("cnt_i", [P, 2, NW], I32)
        ones_f = sb("ones_f", [P, NW], FP32)
        tile_rb = sb("tile_rb", [P, NW], FP32)
        ended = sb("ended", [P, NW], FP32)
        meta_f = sb("meta_f", [P, 2], FP32)
        meta_t = sb("meta_t", [P, 2], I32)
        meta = [sb(f"meta{i}", [P, 4], I32) for i in range(2)]
        sorted_sb = pair("sorted_sb", [P, 2, SLOTS], BF16)
        ps_base = [pb(f"ps_base{i}", [P, NW]) for i in range(2)]
        ps_cnt = [pb(f"ps_cnt{i}", [P, NW]) for i in range(2)]
        ps_sorted = [pb(f"ps_sorted{i}", [P, 2, SLOTS]) for i in range(2)]

        grids = sem("grids_ready")
        staged = sem("staged")
        stage_free_pool = sem("stage_free_pool")
        stage_free_dve = sem("stage_free_dve")
        bucketed = sem("bucketed")
        based = sem("based")
        rank_steps = sem("rank_steps")
        resets_set = sem("resets_set")
        extra_ready = sem("extra_ready")
        main_ready = sem("main_ready")
        placed = sem("placed")
        meta_ready = sem("meta_ready")
        cargoed = sem("cargoed")
        all_stored = sem("all_stored")
        permuted = sem("permuted")
        sorted_out = sem("sorted_copied")
        stored = [sem(f"stored{i}") for i in range(2)]
        meta_stored = [sem(f"meta_stored{i}") for i in range(2)]

        def over_groups(eng, body):
            n = group_pairs(eng, row)
            for b in range(2):
                body(b, b, True)
            with eng.Fori(1, n) as i:
                for b in range(2):
                    body(i * 2 + b, b, False)

        def over_groups_ahead(eng, ahead, body):
            n = group_pairs(eng, row)
            ahead(0, 0, True)
            ahead(1, 1, True)
            body(0, 0, True)
            ahead(2, 0, False)
            body(1, 1, True)
            with eng.Fori(1, n - 1) as i:
                for b in range(2):
                    ahead(i * 2 + b + 1, 1 - b, False)
                    body(i * 2 + b, b, False)
            ahead(n * 2 - 1, 1, False)
            body(n * 2 - 2, 0, False)
            body(n * 2 - 1, 1, False)

        with nc.Block() as block:
            @block.scalar
            def _(act):
                def stage(b, col, w):
                    nc.scalar.activation(st_key[:, bass.ds(b, 1), :].rearrange("p o j -> p (o j)"), key[:, bass.ds(col, J)], ACT.Identity,
                                         bias=minus64w[:, bass.ds(w, 1)])
                    nc.scalar.activation(st_tile[:, bass.ds(b, 1), :].rearrange("p o j -> p (o j)"), tile_of[:, bass.ds(col, J)], ACT.Copy)
                    nc.scalar.activation(st_win[:, bass.ds(b, 1), :].rearrange("p o j -> p (o j)"), window_no[:, bass.ds(w, 1)], ACT.Copy)
                    nc.scalar.activation(st_low[:, bass.ds(b, 1), :, :].rearrange("p o k j -> p (o k) j"), low[:, :, bass.ds(col, J)],
                                         ACT.Copy).then_inc(staged, 1)

                g = act.alloc_register("act_group")
                col = act.alloc_register("act_column")
                act.reg_mov(g, 0)
                with act.Fori(0, NW) as w:
                    col0 = act.value_load(row[0:1, bass.ds(w * 2, 1)], min_val=0, max_val=NT * P)
                    n = act.value_load(row[0:1, bass.ds(w * 2 + 1, 1)], min_val=1, max_val=NCH // J + 1)
                    act.reg_mov(col, col0)
                    with act.Fori(0, n) as i:
                        gs = act.snap(g, min_val=0, max_val=GMAX)
                        act.wait_ge(stage_free_pool, gs + 1)
                        act.wait_ge(stage_free_dve, gs + 1)
                        stage(gs & 1, act.snap(col, min_val=0, max_val=SKIP), w)
                        act.reg_add(g, g, 1)
                        act.reg_add(col, col, J)
                gs = act.snap(g, min_val=0, max_val=GMAX)
                act.wait_ge(stage_free_pool, gs + 1)
                act.wait_ge(stage_free_dve, gs + 1)
                stage(gs & 1, SKIP, NW - 1)

            @block.gpsimd
            def _(pool):
                kw = dict(allow_small_or_imprecise_dtypes=True)
                pool.sem_inc(stage_free_pool, 2)
                nc.gpsimd.iota(grid_a[:, :, :], [[1, NW], [0, J]], 0, 0, **kw).then_inc(grids, 1)
                nc.gpsimd.iota(grid_k[:, :, :], [[1, P], [0, J]], 0, 0, **kw).then_inc(grids, 1)
                nc.gpsimd.iota(grid_x[:, :, :], [[1, XS], [0, J]], 1, 0, **kw).then_inc(grids, 1)
                nc.gpsimd.iota(tile_rb[:, :], [[RB, NW]], 0, 0, **kw).then_inc(grids, 1)

                def cargo_of(g, b, first):
                    pool.wait_ge(extra_ready, g + 1)
                    if not first:
                        pool.wait_ge(permuted, g - 1)
                    for k in range(2):
                        last = nc.gpsimd.tensor_tensor(cargo[b][:, k, NW:SLOTS, :], extra[b][:, :, :],
                                                       st_low[:, b, k, None, :].broadcast_to([P, XS, J]), ALU.mult)
                    last.then_inc(stage_free_pool, 1)
                    pool.wait_ge(main_ready, g + 1)
                    for k in range(2):
                        last = nc.gpsimd.tensor_tensor(cargo[b][:, k, 0:NW, :], bucket[b][:, :, :],
                                                       low_main[b][:, k, None, :].broadcast_to([P, NW, J]), ALU.mult)
                    last.then_inc(cargoed, 1)

                over_groups(pool, cargo_of)

            @block.vector
            def _(dve):
                v = nc.vector
                dve.sem_inc(stage_free_dve, 2)
                v.memset(resets[:, :, :], 0.0)
                v.memset(ones_f[:, :], 1.0).then_inc(grids, 1)
                dve.wait_ge(grids, 5)

                def to_bucket(g, b, first):
                    dve.wait_ge(staged, g + 1)
                    if not first:
                        dve.wait_ge(based, g - 1)
                        dve.wait_ge(cargoed, g - 1)
                    v.tensor_tensor(bucket[b][:, :, :], grid_a[:, :, :],
                                    st_key[:, b, None, :].broadcast_to([P, NW, J]), ALU.is_equal).then_inc(bucketed, 1)

                def copy_out(g, b, first):
                    dve.wait_ge(permuted, g + 1)
                    if not first:
                        dve.wait_ge(stored[b], (g - b) * 8)
                    v.tensor_copy(sorted_sb[b][:, :, :], ps_sorted[b][:, :, :]).then_inc(sorted_out, 1)

                def rank_and_place(g, b, first, last=False):
                    done = [0]

                    def link(ins, on=None):
                        if on is None:
                            done[0] += 1
                            ins.then_inc(rank_steps, 1)
                            dve.wait_ge(rank_steps, g * RANK_STEPS + done[0])
                        else:
                            ins.then_inc(on, 1)
                            dve.wait_ge(on, g + 1)

                    dve.wait_ge(based, g + 1)
                    link(v.tensor_scalar(cnt_i[:, 0, :], ps_cnt[b][:, :], 128.0, -1.0, ALU.max, ALU.add))
                    link(v.tensor_scalar(cnt_i[:, 1, :], cnt_i[:, 0, :], 7, None, ALU.logical_shift_right))
                    link(v.tensor_copy(cnt[:, 0, :], cnt_i[:, 1, :]))
                    link(v.tensor_tensor_scan(cnt[:, 1, :], ones_f[:, :], cnt[:, 0, :], 0.0, ALU.mult, ALU.add))
                    link(v.tensor_tensor(cnt[:, 2, :], cnt[:, 1, :], cnt[:, 0, :], ALU.subtract))
                    link(v.scalar_tensor_tensor(cnt[:, 3, :], cnt[:, 2, :], float(RB), tile_rb[:, :], ALU.mult, ALU.add))
                    link(v.tensor_tensor(resets[:, :, 0], cnt[:, 3, :], ps_base[b][:, :], ALU.add), on=resets_set)
                    link(v.tensor_tensor_scan(ranks[:, :, :].rearrange("p a j -> p (a j)"),
                                                      resets[:, :, :].rearrange("p a j -> p (a j)"),
                                                      bucket[b][:, :, :].rearrange("p a j -> p (a j)"),
                                                      0.0, ALU.max, ALU.add))
                    link(v.tensor_tensor(picked[:, :, :], ranks[:, :, :], bucket[b][:, :, :], ALU.mult))
                    link(v.tensor_reduce(rank[:, :], picked[:, :, :].rearrange("p a j -> p j a"), AX.X, ALU.add))
                    link(v.tensor_scalar(iv[:, 0, :], rank[:, :], -1.0, None, ALU.add))
                    v.tensor_scalar(iv[:, 1, :], iv[:, 0, :], 127, None, ALU.bitwise_and)
                    v.tensor_scalar(iv[:, 4, :], iv[:, 0, :], RB - 1, None, ALU.bitwise_and)
                    link(v.tensor_scalar(iv[:, 2, :], iv[:, 0, :], 13, None, ALU.arith_shift_right))
                    link(v.tensor_scalar(iv[:, 3, :], iv[:, 4, :], 7, None, ALU.arith_shift_right))
                    v.tensor_copy(row_of[:, :], iv[:, 1, :])
                    v.tensor_scalar(is_main[:, :], iv[:, 3, :], 0.0, None, ALU.is_equal)
                    link(v.tensor_tensor(xslot[:, :], iv[:, 2, :], iv[:, 3, :], ALU.add))
                    v.scalar_tensor_tensor(is_extra[:, :], rank[:, :], 0.0, is_main[:, :], ALU.is_gt, ALU.is_gt)
                    link(v.tensor_tensor(xslot[:, :], xslot[:, :], st_tile[:, b, :], ALU.subtract))
                    link(v.tensor_tensor(xslot_b[:, :], xslot[:, :], is_extra[:, :], ALU.mult))
                    if not first:
                        dve.wait_ge(cargoed, g - 1)
                    v.tensor_tensor(extra[b][:, :, :], grid_x[:, :, :],
                                    xslot_b[:, None, :].broadcast_to([P, XS, J]), ALU.is_equal).then_inc(extra_ready, 1)
                    v.tensor_tensor(low_main[b][:, :, :], st_low[:, b, :, :],
                                    is_main[:, None, :].broadcast_to([P, 2, J]), ALU.mult).then_inc(main_ready, 1)
                    if not last:
                        to_bucket(g + 1, 1 - b, b == 0 and first)
                    if not first:
                        dve.wait_ge(permuted, g - 1)
                    v.tensor_tensor(place[b][:, :, :], grid_k[:, :, :],
                                    row_of[:, None, :].broadcast_to([P, P, J]), ALU.is_equal).then_inc(placed, 1)
                    link(v.tensor_scalar(ended[:, :], cnt[:, 1, :], part[:, 0:1], None, ALU.is_le))
                    link(v.tensor_reduce(meta_f[:, 0:1], ended[:, :], AX.X, ALU.add))
                    v.tensor_copy(meta_t[:, 0:1], cnt[:, 1, NW - 1:NW])
                    link(v.tensor_scalar(meta_f[:, 1:2], meta_f[:, 0:1], float(NW - 1), None, ALU.min))
                    link(v.tensor_scalar(meta_t[:, 1:2], meta_t[:, 0:1], 2, None, ALU.logical_shift_right))
                    if not first:
                        dve.wait_ge(meta_stored[b], (g - b) * 8)
                    v.tensor_copy(meta[b][:, 2:3], st_win[:, b, :])
                    v.tensor_copy(meta[b][:, 3:4], st_win[:, b, :]).then_inc(stage_free_dve, 1)
                    v.tensor_copy(meta[b][:, 0:1], meta_f[:, 1:2])
                    v.tensor_scalar(meta[b][:, 1:2], meta_t[:, 1:2], float(MAIN_BLOCKS), None, ALU.add).then_inc(meta_ready, 1)
                    assert done[0] == RANK_STEPS
                    if not (first and b == 0):
                        copy_out(g - 1, 1 - b, first)

                n = group_pairs(dve, row)
                to_bucket(0, 0, True)
                rank_and_place(0, 0, True)
                rank_and_place(1, 1, True)
                with dve.Fori(1, n - 1) as i:
                    rank_and_place(i * 2, 0, False)
                    rank_and_place(i * 2 + 1, 1, False)
                rank_and_place(n * 2 - 2, 0, False)
                rank_and_place(n * 2 - 1, 1, False, last=True)
                copy_out(n * 2 - 1, 1, False)

            @block.tensor
            def _(pe):
                def base(g, b, first):
                    pe.wait_ge(bucketed, g + 1)
                    if not first:
                        pe.wait_ge(resets_set, g - 1)
                    for j in range(J):
                        nc.tensor.matmul(ps_base[b][:, :], tri[:, :], bucket[b][:, :, j],
                                         start=(j == 0), stop=(j == J - 1))
                    for j in range(J):
                        last = nc.tensor.matmul(ps_cnt[b][:, :], ones[:, :], bucket[b][:, :, j],
                                                start=(j == 0), stop=(j == J - 1))
                    last.then_inc(based, 1)

                def permute(g, b, first):
                    pe.wait_ge(placed, g + 1)
                    pe.wait_ge(cargoed, g + 1)
                    pe.wait_ge(stage_free_pool, g + 3)
                    if not first:
                        pe.wait_ge(sorted_out, g - 1)
                    for j in range(J):
                        last = nc.tensor.matmul(ps_sorted[b][:, :, :], place[b][:, :, j], cargo[b][:, :, :, j],
                                                start=(j == 0), stop=(j == J - 1))
                    last.then_inc(permuted, 1)

                over_groups_ahead(pe, base, permute)

            @block.sync
            def _(sp):
                def store(g, b, first):
                    sp.wait_ge(sorted_out, g + 1)
                    sp.dma_start(lists_dram[bass.ds(g, 1), :, :].rearrange("o p k -> (o p) k"),
                                 sorted_sb[b][:, :, :].rearrange("p k s -> p (k s)")).then_inc(stored[b], 16)
                    sp.wait_ge(meta_ready, g + 1)
                    sp.dma_start(meta_dram[bass.ds(g, 1), :, :].rearrange("o p k -> (o p) k"),
                                 meta[b][:, :]).then_inc(meta_stored[b], 16)

                over_groups(sp, store)
                n = group_pairs(sp, row)
                for b in range(2):
                    sp.wait_ge(stored[b], n * 16)
                    sp.wait_ge(meta_stored[b], n * 16)
                sp.sem_inc(all_stored, 1)


def aggregate(nc, tag, lists_dram, meta_dram, row, parts, width, acc):
    ctx = ExitStack()
    with ctx:
        def sb(name, shape, dt):
            return ctx.enter_context(nc.sbuf_tensor(f"{tag}_{name}", shape, dt))

        def sem(name):
            return ctx.enter_context(nc.semaphore(f"{tag}_{name}"))

        RING = 4
        B = MAIN_BLOCKS
        LAST, RARE = RING, RING + 1
        assert (B - 1) % RING == 0
        LAG = 2
        grid4 = sb("grid4", [P, P, 4], BF16)
        lists = [sb(f"lists{i}", [P, 2, SLOTS], BF16) for i in range(2)]
        metas = [sb(f"metas{i}", [1, P, 4], I32) for i in range(2)]
        hot = [sb(f"hot{i}", [P, 2, P, 4], BF16) for i in range(RING + 2)]
        cnts = [sb(f"cnts{i}", [P, 4, P], BF16) for i in range(RING + 2)]
        total = sb("total", [P, width], FP32)
        ps_cnts = [ctx.enter_context(nc.psum_tensor(f"{tag}_ps_cnts{i}", [P, 4, P], FP32)) for i in range(RING + 2)]
        ps_out = [ctx.enter_context(nc.psum_tensor(f"{tag}_ps_out{i}", [P, 3, width], FP32)) for i in range(2)]

        grid_ready = sem("grid_ready")
        list_in = [sem(f"list_in{i}") for i in range(2)]
        meta_in = [sem(f"meta_in{i}") for i in range(2)]
        hot_ready = sem("hot_ready")
        cnt_ready = sem("cnt_ready")
        cnt_copied = sem("cnt_copied")
        cnt_used = sem("cnt_used")
        rare_hot = sem("rare_hot")
        rare_ready = sem("rare_ready")
        rare_copied = sem("rare_copied")
        rare_used = sem("rare_used")
        group_out = sem("group_out")
        totalled = sem("totalled")
        added = sem("added")
        act_read = sem("act_read_meta")
        meta_seen = sem("meta_seen")

        def over_groups(eng, body):
            n = group_pairs(eng, row)
            for b in range(2):
                body(b, b)
            with eng.Fori(1, n) as i:
                for b in range(2):
                    body(i * 2 + b, b)
            return n

        def slot(k):
            return k % RING if k < B - 1 else LAST

        def earlier(g, k):
            if k == B - 1:
                return g * B
            return g * B + k - RING + (1 if k >= RING else 0)

        def unused(g, k):
            return is_static(g, 1) and (k < RING or k == B - 1)

        def is_static(g, upto):
            return isinstance(g, int) and g < upto

        def blocks_of(eng, g, b):
            return eng.value_load(metas[b][0:1, 0, 1:2], min_val=B, max_val=SLOTS // 4)

        def rare(eng, nb, counter, body):
            with eng.If(nb > B):
                with eng.Fori(B, nb) as t:
                    body(t, eng.snap(counter, min_val=0, max_val=1 << 20))
                    eng.reg_add(counter, counter, 1)

        with nc.Block() as block:
            @block.gpsimd
            def _(pool):
                nc.gpsimd.iota(grid4[:, :, :], [[1, P], [0, 4]], 1, 0,
                               allow_small_or_imprecise_dtypes=True).then_inc(grid_ready, 1)

            @block.sync
            def _(sp):
                def load(g, b):
                    if not is_static(g, 2):
                        sp.wait_ge(added, g - 1)
                        sp.wait_ge(act_read, g - 1)
                    sp.dma_start(lists[b][:, :, :].rearrange("p k s -> p (k s)"),
                                 lists_dram[bass.ds(g, 1), :, :].rearrange("o p k -> (o p) k")).then_inc(list_in[b], 16)
                    sp.dma_start(metas[b][:, :, :].rearrange("o p k -> o (p k)"),
                                 meta_dram[bass.ds(g, 1), :, :].rearrange("o p k -> o (p k)")).then_inc(meta_in[b], 16)

                over_groups(sp, load)

            @block.vector
            def _(dve):
                v = nc.vector
                counter = dve.alloc_register(f"{tag}_dve_rare")
                dve.reg_mov(counter, 1)
                dve.wait_ge(grid_ready, 1)

                def one_hots(to, b, columns):
                    return v.tensor_tensor(to[:, :, :, :], grid4[:, None, :, :].broadcast_to([P, 2, P, 4]),
                                           lists[b][:, :, None, columns].broadcast_to([P, 2, P, 4]), ALU.is_equal)

                def add_group(g, b, w):
                    dve.wait_ge(group_out, g + 1)
                    v.tensor_reduce(total[:, :], ps_out[b][:, :, :].rearrange("p t f -> p f t"), AX.X,
                                    ALU.add).then_inc(totalled, 1)
                    dve.wait_ge(totalled, g + 1)
                    to = acc[:, bass.ds(w, 1), :].rearrange("p o f -> p (o f)")
                    v.tensor_tensor(to, to, total[:, :], ALU.add).then_inc(added, 1)

                wreg = dve.alloc_register(f"{tag}_dve_window")

                def group(g, b):
                    dve.wait_ge(list_in[b], (g - b) * 8 + 16)
                    dve.wait_ge(meta_in[b], (g - b) * 8 + 16)
                    dve.sem_inc(meta_seen, 1)
                    nb = blocks_of(dve, g, b)
                    for k in range(B):
                        if not unused(g, k):
                            dve.wait_ge(cnt_ready, earlier(g, k))
                        one_hots(hot[slot(k)], b,
                                 slice(4 * k, 4 * k + 4)).then_inc(hot_ready, 1)
                        if k == LAG:
                            def more(t, m):
                                dve.wait_ge(rare_ready, m)
                                one_hots(hot[RARE], b, bass.ds(t * 4, 4)).then_inc(rare_hot, 1)
                            rare(dve, nb, counter, more)
                        if k == LAG + 3 and not is_static(g, 1):
                            add_group(g - 1, 1 - b, dve.snap(wreg, min_val=0, max_val=NW - 1))
                    w = dve.value_load(metas[b][0:1, 0, 2:3], min_val=0, max_val=NW - 1)
                    dve.reg_mov(wreg, w)

                n = over_groups(dve, group)
                add_group(n * 2 - 1, 1, dve.snap(wreg, min_val=0, max_val=NW - 1))

            @block.tensor
            def _(pe):
                counter = pe.alloc_register(f"{tag}_pe_rare")
                pe.reg_mov(counter, 1)
                pe.sem_inc(rare_ready, 1)
                pe.sem_inc(rare_used, 1)

                def count(to, of):
                    for c in range(4):
                        last = nc.tensor.matmul(to[:, c, :], of[:, 0, :, c], of[:, 1, :, c], start=True, stop=True)
                    return last

                def gather(to, of, tiles, first, last_one):
                    for c in range(4):
                        last = nc.tensor.matmul(to[:, :, :], of[:, c, :], tiles[c],
                                                start=(first and c == 0), stop=(last_one and c == 3))
                    return last

                def use(g, b, k, tiles):
                    pe.wait_ge(cnt_copied, g * B + k + 1)
                    if k == 0 and not is_static(g, 2):
                        pe.wait_ge(added, g - 1)
                    gather(ps_out[b], cnts[slot(k)], tiles, k == 0, k == B - 1).then_inc(
                        group_out if k == B - 1 else cnt_used, 1)

                def main_tiles(k):
                    return [parts[:, 4 * k + c, :, :] for c in range(4)]

                areg = [pe.alloc_register(f"{tag}_pe_tile{x}") for x in range(3)]

                def last_tiles():
                    return [parts[:, NW - 1, :, :]] + [
                        parts[:, bass.ds(pe.snap(r, min_val=0, max_val=NW - 1), 1), :, :].rearrange("p o t f -> p (o t) f")
                        for r in areg]

                def group(g, b):
                    pe.wait_ge(meta_in[b], (g - b) * 8 + 16)
                    pe.sem_inc(meta_seen, 1)
                    nb = blocks_of(pe, g, b)
                    for k in range(B):
                        pe.wait_ge(hot_ready, g * B + k + 1)
                        if not unused(g, k):
                            pe.wait_ge(cnt_copied, earlier(g, k))
                        count(ps_cnts[slot(k)], hot[slot(k)]).then_inc(cnt_ready, 1)
                        if k >= LAG:
                            use(g, b, k - LAG, main_tiles(k - LAG))
                        elif not is_static(g, 1):
                            k0 = B - LAG + k
                            use(g - 1, 1 - b, k0, main_tiles(k0) if k0 < B - 1 else last_tiles())
                        if k == LAG:
                            def more(t, m):
                                pe.wait_ge(rare_hot, m)
                                count(ps_cnts[RARE], hot[RARE]).then_inc(rare_ready, 1)
                                tiles = []
                                for c in range(4):
                                    a = pe.value_load(metas[b][0:1, bass.ds(t * 4 + (c - NW), 1), 0:1].rearrange("o s k -> o (s k)"),
                                                      min_val=0, max_val=NW - 1)
                                    tiles.append(parts[:, bass.ds(a, 1), :, :].rearrange("p o t f -> p (o t) f"))
                                pe.wait_ge(rare_copied, m)
                                gather(ps_out[b], cnts[RARE], tiles, False, False).then_inc(rare_used, 1)
                            rare(pe, nb, counter, more)
                    for x in range(3):
                        a = pe.value_load(metas[b][0:1, x, 0:1], min_val=0, max_val=NW - 1)
                        pe.reg_mov(areg[x], a)

                n = over_groups(pe, group)
                for k in range(B - LAG, B):
                    use(n * 2 - 1, 1, k, main_tiles(k) if k < B - 1 else last_tiles())

            @block.scalar
            def _(act):
                counter = act.alloc_register(f"{tag}_act_rare")
                act.reg_mov(counter, 1)

                def group(g, b):
                    act.wait_ge(meta_in[b], (g - b) * 8 + 16)
                    act.sem_inc(meta_seen, 1)
                    nb = blocks_of(act, g, b)
                    for k in range(B):
                        act.wait_ge(cnt_ready, g * B + k + 1)
                        if k == B - 1 and not is_static(g, 1):
                            act.wait_ge(group_out, g)
                        elif k < B - 1 and not unused(g, k):
                            act.wait_ge(cnt_used, g * (B - 1) + k - RING + 1)
                        nc.scalar.activation(cnts[slot(k)][:, :, :], ps_cnts[slot(k)][:, :, :],
                                             ACT.Copy).then_inc(cnt_copied, 1)
                        if k == LAG:
                            def more(t, m):
                                act.wait_ge(rare_ready, m + 1)
                                act.wait_ge(rare_used, m)
                                nc.scalar.activation(cnts[RARE][:, :, :], ps_cnts[RARE][:, :, :],
                                                     ACT.Copy).then_inc(rare_copied, 1)
                            rare(act, nb, counter, more)
                    act.sem_inc(act_read, 1)

                over_groups(act, group)


def normalize(nc, tag, x, out, scratch):
    with ExitStack() as ctx:
        stats = ctx.enter_context(nc.sbuf_tensor(f"{tag}_stats", [P, 4, NWP], FP32))
        eps = ctx.enter_context(nc.sbuf_tensor(f"{tag}_eps", [P, 1], FP32))
        step = ctx.enter_context(nc.semaphore(f"{tag}_normalize_steps"))
        rooted = ctx.enter_context(nc.semaphore(f"{tag}_rooted"))
        with nc.Block() as block:
            @block.vector
            def _(dve):
                v = nc.vector
                done = [0]

                def link(ins):
                    done[0] += 1
                    ins.then_inc(step, 1)
                    dve.wait_ge(step, done[0])

                shape = [P, NWP, F]
                v.memset(eps[:, :], 1e-5)
                link(v.tensor_reduce(stats[:, 0, :], x, AX.X, ALU.add))
                link(v.tensor_scalar(stats[:, 1, :], stats[:, 0, :], 1.0 / F, None, ALU.mult))
                link(v.tensor_tensor(out, x, stats[:, 1, :, None].broadcast_to(shape), ALU.subtract))
                link(v.tensor_tensor(scratch, out, out, ALU.mult))
                link(v.tensor_reduce(stats[:, 2, :], scratch, AX.X, ALU.add))
                dve.wait_ge(rooted, 1)
                link(v.reciprocal(stats[:, 0, :], stats[:, 3, :]))
                link(v.scalar_tensor_tensor(out, out, 0.0, stats[:, 0, :, None].broadcast_to(shape), ALU.max, ALU.mult))

            @block.scalar
            def _(act):
                act.wait_ge(step, 5)
                nc.scalar.activation(stats[:, 3, :], stats[:, 2, :], ACT.Sqrt, bias=eps[:, 0:1], scale=1.0 / F).then_inc(rooted, 1)


def split_parts(nc, tag, x, parts, scratch):
    with ExitStack() as ctx:
        half = [ctx.enter_context(nc.semaphore(f"{tag}_split{i}")) for i in range(4)]
        with nc.Block() as block:
            @block.scalar
            def _(act):
                nc.scalar.activation(parts[:, :, 0, :], x, ACT.Copy).then_inc(half[0], 1)
                act.wait_ge(half[1], 1)
                nc.scalar.activation(parts[:, :, 1, :], scratch, ACT.Copy).then_inc(half[2], 1)

            @block.vector
            def _(dve):
                v = nc.vector
                dve.wait_ge(half[0], 1)
                v.tensor_tensor(scratch, x, parts[:, :, 0, :], ALU.subtract).then_inc(half[1], 1)
                dve.wait_ge(half[2], 1)
                dve.wait_ge(half[1], 1)
                v.tensor_tensor(parts[:, :, 2, :], scratch, parts[:, :, 1, :], ALU.subtract).then_inc(half[3], 1)
                dve.wait_ge(half[3], 1)


def perceptron(nc, tag, ident, x, hidden, last, width, finish):
    with ExitStack() as ctx:
        k = x.shape[2]
        xt = [ctx.enter_context(nc.sbuf_tensor(f"{tag}_xt{i}", [k, 4 * P], FP32)) for i in range(2)]
        hid = [[ctx.enter_context(nc.sbuf_tensor(f"{tag}_hid{i}_{n}", [P, 4 * P], FP32)) for n in range(len(hidden))]
               for i in range(2)]
        ps_t = [ctx.enter_context(nc.psum_tensor(f"{tag}_ps_t{i}", [k, 4, P], FP32)) for i in range(2)]
        ps_h = [ctx.enter_context(nc.psum_tensor(f"{tag}_ps_h{i}", [P, 4 * P], FP32)) for i in range(2)]
        ps_f = [ctx.enter_context(nc.psum_tensor(f"{tag}_ps_f{i}", [P, 4, width], FP32)) for i in range(2)]
        xs = [ctx.enter_context(nc.sbuf_tensor(f"{tag}_xs{i}", [P, 4, k], FP32)) for i in range(2)]
        fetched = ctx.enter_context(nc.semaphore(f"{tag}_fetched"))
        seen = ctx.enter_context(nc.semaphore(f"{tag}_fetched_seen"))
        turned = ctx.enter_context(nc.semaphore(f"{tag}_turned"))
        copied = ctx.enter_context(nc.semaphore(f"{tag}_turned_copied"))
        product = [ctx.enter_context(nc.semaphore(f"{tag}_product{n}")) for n in range(len(hidden))]
        relued = [ctx.enter_context(nc.semaphore(f"{tag}_relued{n}")) for n in range(len(hidden))]
        last_product = ctx.enter_context(nc.semaphore(f"{tag}_last_product"))
        finished = ctx.enter_context(nc.semaphore(f"{tag}_finished"))
        finishing = ctx.enter_context(nc.semaphore(f"{tag}_finishing"))

        def over_batches(eng, stages):
            with eng.Fori(0, NB4 // 2) as i:
                for s in stages:
                    for b in range(2):
                        s(i * 2 + b, b)
            if NB4 % 2:
                for s in stages:
                    s(NB4 - 1, 0)

        with nc.Block() as block:
            @block.tensor
            def _(pe):
                def turn(n, b):
                    pe.wait_ge(fetched, n + 1)
                    pe.sem_inc(seen, 1)
                    for c in range(4):
                        last_ = nc.tensor.transpose(ps_t[b][:, c, :], xs[b][:, c, :], ident[:, :])
                    last_.then_inc(turned, 1)

                def layer(m):
                    def run(n, b):
                        if m:
                            pe.wait_ge(relued[m - 1], n + 1)
                        else:
                            pe.wait_ge(copied, n + 3)
                        nc.tensor.matmul(ps_h[b][:, :], hidden[m][0], (hid[b][m - 1] if m else xt[b])[:, :],
                                         start=True, stop=True).then_inc(product[m], 1)
                    return run

                def back(n, b):
                    pe.wait_ge(relued[-1], n + 1)
                    pe.wait_ge(finished, n + 1)
                    for c in range(4):
                        last_ = nc.tensor.matmul(ps_f[b][:, c, :], hid[b][-1][:, c * P:(c + 1) * P], last,
                                                 start=True, stop=True)
                    last_.then_inc(last_product, 1)

                over_batches(pe, [turn] + [layer(m) for m in range(len(hidden))] + [back])

            @block.gpsimd
            def _(pool):
                pool.sem_inc(copied, 2)

                def fetch(n, b):
                    pool.wait_ge(copied, n + 1)
                    nc.gpsimd.tensor_copy(xs[b][:, :, :], x[:, bass.ds(n * 4, 4), :]).then_inc(fetched, 1)

                over_batches(pool, [fetch])

            @block.scalar
            def _(act):
                def relu(m):
                    def run(n, b):
                        act.wait_ge(product[m], n + 1)
                        nc.scalar.activation(hid[b][m][:, :], ps_h[b][:, :], ACT.Relu, bias=hidden[m][1]).then_inc(relued[m], 1)
                    return run

                over_batches(act, [relu(m) for m in range(len(hidden))])

            @block.vector
            def _(dve):
                dve.sem_inc(finished, 2)

                def copy(n, b):
                    dve.wait_ge(turned, n + 1)
                    nc.vector.tensor_copy(xt[b][:, :].rearrange("p (c e) -> p c e", c=4), ps_t[b][:, :, :]).then_inc(copied, 1)

                def end(n, b):
                    dve.wait_ge(last_product, n + 1)
                    finish(dve, n, ps_f[b], finishing).then_inc(finished, 1)

                over_batches(dve, [copy, end])


_INS = ["x", "src", "dst",
        "L0_gnn_W1", "L0_gnn_b1", "L0_gnn_W2", "L0_gnn_b2", "L0_gnn_W3", "L0_gnn_b3", "L0_gnn_W4", "L0_gnn_b4",
        "L1_gnn_WM1", "L1_gnn_bM1", "L1_gnn_WM2", "L1_gnn_bM2", "L1_gnn_WM3", "L1_gnn_bM3",
        "L1_gnn_WU1", "L1_gnn_bU1", "L1_gnn_WU2", "L1_gnn_bU2", "L1_gnn_WU3", "L1_gnn_bU3"]


def gnn(nc, a, out):
    with ExitStack() as ctx:
        def sb(name, shape, dt=FP32):
            return ctx.enter_context(nc.sbuf_tensor(name, shape, dt))

        lists_dram = nc.dram_tensor("sorted_lists", [GMAX, P, 2 * SLOTS], BF16).ap()
        meta_dram = nc.dram_tensor("group_tables", [GMAX, P, 4], I32).ap()
        window_dram = nc.dram_tensor("window_table", [2 * NW + 1], I32).ap()

        row = sb("row", [1, 2 * NW + 1], I32)
        ident = sb("identity", [P, P])
        xres = sb("xres", [P, NWP, F])
        feat = sb("feat", [P, NWP, H])

        weight, bias = {}, {}
        LAST = ("L0_gnn_b2", "L0_gnn_b4", "L1_gnn_bM3", "L1_gnn_bU3")
        for name in _INS[3:]:
            if a[name].shape.__len__() == 2:
                weight[name] = sb("w_" + name, list(a[name].shape))
            elif name in LAST:
                bias[name] = sb("b_" + name, [P, a[name].shape[0]])
            else:
                bias[name] = sb("b_" + name, [a[name].shape[0], 1])

        whole = N // P
        loaded = ctx.enter_context(nc.semaphore("inputs_loaded"))
        zeroed = ctx.enter_context(nc.semaphore("padding_zeroed"))
        idx = ctx.enter_context(nc.semaphore("index_ready"))
        with nc.sbuf_tensor("ramp", [P, P], FP32) as ramp, nc.sbuf_tensor("lane", [P, 1], FP32) as lane, nc.Block() as block:
            @block.sync
            def _(sp):
                loads = 0
                for name in _INS[3:]:
                    if name in weight:
                        sp.dma_start(weight[name][:, :], a[name]).then_inc(loaded, 16)
                    elif name in LAST:
                        w = a[name].shape[0]
                        sp.dma_start(bias[name][:, :], a[name].rearrange("(o f) -> o f", o=1).broadcast_to([P, w])
                                     ).then_inc(loaded, 16)
                    else:
                        sp.dma_start(bias[name][:, :], a[name].rearrange("(f o) -> f o", o=1)).then_inc(loaded, 16)
                    loads += 1
                sp.wait_ge(zeroed, 1)
                sp.dma_start(xres[:, 0:whole, :], a["x"][0:whole * P, :].rearrange("(w p) f -> p w f", p=P)).then_inc(loaded, 16)
                sp.dma_start(xres[0:N - whole * P, whole, :], a["x"][whole * P:N, :]).then_inc(loaded, 16)
                sp.wait_ge(loaded, 16 * (loads + 2))

            @block.gpsimd
            def _(pool):
                nc.gpsimd.memset(xres[:, whole:NWP, :], 0.0).then_inc(zeroed, 1)
                kw = dict(allow_small_or_imprecise_dtypes=True)
                nc.gpsimd.iota(ramp[:, :], [[1, P]], 0, 0, **kw).then_inc(idx, 1)
                nc.gpsimd.iota(lane[:, :], [[0, 1]], 0, 1, **kw).then_inc(idx, 1)

            @block.vector
            def _(dve):
                dve.wait_ge(idx, 2)
                nc.vector.tensor_scalar(ident[:, :], ramp[:, :], lane[:, 0:1], None, ALU.is_equal).then_inc(idx, 1)
                dve.wait_ge(idx, 3)

        sort_edges(nc, a["src"], a["dst"], lists_dram, meta_dram, window_dram, row)

        parts = sb("parts", [P, NWP, 3, H], BF16)
        parts64 = parts[:, :, :, :].rearrange("p w t f -> p (w t f)")[:, 0:NWP * 3 * F].rearrange(
            "p (w t f) -> p w t f", t=3, f=F)
        scratch = sb("scratch", [P, NWP, H])
        h64, z64 = feat[:, :, 0:F], feat[:, :, F:H]
        W, Bc = weight, bias

        def biased(name, out_of, width, relu=False):
            def finish(dve, n, ps, sem):
                v = nc.vector
                to = out_of[:, bass.ds(n * 4, 4), :]
                ins = v.tensor_tensor(to, ps[:, :, :], Bc[name][:, None, :].broadcast_to([P, 4, width]), ALU.add)
                if not relu:
                    return ins
                ins.then_inc(sem, 1)
                dve.wait_ge(sem, n + 1)
                return v.tensor_scalar(to, to, 0.0, None, ALU.max)
            return finish

        normalize(nc, "norm0", xres[:, :, :], h64, scratch[:, :, 0:F])
        split_parts(nc, "split0", h64, parts64, scratch[:, :, 0:F])
        aggregate(nc, "sum0", lists_dram, meta_dram, row, parts64, F, h64)
        perceptron(nc, "mlp0", ident, h64, [(W["L0_gnn_W1"][:, :], Bc["L0_gnn_b1"][:, 0:1])], W["L0_gnn_W2"][:, :], H,
                   biased("L0_gnn_b2", feat[:, :, :], H, relu=True))
        split_parts(nc, "split1", feat[:, :, :], parts[:, :, :, :], scratch[:, :, :])
        aggregate(nc, "sum1", lists_dram, meta_dram, row, parts[:, :, :, :], H, feat[:, :, :])
        perceptron(nc, "mlp1", ident, feat[:, :, :], [(W["L0_gnn_W3"][:, :], Bc["L0_gnn_b3"][:, 0:1])], W["L0_gnn_W4"][:, :], F,
                   residual(nc, Bc["L0_gnn_b4"], xres[:, :, :], xres[:, :, :], scratch[:, :, 0:F]))
        normalize(nc, "norm1", xres[:, :, :], h64, scratch[:, :, 0:F])
        perceptron(nc, "mlp2", ident, h64, [(W["L1_gnn_WM1"][:, :], Bc["L1_gnn_bM1"][:, 0:1]),
                                    (W["L1_gnn_WM2"][:, :], Bc["L1_gnn_bM2"][:, 0:1])], W["L1_gnn_WM3"][:, :], F,
                   biased("L1_gnn_bM3", z64, F))
        split_parts(nc, "split2", z64, parts64, scratch[:, :, 0:F])
        clear(nc, z64)
        aggregate(nc, "sum2", lists_dram, meta_dram, row, parts64, F, z64)
        perceptron(nc, "mlp3", ident, feat[:, :, :], [(W["L1_gnn_WU1"][:, :], Bc["L1_gnn_bU1"][:, 0:1]),
                                              (W["L1_gnn_WU2"][:, :], Bc["L1_gnn_bU2"][:, 0:1])], W["L1_gnn_WU3"][:, :], F,
                   residual(nc, Bc["L1_gnn_bU3"], xres[:, :, :], xres[:, :, :], scratch[:, :, 0:F]))

        stored = ctx.enter_context(nc.semaphore("result_stored"))
        with nc.Block() as block:
            @block.sync
            def _(sp):
                sp.dma_start(out[0:whole * P, :].rearrange("(w p) f -> p w f", p=P), xres[:, 0:whole, :]).then_inc(stored, 16)
                sp.dma_start(out[whole * P:N, :], xres[0:N - whole * P, whole, :]).then_inc(stored, 16)
                sp.wait_ge(stored, 32)


def residual(nc, bias, x, to, scratch):
    def finish(dve, n, ps, sem):
        v = nc.vector
        mid = scratch[:, bass.ds(n * 4, 4), :]
        v.tensor_tensor(mid, ps[:, :, :], bias[:, None, :].broadcast_to([P, 4, F]), ALU.add).then_inc(sem, 1)
        dve.wait_ge(sem, n + 1)
        return v.tensor_tensor(to[:, bass.ds(n * 4, 4), :], mid, x[:, bass.ds(n * 4, 4), :], ALU.add)
    return finish


def clear(nc, x):
    with nc.Block() as block:
        @block.vector
        def _(dve):
            nc.vector.memset(x, 0.0)


def kernel(**inputs):
    import concourse.bacc as bacc
    from concourse.bass_utils import run_bass_kernel_spmd

    nc = bacc.Bacc("TRN2", target_bir_lowering=False, num_devices=1)
    arrays, aps = {}, {}
    for name in _INS:
        arr = np.ascontiguousarray(inputs[name])
        arrays[f"in_{name}"] = arr
        aps[name] = nc.dram_tensor(f"in_{name}", arr.shape, mybir.dt.from_np(arr.dtype), kind="ExternalInput").ap()
    out = nc.dram_tensor("out", (N, F), FP32, kind="ExternalOutput").ap()
    gnn(nc, aps, out)
    r = run_bass_kernel_spmd(nc, [arrays], core_ids=[0])
    return r.results[0]["out"]
```

```python
import numpy as np
import concourse.bass as bass
from concourse import mybir
from contextlib import ExitStack

FP32 = mybir.dt.float32
BF16 = mybir.dt.bfloat16
I32 = mybir.dt.int32
ALU = mybir.AluOpType
ACT = mybir.ActivationFunctionType
AX = mybir.AxisListType

P = 128
N = 6250
E = 206250
F = 64
H = 128
NW = -(-N // P)
NWP = -(-NW // 4) * 4
NB4 = NWP // 4
NT = -(-E // (P * P))
NCH = -(-E // P)
J = 38
COLS = NT * P + 40
XM = J - 1
SLOTS = -(-(NW + XM) // 4) * 4
XS = SLOTS - NW
MAIN_BLOCKS = -(-(NW + 3) // 4)
GROUP_STEPS = 18
ROWS_DONE = 10
ENDS_DONE = 15
GMAX = NW * -(-NCH // J) + 3
RB = 8192
FAR = 64 * P
SKIP = NT * P
KEPT = 64
assert J * P < RB and NW <= 64


class Phase:

    def __init__(self, nc, tag):
        self.nc, self.tag, self.ctx, self.sems = nc, tag, ExitStack(), []

    def sb(self, name, shape, dt=FP32):
        return self.ctx.enter_context(self.nc.sbuf_tensor(f"{self.tag}_{name}", shape, dt))

    def ps(self, name, shape, dt=FP32):
        return self.ctx.enter_context(self.nc.psum_tensor(f"{self.tag}_{name}", shape, dt))

    def sem(self, name):
        self.sems.append(self.ctx.enter_context(self.nc.semaphore(f"{self.tag}_{name}")))
        return self.sems[-1]

    def __enter__(self):
        return self

    def __exit__(self, *error):
        if error[0] is None:
            with self.nc.Block() as block:
                @block.gpsimd
                def _(pool):
                    for s in self.sems:
                        pool.sem_clear(s)
        return self.ctx.__exit__(*error)


def group_pairs(eng, row):
    return eng.value_load(row[0:1, 2 * NW:2 * NW + 1], min_val=NW // 2 - 2, max_val=GMAX // 2 - 2) + 2


def sort_edges(nc, tag, src, dst, dram, row, left):
    with ExitStack() as ctx:
        def sb(name, shape, dt):
            return ctx.enter_context(nc.sbuf_tensor(name, shape, dt))

        key = sb("key", [P, COLS], FP32)
        tile_of = sb("tile_of", [P, COLS], BF16)
        low = sb("low", [P, 2, COLS], BF16)
        ident = sb("ident", [P, P], FP32)
        tri = sb("tri", [P, P], BF16)
        ones = sb("ones", [P, P], BF16)
        free = sb("free", [P, P], FP32)
        part = sb("part", [P, 1], FP32)
        part_k = sb("part_k", [P, 1], FP32)
        window_no = sb("window_no", [P, NW], FP32)
        minus64w = sb("minus64w", [P, NW], FP32)

        with Phase(nc, "columns") as ph:
            tmp = ph.sb

            srow = tmp("srow", [P, NT, P], I32)
            drow = tmp("drow", [P, NT, P], I32)
            bits = tmp("bits", [P, NT, P], I32)
            hi = tmp("hi", [P, NT, P], I32)
            rows = [tmp(n, [P, NT, P], FP32) for n in ("key_row", "tile_row", "slow_row", "dlow_row")]
            dhi = tmp("dhi", [P, NT, P], FP32)
            dmax = tmp("dmax", [P, NT], FP32)
            dmin = tmp("dmin", [P, NT], FP32)
            cid1 = tmp("cid1", [P, NT], FP32)
            wgrid = tmp("wgrid", [P, NW, NT], FP32)
            hit = tmp("hit", [P, 2, NW, NT], FP32)
            ends = tmp("ends", [P, 2, NW], FP32)
            span = tmp("span", [NW, 4], FP32)
            span_i = tmp("span_i", [NW, 2], I32)
            steps = tmp("steps", [NW, NCH // J + 1], FP32)
            stepped = tmp("stepped", [NW, NCH // J + 1], FP32)
            onesf = tmp("onesf", [NW, P], FP32)
            pairs_i = tmp("pairs_i", [1, 2], I32)
            pairs_f = tmp("pairs_f", [1, 1], FP32)
            pt = [ph.ps(f"pt{i}", [P, 4, P]) for i in range(4)]
            pe_ends = ph.ps("pe_ends", [NW, 2, P])
            pe_tot = ph.ps("pe_tot", [P, 1])

            loaded = ph.sem("edges_loaded")
            padded = ph.sem("padding_set")
            consts = ph.sem("constants_ready")
            step = ph.sem("vector_steps")
            turned = ph.sem("columns_turned")
            copied = ph.sem("columns_copied")
            ends_turned = ph.sem("ends_turned")
            counted = ph.sem("groups_counted")
            summed = ph.sem("groups_summed")
            table_out = ph.sem("table_written")
            table_in = ph.sem("table_read")
            table_done = ph.sem("table_ready")

            full = E // P
            in_last = full - (NT - 1) * P
            rest = E - full * P

            with nc.Block() as block:
                @block.sync
                def _(sp):
                    sp.wait_ge(padded, 2)
                    for edges, to in ((dst, drow), (src, srow)):
                        sp.dma_start(to[:, 0:NT - 1, :],
                                     edges[0:(NT - 1) * P * P].rearrange("(t c e) -> c t e", c=P, e=P)
                                     ).then_inc(loaded, 16)
                        sp.dma_start(to[0:in_last, NT - 1, :],
                                     edges[(NT - 1) * P * P:full * P].rearrange("(c e) -> c e", e=P)
                                     ).then_inc(loaded, 16)
                        if rest:
                            sp.dma_start(to[in_last:in_last + 1, NT - 1, 0:rest],
                                         edges[full * P:E].rearrange("(c e) -> c e", c=1)
                                         ).then_inc(loaded, 16)
                    sp.wait_ge(table_done, 1)
                    sp.dma_start(dram["window"][:].rearrange("(w k) -> w k", k=2),
                                 span_i[:, :]).then_inc(table_out, 16)
                    sp.wait_ge(table_out, 16)
                    sp.dma_start(row[:, 0:2 * NW], dram["window"][:].rearrange("(o k) -> o k", o=1)
                                 ).then_inc(table_in, 16)
                    sp.wait_ge(table_in, 16)

                @block.gpsimd
                def _(pool):
                    nc.gpsimd.memset(drow[:, NT - 1, :], FAR).then_inc(padded, 1)
                    nc.gpsimd.memset(srow[:, NT - 1, :], 0).then_inc(padded, 1)
                    kw = dict(allow_small_or_imprecise_dtypes=True)
                    nc.gpsimd.iota(free[:, :], [[1, P]], 0, 0, **kw).then_inc(consts, 1)
                    nc.gpsimd.iota(part[:, :], [[0, 1]], 0, 1, **kw).then_inc(consts, 1)
                    nc.gpsimd.iota(window_no[:, :], [[1, NW]], 0, 0, **kw).then_inc(consts, 1)
                    nc.gpsimd.iota(minus64w[:, :], [[-64, NW]], 0, 0, **kw).then_inc(consts, 1)
                    nc.gpsimd.iota(cid1[:, :], [[P, NT]], 1, 1, **kw).then_inc(consts, 1)
                    nc.gpsimd.iota(wgrid[:, :, :], [[1, NW], [0, NT]], 0, 0, **kw).then_inc(consts, 1)
                    nc.gpsimd.iota(steps[:, :], [[J, NCH // J + 1]], 0, 0, **kw).then_inc(consts, 1)
                    nc.gpsimd.memset(ones[:, :], 1.0)
                    nc.gpsimd.memset(onesf[:, :], 1.0)
                    nc.gpsimd.memset(key[:, NT * P:COLS], float(FAR))
                    nc.gpsimd.memset(tile_of[:, NT * P:COLS], 0.0)
                    nc.gpsimd.memset(low[:, :, NT * P:COLS], 0.0).then_inc(consts, 1)

                @block.vector
                def _(dve):
                    done = [0]

                    def link(ins):
                        done[0] += 1
                        ins.then_inc(step, 1)
                        dve.wait_ge(step, done[0])

                    v = nc.vector
                    dve.wait_ge(consts, 8)
                    v.tensor_scalar(ident[:, :], free[:, :], part[:, 0:1], None, ALU.is_equal)
                    link(v.tensor_scalar(tri[:, :], free[:, :], part[:, 0:1], None, ALU.is_gt))
                    key_row, tile_row, slow_row, dlow_row = rows
                    dve.wait_ge(loaded, 96 if rest else 64)
                    link(v.tensor_scalar(hi[:, :, :], drow[:, :, :], 7, 6, ALU.logical_shift_right, ALU.logical_shift_left))
                    v.tensor_scalar(key_row[:, :, :], hi[:, :, :], 1.0, None, ALU.mult)
                    link(v.tensor_scalar(bits[:, :, :], srow[:, :, :], 7, None, ALU.logical_shift_right))
                    link(v.tensor_copy(tile_row[:, :, :], bits[:, :, :]))
                    link(v.tensor_scalar(dhi[:, :, :], hi[:, :, :], 1.0 / 64, None, ALU.mult))
                    link(v.tensor_tensor(key_row[:, :, :], key_row[:, :, :], tile_row[:, :, :], ALU.add))
                    link(v.tensor_scalar(bits[:, :, :], srow[:, :, :], 127, None, ALU.bitwise_and))
                    link(v.tensor_scalar(slow_row[:, :, :], bits[:, :, :], 1.0, None, ALU.add))
                    link(v.tensor_scalar(hi[:, :, :], drow[:, :, :], 127, None, ALU.bitwise_and))
                    link(v.tensor_scalar(dlow_row[:, :, :], hi[:, :, :], 1.0, None, ALU.add))
                    rows_done = done[0]
                    assert rows_done == ROWS_DONE
                    v.tensor_reduce(dmax[:, :], dhi[:, :, :], AX.X, ALU.max)
                    link(v.tensor_reduce(dmin[:, :], dhi[:, :, :], AX.X, ALU.min))
                    wide = [P, NW, NT]
                    v.tensor_tensor(hit[:, 0, :, :], dmax[:, None, :].broadcast_to(wide), wgrid[:, :, :], ALU.is_ge)
                    link(v.tensor_tensor(hit[:, 1, :, :], dmin[:, None, :].broadcast_to(wide), wgrid[:, :, :], ALU.is_le))
                    link(v.tensor_scalar(dmax[:, :], cid1[:, :], float(-1 - NT * P), None, ALU.add))
                    v.tensor_tensor(hit[:, 0, :, :], hit[:, 0, :, :], dmax[:, None, :].broadcast_to(wide), ALU.mult)
                    link(v.tensor_tensor(hit[:, 1, :, :], hit[:, 1, :, :], cid1[:, None, :].broadcast_to(wide), ALU.mult))
                    v.tensor_reduce(ends[:, 0, :], hit[:, 0, :, :], AX.X, ALU.min)
                    link(v.tensor_reduce(ends[:, 1, :], hit[:, 1, :, :], AX.X, ALU.max))
                    assert done[0] == ENDS_DONE
                    for t in range(NT):
                        dve.wait_ge(turned, t + 1)
                        c = slice(t * P, (t + 1) * P)
                        b = pt[t % 4]
                        v.tensor_copy(key[:, c], b[:, 0, :])
                        v.tensor_copy(tile_of[:, c], b[:, 1, :])
                        v.tensor_copy(low[:, :, c], b[:, 2:4, :]).then_inc(copied, 1)
                    dve.wait_ge(ends_turned, 2)
                    v.tensor_reduce(span[:, 0:1], pe_ends[:, 0, :], AX.X, ALU.min)
                    link(v.tensor_reduce(span[:, 1:2], pe_ends[:, 1, :], AX.X, ALU.max))
                    link(v.tensor_scalar(span[:, 0:1], span[:, 0:1], float(NT * P), None, ALU.add))
                    link(v.tensor_tensor(span[:, 2:3], span[:, 1:2], span[:, 0:1], ALU.subtract))
                    link(v.tensor_scalar(stepped[:, :], steps[:, :], span[:, 2:3], None, ALU.is_lt))
                    link(v.tensor_reduce(span[:, 3:4], stepped[:, :], AX.X, ALU.add))
                    link(v.tensor_scalar(span[:, 3:4], span[:, 3:4], 1.0, None, ALU.max))
                    v.tensor_copy(span_i[:, 0:1], span[:, 0:1])
                    v.tensor_copy(span_i[:, 1:2], span[:, 3:4]).then_inc(table_done, 1)
                    v.engine_nop().then_inc(counted, 1)
                    dve.wait_ge(summed, 1)
                    link(v.tensor_scalar(pairs_i[:, 0:1], pe_tot[0:1, :], -3.0, None, ALU.add))
                    link(v.tensor_scalar(pairs_i[:, 1:2], pairs_i[:, 0:1], 1, None, ALU.logical_shift_right))
                    link(v.tensor_copy(pairs_f[:, 0:1], pairs_i[:, 1:2]))
                    v.tensor_copy(row[:, 2 * NW:2 * NW + 1], pairs_f[:, 0:1])
                    v.tensor_scalar(row[:, 2 * NW + 1:2 * NW + 2], pairs_f[:, 0:1], float(KEPT // 2 - 2), None, ALU.min)
                    v.tensor_scalar(row[:, 2 * NW + 2:2 * NW + 3], pairs_f[:, 0:1], 2.0, 4.0, ALU.mult, ALU.add).then_inc(table_done, 1)

                @block.tensor
                def _(pe):
                    pe.wait_ge(step, ROWS_DONE)
                    for t in range(NT):
                        if t >= 4:
                            pe.wait_ge(copied, t - 3)
                        for k in range(4):
                            last = nc.tensor.transpose(pt[t % 4][:, k, :], rows[k][:, t, :], ident[:, :])
                        last.then_inc(turned, 1)
                    pe.wait_ge(step, ENDS_DONE)
                    for k in range(2):
                        nc.tensor.transpose(pe_ends[:, k, :], ends[:, k, :], ident[:, :]).then_inc(ends_turned, 1)
                    pe.wait_ge(counted, 1)
                    nc.tensor.matmul(pe_tot[:, :], onesf[:, :], span[:, 3:4], start=True, stop=True).then_inc(summed, 1)

        ph = ctx.enter_context(Phase(nc, "sort"))
        sb, MAIN = ph.sb, 4 * MAIN_BLOCKS

        def pair(name, shape, dt):
            return [ph.sb(f"{name}{i}", shape, dt) for i in range(2)]

        grid_k = sb("grid_k", [P, P, J], BF16)
        grid_a = sb("grid_a", [P, NW, J], BF16)
        grid_x = sb("grid_x", [P, 3, J], FP32)
        grid_r = sb("grid_r", [P, SLOTS - MAIN], FP32)
        stage_key = sb("stage_key", [P, 2, J], BF16)
        stage_tile = sb("stage_tile", [P, 2, J], BF16)
        stage_low = sb("stage_low", [P, 2, 2, J], BF16)
        stage_win = sb("stage_win", [P, 2, 1], FP32)
        bucket = pair("bucket", [P, NW, J], BF16)
        place = pair("place", [P, P, J], BF16)
        cargo = pair("cargo", [P, 2, SLOTS, J], BF16)
        extra = pair("extra", [P, 3, J], BF16)
        low_main = pair("low_main", [P, 2, J], BF16)
        low_f = sb("low_f", [P, 2, J])
        resets = sb("resets", [P, NW, J])
        ranks = sb("ranks", [P, NW, J])
        picked = sb("picked", [P, NW, J])
        rank = sb("rank", [P, J])
        fields = sb("fields", [P, 5, J], I32)
        row_of = pair("row_of", [P, J], BF16)
        is_main = sb("is_main", [P, J], BF16)
        is_extra = sb("is_extra", [P, J], BF16)
        xslot = pair("xslot", [P, J], FP32)
        nx_i = sb("nx_i", [P, 2, NW], I32)
        nx = sb("nx", [P, 3, NW])
        nx_end = pair("nx_end", [P, NW], FP32)
        nb_i = sb("nb_i", [P, 2], I32)
        nb_max = sb("nb_max", [P, 1])
        left_f = sb("left_f", [1, 2])
        ones_f = sb("ones_f", [P, NW])
        tile_rb = sb("tile_rb", [P, NW])
        ended = sb("ended", [P, NW - 1])
        ended_n = sb("ended_n", [P, 1])
        lane_x = sb("lane_x", [P, 3])
        meta = pair("meta", [P, 4], I32)
        sorted_sb = pair("sorted_sb", [P, 2, SLOTS], BF16)
        ps_base = [ph.ps(f"ps_base{i}", [P, NW]) for i in range(2)]
        ps_cnt = [ph.ps(f"ps_cnt{i}", [P, NW]) for i in range(2)]
        ps_rank = ph.ps("ps_rank", [P, 7, J])
        ps_sorted = [ph.ps(f"ps_sorted{i}", [P, 2, SLOTS]) for i in range(2)]
        assert NW % 7 == 0

        sem = ph.sem
        grids = sem("grids_ready")
        lanes = sem("lanes_ready")
        zeroed = sem("rare_columns_zeroed")
        staged = sem("staged")
        stage_free_pool = sem("stage_free_pool")
        stage_free_dve = sem("stage_free_dve")
        bucketed = sem("bucketed")
        based = sem("based")
        steps = sem("rank_steps")
        meta_steps = sem("meta_steps")
        resets_set = sem("resets_set")
        nb_ready = sem("nb_ready")
        picked_ready = sem("picked_ready")
        summed = sem("ranks_summed")
        rare_scalars = sem("rare_scalars")
        extra_ready = sem("extra_ready")
        main_ready = sem("main_ready")
        placed = sem("placed")
        meta_ready = sem("meta_ready")
        cargoed = sem("cargoed")
        permuted = sem("permuted")
        sorted_out = sem("sorted_copied")
        stored = [sem(f"stored{i}") for i in range(2)]
        rare_stored = [sem(f"rare_stored{i}") for i in range(2)]
        meta_stored = [sem(f"meta_stored{i}") for i in range(2)]
        passed = sem("passed")

        def over_groups(eng, body):
            n = group_pairs(eng, row)
            for b in range(2):
                body(b, b, True)
            with eng.Fori(1, n) as i:
                for b in range(2):
                    body(i * 2 + b, b, False)
            return n

        def over_groups_peeled(eng, body):
            n = group_pairs(eng, row)
            body(0, 0, True, True, False)
            body(1, 1, False, True, False)
            with eng.Fori(1, n - 1) as i:
                body(i * 2, 0, False, False, False)
                body(i * 2 + 1, 1, False, False, False)
            body(n * 2 - 2, 0, False, False, False)
            body(n * 2 - 1, 1, False, False, True)
            return n

        with nc.Block() as block:
            @block.scalar
            def _(act):
                def stage(b, col, w):
                    def of(t):
                        return t[:, bass.ds(b, 1), :].rearrange("p o j -> p (o j)")

                    nc.scalar.activation(of(stage_key), key[:, bass.ds(col, J)], ACT.Identity, bias=minus64w[:, bass.ds(w, 1)])
                    nc.scalar.activation(of(stage_tile), tile_of[:, bass.ds(col, J)], ACT.Identity)
                    nc.scalar.activation(of(stage_win), window_no[:, bass.ds(w, 1)], ACT.Identity)
                    nc.scalar.activation(stage_low[:, bass.ds(b, 1), :, :].rearrange("p o k j -> p (o k) j"), low[:, :, bass.ds(col, J)],
                                         ACT.Identity).then_inc(staged, 1)

                g_r = act.alloc_register("act_group")
                col_r = act.alloc_register("act_column")

                def stage_next(col, w):
                    g = act.snap(g_r, min_val=0, max_val=GMAX)
                    act.wait_ge(stage_free_pool, g + 1)
                    act.wait_ge(stage_free_dve, g + 1)
                    stage(g & 1, col, w)

                act.reg_mov(g_r, 0)
                with act.Fori(0, NW) as w:
                    act.reg_mov(col_r, act.value_load(row[0:1, bass.ds(w * 2, 1)], min_val=0, max_val=NT * P))
                    n = act.value_load(row[0:1, bass.ds(w * 2 + 1, 1)], min_val=1, max_val=NCH // J + 1)
                    with act.Fori(0, n):
                        stage_next(act.snap(col_r, min_val=0, max_val=SKIP), w)
                        act.reg_add(g_r, g_r, 1)
                        act.reg_add(col_r, col_r, J)
                stage_next(SKIP, NW - 1)

            @block.gpsimd
            def _(pool):
                kw = dict(allow_small_or_imprecise_dtypes=True)
                pool.sem_inc(stage_free_pool, 2)
                nc.gpsimd.iota(grid_a[:, :, :], [[1, NW], [0, J]], 0, 0, **kw)
                nc.gpsimd.iota(tile_rb[:, :], [[RB, NW]], 0, 0, **kw)
                nc.gpsimd.iota(lane_x[:, 0:1], [[0, 1]], -NW, 1, **kw)
                nc.gpsimd.iota(grid_k[:, :, :], [[1, P], [0, J]], 0, 0, **kw)
                nc.gpsimd.iota(grid_x[:, :, :], [[1, 3], [0, J]], 1, 0, **kw)
                nc.gpsimd.iota(grid_r[:, :], [[1, SLOTS - MAIN]], MAIN - NW + 1, 0, **kw).then_inc(grids, 1)
                for b in range(2):
                    nc.gpsimd.memset(cargo[b][:, :, MAIN:SLOTS, :], 0.0).then_inc(zeroed, 1)
                dirty = [pool.alloc_register(f"pool_dirty{b}") for b in range(2)]
                for b in range(2):
                    pool.reg_mov(dirty[b], 0)
                copies = pool.alloc_register("pool_rare_groups")
                pool.reg_mov(copies, 1)

                def cargo_of(g, b, first):
                    pool.wait_ge(nb_ready, g + 1)
                    pool.sem_inc(passed, 1)
                    nb = pool.value_load(meta[b][0:1, 1:2], min_val=0, max_val=SLOTS // 4)
                    pool.wait_ge(extra_ready, g + 1)
                    pool.wait_ge(permuted, g + 1)
                    pool.sem_inc(passed, 1)
                    with pool.If(pool.snap(dirty[b], min_val=0, max_val=1) > 0):
                        nc.gpsimd.memset(cargo[b][:, :, MAIN:SLOTS, :], 0.0).then_inc(zeroed, 1)
                        pool.reg_mov(dirty[b], 0)
                    with pool.If(nb > MAIN_BLOCKS):
                        done = pool.snap(copies, min_val=1, max_val=1 << 20)
                        nc.gpsimd.tensor_copy(low_f[:, :, :], stage_low[:, b, :, :]).then_inc(rare_scalars, 1)
                        pool.wait_ge(rare_scalars, done)
                        pool.sem_inc(passed, 1)
                        for k in range(2):
                            for j in range(J):
                                nc.gpsimd.tensor_scalar(cargo[b][:, k, MAIN:SLOTS, j], grid_r[:, :], xslot[b][:, j:j + 1],
                                                        low_f[:, k, j:j + 1], ALU.is_equal, ALU.mult)
                        pool.reg_mov(dirty[b], 1)
                        pool.reg_add(copies, copies, 1)
                    for k in range(2):
                        last = nc.gpsimd.tensor_tensor(cargo[b][:, k, NW:MAIN, :], extra[b][:, :, :],
                                                       stage_low[:, b, k, None, :].broadcast_to([P, 3, J]), ALU.mult)
                    last.then_inc(stage_free_pool, 1)
                    pool.wait_ge(main_ready, g + 1)
                    for k in range(2):
                        last = nc.gpsimd.tensor_tensor(cargo[b][:, k, 0:NW, :], bucket[b][:, :, :],
                                                       low_main[b][:, k, None, :].broadcast_to([P, NW, J]), ALU.mult)
                    last.then_inc(cargoed, 1)

                over_groups(pool, cargo_of)

            @block.vector
            def _(dve):
                v = nc.vector
                dve.sem_inc(stage_free_dve, 2)
                dve.sem_inc(sorted_out, 2)
                v.memset(resets[:, :, :], 0.0)
                v.memset(nb_max[:, :], 0.0)
                v.memset(ones_f[:, :], 1.0)
                dve.wait_ge(grids, 1)
                v.tensor_scalar(lane_x[:, 1:2], lane_x[:, 0:1], 0.0, None, ALU.is_ge).then_inc(lanes, 1)
                v.tensor_scalar(lane_x[:, 2:3], lane_x[:, 0:1], 0.0, None, ALU.is_lt).then_inc(lanes, 1)
                dve.wait_ge(lanes, 2)
                v.tensor_tensor(lane_x[:, 2:3], lane_x[:, 2:3], part[:, :], ALU.mult).then_inc(lanes, 1)
                dve.wait_ge(lanes, 3)

                def to_bucket(g, b, first):
                    dve.wait_ge(staged, g + 1)
                    if not first:
                        dve.wait_ge(cargoed, g - 1)
                    v.tensor_tensor(bucket[b][:, :, :], grid_a[:, :, :],
                                    stage_key[:, b, None, :].broadcast_to([P, NW, J]), ALU.is_equal).then_inc(bucketed, 1)

                def place_rows(g, b):
                    dve.wait_ge(permuted, g + 1)
                    v.tensor_tensor(place[b][:, :, :], grid_k[:, :, :],
                                    row_of[b][:, None, :].broadcast_to([P, P, J]), ALU.is_equal).then_inc(placed, 1)

                def copy_out(g, b):
                    dve.wait_ge(permuted, g + 3)
                    dve.wait_ge(stored[b], (g - b) * 8 + 16)
                    dve.wait_ge(rare_stored[b], (g - b) * 8 + 16)
                    v.tensor_copy(sorted_sb[b][:, :, :], ps_sorted[b][:, :, :]).then_inc(sorted_out, 1)

                def ended_before(g, b):
                    v.tensor_scalar(ended[:, :], nx_end[b][:, 0:NW - 1], lane_x[:, 0:1], None, ALU.is_le).then_inc(meta_steps, 1)

                def count_ended(g, b):
                    dve.wait_ge(meta_steps, g * 2 + 1)
                    v.tensor_reduce(ended_n[:, :], ended[:, :], AX.X, ALU.add).then_inc(meta_steps, 1)

                def column_tile(g, b):
                    dve.wait_ge(meta_steps, g * 2 + 2)
                    v.tensor_scalar(meta[b][:, 0:1], ended_n[:, :], lane_x[:, 1:2], lane_x[:, 2:3], ALU.mult, ALU.add).then_inc(meta_ready, 1)

                def group(g, b, head, first, last):
                    done = [0]

                    def step(ins):
                        ins.then_inc(steps, 1)
                        done[0] += 1
                        return done[0]

                    def after(number):
                        dve.wait_ge(steps, g * GROUP_STEPS + number)

                    before = (lambda f, *a: None) if head else (lambda f, *a: f(g - 1, 1 - b, *a))
                    dve.wait_ge(based, g + 1)
                    a = step(v.tensor_scalar(nx_i[:, 0, :], ps_cnt[b][:, :], 128.0, -1.0, ALU.max, ALU.add))
                    before(ended_before)
                    after(a)
                    a = step(v.tensor_scalar(nx_i[:, 1, :], nx_i[:, 0, :], 7, None, ALU.logical_shift_right))
                    before(count_ended)
                    after(a)
                    a = step(v.tensor_copy(nx[:, 0, :], nx_i[:, 1, :]))
                    before(column_tile)
                    after(a)
                    a = step(v.tensor_tensor_scan(nx_end[b][:, :], ones_f[:, :], nx[:, 0, :], 0.0, ALU.mult, ALU.add))
                    if not first:
                        copy_out(g - 2, b)
                    after(a)
                    a = step(v.tensor_tensor(nx[:, 1, :], nx_end[b][:, :], nx[:, 0, :], ALU.subtract))
                    v.tensor_copy(nb_i[:, 0:1], nx_end[b][:, NW - 1:NW])
                    after(a)
                    a = step(v.scalar_tensor_tensor(nx[:, 2, :], nx[:, 1, :], float(RB), tile_rb[:, :], ALU.mult, ALU.add))
                    after(a)
                    c = step(v.tensor_scalar(nb_i[:, 1:2], nb_i[:, 0:1], 2, None, ALU.logical_shift_right))
                    v.tensor_tensor(resets[:, :, 0], nx[:, 2, :], ps_base[b][:, :], ALU.add).then_inc(resets_set, 1)
                    after(c)
                    if not first:
                        dve.wait_ge(meta_stored[b], (g - b) * 8)
                    v.tensor_scalar(meta[b][:, 1:2], nb_i[:, 1:2], float(MAIN_BLOCKS), None, ALU.add).then_inc(nb_ready, 1)
                    dve.wait_ge(resets_set, g + 1)
                    a = step(v.tensor_tensor_scan(ranks[:, :, :].rearrange("p a j -> p (a j)"),
                                                  resets[:, :, :].rearrange("p a j -> p (a j)"),
                                                  bucket[b][:, :, :].rearrange("p a j -> p (a j)"),
                                                  0.0, ALU.max, ALU.add))
                    dve.wait_ge(nb_ready, g + 1)
                    v.tensor_tensor(nb_max[:, :], nb_max[:, :], meta[b][:, 1:2], ALU.max)
                    after(a)
                    v.tensor_tensor(picked[:, :, :], ranks[:, :, :], bucket[b][:, :, :], ALU.mult).then_inc(picked_ready, 1)
                    before(place_rows)
                    v.tensor_copy(meta[b][:, 2:3], stage_win[:, b, :])
                    v.tensor_copy(meta[b][:, 3:4], stage_win[:, b, :])
                    dve.wait_ge(summed, g + 1)
                    a = step(v.tensor_reduce(rank[:, :], ps_rank[:, :, :].rearrange("p a j -> p j a"), AX.X, ALU.add))
                    after(a)
                    a = step(v.tensor_scalar(fields[:, 0, :], rank[:, :], -1.0, None, ALU.add))
                    if not last:
                        to_bucket(g + 1, 1 - b, head)
                    after(a)
                    r = step(v.tensor_scalar(fields[:, 1, :], fields[:, 0, :], 127, None, ALU.bitwise_and))
                    q = step(v.tensor_scalar(fields[:, 4, :], fields[:, 0, :], RB - 1, None, ALU.bitwise_and))
                    f = step(v.tensor_scalar(fields[:, 2, :], fields[:, 0, :], 13, None, ALU.arith_shift_right))
                    after(q)
                    q = step(v.tensor_scalar(fields[:, 3, :], fields[:, 4, :], 7, None, ALU.arith_shift_right))
                    v.tensor_copy(row_of[b][:, :], fields[:, 1, :])
                    after(q)
                    m = step(v.tensor_scalar(is_main[:, :], fields[:, 3, :], 0.0, None, ALU.is_equal))
                    x = step(v.tensor_tensor(xslot[b][:, :], fields[:, 2, :], fields[:, 3, :], ALU.add))
                    after(m)
                    v.tensor_tensor(low_main[b][:, :, :], stage_low[:, b, :, :],
                                    is_main[:, None, :].broadcast_to([P, 2, J]), ALU.mult).then_inc(main_ready, 1)
                    e = step(v.scalar_tensor_tensor(is_extra[:, :], rank[:, :], 0.0, is_main[:, :], ALU.is_gt, ALU.is_gt))
                    after(x)
                    v.tensor_tensor(xslot[b][:, :], xslot[b][:, :], stage_tile[:, b, :], ALU.subtract).then_inc(stage_free_dve, 1)
                    dve.wait_ge(stage_free_dve, g + 3)
                    x = step(v.tensor_tensor(xslot[b][:, :], xslot[b][:, :], is_extra[:, :], ALU.mult))
                    after(x)
                    v.tensor_tensor(extra[b][:, :, :], grid_x[:, :, :],
                                    xslot[b][:, None, :].broadcast_to([P, 3, J]), ALU.is_equal).then_inc(extra_ready, 1)
                    dve.sem_inc(passed, 1)
                    assert done[0] == GROUP_STEPS

                to_bucket(0, 0, True)
                n = over_groups_peeled(dve, group)
                place_rows(n * 2 - 1, 1)
                ended_before(n * 2 - 1, 1)
                copy_out(n * 2 - 2, 0)
                count_ended(n * 2 - 1, 1)
                column_tile(n * 2 - 1, 1)
                copy_out(n * 2 - 1, 1)
                v.tensor_scalar(left_f[:, 0:1], nb_max[0:1, :], float(MAIN_BLOCKS), None, ALU.is_gt)
                v.tensor_scalar(left_f[:, 1:2], row[0:1, 2 * NW + 2:2 * NW + 3], float(KEPT), None, ALU.is_gt).then_inc(lanes, 1)
                dve.wait_ge(lanes, 4)
                v.tensor_tensor(left[:, :], left_f[:, 0:1], left_f[:, 1:2], ALU.max)

            @block.tensor
            def _(pe):
                def base(g, b, first):
                    pe.wait_ge(bucketed, g + 1)
                    if not first:
                        pe.wait_ge(resets_set, g - 1)
                    for j in range(J):
                        nc.tensor.matmul(ps_base[b][:, :], tri[:, :], bucket[b][:, :, j],
                                         start=(j == 0), stop=(j == J - 1))
                    for j in range(J):
                        last = nc.tensor.matmul(ps_cnt[b][:, :], ones[:, :], bucket[b][:, :, j],
                                                start=(j == 0), stop=(j == J - 1))
                    last.then_inc(based, 1)

                def permute(g, b):
                    pe.wait_ge(placed, g + 1)
                    pe.wait_ge(cargoed, g + 1)
                    pe.wait_ge(stage_free_pool, g + 3)
                    pe.wait_ge(sorted_out, g + 1)
                    for j in range(J):
                        last = nc.tensor.matmul(ps_sorted[b][:, :, :], place[b][:, :, j], cargo[b][:, :, :, j],
                                                start=(j == 0), stop=(j == J - 1))
                    last.then_inc(permuted, 1)

                def group(g, b, head, first, last):
                    pe.wait_ge(picked_ready, g + 1)
                    for i in range(NW // 7):
                        end = nc.tensor.matmul(ps_rank[:, :, :], ident[:, :], picked[:, 7 * i:7 * i + 7, :],
                                               start=(i == 0), stop=(i == NW // 7 - 1))
                    end.then_inc(summed, 1)
                    if not last:
                        base(g + 1, 1 - b, head)
                    if not head:
                        permute(g - 1, 1 - b)

                pe.sem_inc(permuted, 2)
                base(0, 0, True)
                n = over_groups_peeled(pe, group)
                permute(n * 2 - 1, 1)

            @block.sync
            def _(sp):
                def store(g, b, first):
                    sp.wait_ge(sorted_out, g + 3)
                    sp.dma_start(dram["main"][bass.ds(g, 1), :, :].rearrange("o p (k s) -> (o p) k s", k=2),
                                 sorted_sb[b][:, :, 0:MAIN]).then_inc(stored[b], 16)
                    sp.dma_start(dram["rare"][bass.ds(g, 1), :, :].rearrange("o p (k s) -> (o p) k s", k=2),
                                 sorted_sb[b][:, :, MAIN:SLOTS]).then_inc(rare_stored[b], 16)
                    sp.wait_ge(meta_ready, g + 1)
                    sp.dma_start(dram["meta"][bass.ds(g, 1), :, :].rearrange("o p k -> (o p) k"),
                                 meta[b][:, :]).then_inc(meta_stored[b], 16)

                for b in range(2):
                    sp.sem_inc(stored[b], 16)
                    sp.sem_inc(rare_stored[b], 16)
                n = over_groups(sp, store)
                for b in range(2):
                    sp.wait_ge(stored[b], n * 16 + 16)
                    sp.wait_ge(rare_stored[b], n * 16 + 16)
                    sp.wait_ge(meta_stored[b], n * 16)
                sp.sem_inc(passed, 1)


def known_pairs(eng, row):
    return eng.value_load(row[0:1, 2 * NW + 1:2 * NW + 2], min_val=NW // 2 - 2, max_val=KEPT // 2 - 2) + 2


def over_pairs(eng, row, body):
    n = known_pairs(eng, row)
    for b in range(2):
        body(b, b)
    with eng.Fori(1, n) as i:
        for b in range(2):
            body(i * 2 + b, b)
    return n


def aggregate(nc, tag, dram, row, parts, width, acc, build):
    with Phase(nc, tag) as ph:
        B = MAIN_BLOCKS
        RING = 4
        LAG = 2
        PIECE = 4
        PIECES = -(-B // PIECE)
        assert (B - 1) % RING == 0
        metas = [ph.sb(f"metas{i}", [1, P, 4], I32) for i in range(2)]
        cnts = [ph.sb(f"cnts{i}", [P, B, 4, P], BF16) for i in range(2)]
        xtiles = [ph.sb(f"xtiles{i}", [P, 3, 3 * width], BF16) for i in range(2)]
        total = [ph.sb(f"total{i}", [P, width]) for i in range(2)]
        ps_out = [ph.ps(f"ps_out{i}", [P, 3, width]) for i in range(2)]
        meta_in = [ph.sem(f"meta_in{i}") for i in range(2)]
        meta_seen = ph.sem("meta_seen")
        tiles_ready = ph.sem("tiles_ready")
        group_out = ph.sem("group_out")
        totalled = ph.sem("totalled")
        added = ph.sem("added")
        if build:
            grid4 = ph.sb("grid4", [P, P, 4], BF16)
            lists = [ph.sb(f"lists{i}", [P, 2, 4 * B], BF16) for i in range(2)]
            hot = [ph.sb(f"hot{i}", [P, 2, P, 4], BF16) for i in range(RING + 1)]
            ps_cnts = [ph.ps(f"ps_cnts{i}", [P, 4, P]) for i in range(RING + 1)]
            grid_ready = ph.sem("grid_ready")
            list_in = [ph.sem(f"list_in{i}") for i in range(2)]
            hot_ready = ph.sem("hot_ready")
            cnt_ready = ph.sem("cnt_ready")
            cnt_copied = ph.sem("cnt_copied")
            kept = [ph.sem(f"kept{i}") for i in range(2)]
        else:
            piece_in = [[ph.sem(f"piece_in{i}_{p}") for p in range(PIECES)] for i in range(2)]
            piece_used = ph.sem("piece_used")

        def at_start(g, upto):
            return isinstance(g, int) and g < upto

        def slot(k):
            return k % RING if k < B - 1 else RING

        def earlier(g, k):
            if k == B - 1:
                return g * B
            return g * B + k - RING + (1 if k >= RING else 0)

        def unused(g, k):
            return at_start(g, 1) and (k < RING or k == B - 1)

        def tile(b, c):
            return parts[:, c, :, :] if c < NW else xtiles[b][:, c - NW, :]

        with nc.Block() as block:
            @block.sync
            def _(sp):
                def load(g, b):
                    if not at_start(g, 2):
                        sp.wait_ge(added, g - 1)
                    sp.dma_start(metas[b][:, :, :].rearrange("o p k -> o (p k)"),
                                 dram["meta"][bass.ds(g, 1), :, :].rearrange("o p k -> o (p k)")).then_inc(meta_in[b], 16)
                    if build:
                        sp.dma_start(lists[b][:, :, :].rearrange("p k s -> p (k s)"),
                                     dram["main"][bass.ds(g, 1), :, :].rearrange("o p k -> (o p) k")).then_inc(list_in[b], 16)

                def load_counts(g, b):
                    for p in range(PIECES):
                        ks = slice(p * PIECE, min(B, (p + 1) * PIECE))
                        if not at_start(g, 2):
                            if p < PIECES - 1:
                                sp.wait_ge(piece_used, (g - 2) * (PIECES - 1) + p + 1)
                            else:
                                sp.wait_ge(group_out, g - 1)
                        sp.dma_start(cnts[b][:, ks, :, :].rearrange("p k c d -> p (k c d)"),
                                     dram["counts"][bass.ds(g, 1), :, ks.start * 4 * P:ks.stop * 4 * P].rearrange("o p k -> (o p) k")
                                     ).then_inc(piece_in[b][p], 16)

                def both(g, b):
                    load_counts(g, b)
                    load(g, b)

                over_pairs(sp, row, load if build else both)

            @block.gpsimd
            def _(pool):
                if build:
                    nc.gpsimd.iota(grid4[:, :, :], [[1, P], [0, 4]], 1, 0,
                                   allow_small_or_imprecise_dtypes=True).then_inc(grid_ready, 1)

                def fetch_tiles(g, b):
                    pool.wait_ge(meta_in[b], (g - b) * 8 + 16)
                    pool.sem_inc(meta_seen, 1)
                    a = [pool.value_load(metas[b][0:1, NW + x, 0:1], min_val=0, max_val=NW - 1) for x in range(3)]
                    if not at_start(g, 2):
                        pool.wait_ge(group_out, g - 1)
                    for x in range(3):
                        last = nc.gpsimd.tensor_copy(
                            xtiles[b][:, x, :].bitcast(I32),
                            parts[:, bass.ds(a[x], 1), :, :].rearrange("p o t f -> p (o t f)").bitcast(I32))
                    last.then_inc(tiles_ready, 1)

                over_pairs(pool, row, fetch_tiles)

            @block.vector
            def _(dve):
                v = nc.vector
                wreg = dve.alloc_register(f"{tag}_window")

                def load_window(g, b):
                    dve.wait_ge(meta_in[b], (g - b) * 8 + 16)
                    dve.sem_inc(meta_seen, 1)
                    dve.reg_mov(wreg, dve.value_load(metas[b][0:1, 0, 2:3], min_val=0, max_val=NW - 1))

                def add_group(g, b):
                    w = dve.snap(wreg, min_val=0, max_val=NW - 1)
                    dve.wait_ge(group_out, g + 1)
                    v.tensor_reduce(total[b][:, :], ps_out[b][:, :, :].rearrange("p t f -> p f t"), AX.X,
                                    ALU.add).then_inc(totalled, 1)
                    dve.wait_ge(totalled, g + 1)
                    to = acc[:, bass.ds(w, 1), :].rearrange("p o f -> p (o f)")
                    v.tensor_tensor(to, to, total[b][:, :], ALU.add).then_inc(added, 1)

                def one_hots(g, b):
                    dve.wait_ge(list_in[b], (g - b) * 8 + 16)
                    for k in range(B):
                        if not unused(g, k):
                            dve.wait_ge(cnt_ready, earlier(g, k))
                        v.tensor_tensor(hot[slot(k)][:, :, :, :], grid4[:, None, :, :].broadcast_to([P, 2, P, 4]),
                                        lists[b][:, :, None, 4 * k:4 * k + 4].broadcast_to([P, 2, P, 4]),
                                        ALU.is_equal).then_inc(hot_ready, 1)
                        if k == LAG + 3 and not at_start(g, 1):
                            add_group(g - 1, 1 - b)
                        if k == LAG + 5:
                            load_window(g, b)

                def add_only(g, b):
                    load_window(g, b)
                    add_group(g, b)

                if build:
                    dve.wait_ge(grid_ready, 1)
                    n = over_pairs(dve, row, one_hots)
                    add_group(n * 2 - 1, 1)
                else:
                    over_pairs(dve, row, add_only)

            @block.tensor
            def _(pe):
                def use(g, b, k):
                    if build:
                        pe.wait_ge(cnt_copied, g * B + k + 1)
                    elif k % PIECE == 0:
                        pe.wait_ge(piece_in[b][k // PIECE], (g - b) * 8 + 16)
                    if k == 0 and not at_start(g, 2):
                        pe.wait_ge(added, g - 1)
                    if k == B - 1:
                        pe.wait_ge(tiles_ready, g + 1)
                    for c in range(4):
                        last = nc.tensor.matmul(ps_out[b][:, :, :], cnts[b][:, k, c, :], tile(b, 4 * k + c),
                                                start=(k == 0 and c == 0), stop=(k == B - 1 and c == 3))
                    if k == B - 1:
                        last.then_inc(group_out, 1)
                    elif not build and k % PIECE == PIECE - 1:
                        last.then_inc(piece_used, 1)

                def count_and_use(g, b):
                    for k in range(B):
                        pe.wait_ge(hot_ready, g * B + k + 1)
                        if not unused(g, k):
                            pe.wait_ge(cnt_copied, earlier(g, k))
                        for c in range(4):
                            last = nc.tensor.matmul(ps_cnts[slot(k)][:, c, :], hot[slot(k)][:, 0, :, c],
                                                    hot[slot(k)][:, 1, :, c], start=True, stop=True)
                        last.then_inc(cnt_ready, 1)
                        if k >= LAG:
                            use(g, b, k - LAG)
                        elif not at_start(g, 1):
                            use(g - 1, 1 - b, B - LAG + k)

                def use_all(g, b):
                    for k in range(B):
                        use(g, b, k)

                if build:
                    n = over_pairs(pe, row, count_and_use)
                    for k in range(B - LAG, B):
                        use(n * 2 - 1, 1, k)
                else:
                    over_pairs(pe, row, use_all)

            if build:
                @block.scalar
                def _(act):
                    def copy_counts(g, b):
                        if not at_start(g, 2):
                            act.wait_ge(group_out, g - 1)
                            act.wait_ge(kept[b], (g - b) * 8)
                        for k in range(B):
                            act.wait_ge(cnt_ready, g * B + k + 1)
                            nc.scalar.activation(cnts[b][:, k, :, :], ps_cnts[slot(k)][:, :, :],
                                                 ACT.Identity).then_inc(cnt_copied, 1)
                        act.wait_ge(cnt_copied, g * B + B)
                        act.dma_start(dram["counts"][bass.ds(g, 1), :, :].rearrange("o p k -> (o p) k"),
                                      cnts[b][:, :, :, :].rearrange("p k c d -> p (k c d)")).then_inc(kept[b], 16)

                    n = over_pairs(act, row, copy_counts)
                    for b in range(2):
                        act.wait_ge(kept[b], n * 16)
                    act.sem_inc(meta_seen, 1)


def aggregate_rest(nc, tag, dram, row, left, parts, width, acc):
    with Phase(nc, tag) as ph:
        meta = ph.sb("meta", [1, P, 4], I32)
        grid4 = ph.sb("grid4", [P, P, 4], BF16)
        cols = ph.sb("cols", [P, 2, SLOTS], BF16)
        hot = ph.sb("hot", [P, 2, P, 4], BF16)
        cnts = ph.sb("cnts", [P, 4, P], BF16)
        total = ph.sb("total", [P, width])
        ps_cnts = ph.ps("ps_cnts", [P, 4, P])
        ps_out = ph.ps("ps_out", [P, 3, width])
        grid_ready = ph.sem("grid_ready")
        meta_in = ph.sem("meta_in")
        main_in = ph.sem("main_in")
        rare_in = ph.sem("rare_in")
        cols_ready = ph.sem("cols_ready")
        passed = ph.sem("passed")
        hot_ready = ph.sem("hot_ready")
        cnt_ready = ph.sem("cnt_ready")
        cnt_copied = ph.sem("cnt_copied")
        block_out = ph.sem("block_out")
        totalled = ph.sem("totalled")
        added = ph.sem("added")
        seen = {e: ph.sem(f"{e}_seen") for e in ("sp", "dve", "act", "pe")}

        def over_rest(eng, name, of_group, of_block):
            def registers(what):
                r = eng.alloc_register(f"{tag}_{name}_{what}")
                eng.reg_mov(r, 1)
                return r, lambda: eng.snap(r, min_val=1, max_val=1 << 24)

            (block_r, block_no), (group_r, group_no) = registers("blocks"), registers("groups")
            any_left = eng.value_load(left[0:1, 0:1], min_val=0, max_val=1)

            def groups(lo, hi, first_block):
                with eng.Fori(lo, hi) as g:
                    if name == "sp":
                        for s in seen.values():
                            eng.wait_ge(s, g + 1)
                        eng.dma_start(meta[:, :, :].rearrange("o p k -> o (p k)"),
                                      dram["meta"][bass.ds(g, 1), :, :].rearrange("o p k -> o (p k)")).then_inc(meta_in, 16)
                    eng.wait_ge(meta_in, g * 16 + 16)
                    eng.sem_inc(passed, 1)
                    nb = eng.value_load(meta[0:1, 0, 1:2], min_val=0, max_val=SLOTS // 4)
                    with eng.If(nb > first_block):
                        of_group(g, group_no(), block_no())
                        eng.reg_add(group_r, group_r, 1)
                        with eng.Fori(first_block, nb) as t:
                            of_block(t, block_no())
                            eng.reg_add(block_r, block_r, 1)
                    eng.sem_inc(seen[name], 1)

            with eng.If(any_left > 0):
                n = known_pairs(eng, row)
                groups(0, n * 2, MAIN_BLOCKS)
                more = eng.value_load(row[0:1, 2 * NW + 2:2 * NW + 3], min_val=0, max_val=GMAX)
                with eng.If(more > KEPT):
                    groups(KEPT, more, 0)

        with nc.Block() as block:
            @block.gpsimd
            def _(pool):
                nc.gpsimd.iota(grid4[:, :, :], [[1, P], [0, 4]], 1, 0,
                               allow_small_or_imprecise_dtypes=True).then_inc(grid_ready, 1)
                for s in seen.values():
                    pool.sem_inc(s, 1)
                pool.sem_inc(added, 1)

            @block.sync
            def _(sp):
                def load_columns(g, number, m):
                    sp.wait_ge(added, m)
                    sp.dma_start(cols[:, :, 0:4 * MAIN_BLOCKS],
                                 dram["main"][bass.ds(g, 1), :, :].rearrange("o p (k s) -> (o p) k s", k=2)).then_inc(main_in, 16)
                    sp.wait_ge(main_in, number * 16)
                    sp.sem_inc(passed, 1)
                    rare = sp.value_load(meta[0:1, 0, 1:2], min_val=0, max_val=SLOTS // 4)
                    with sp.If(rare > MAIN_BLOCKS):
                        sp.dma_start(cols[:, :, 4 * MAIN_BLOCKS:SLOTS],
                                     dram["rare"][bass.ds(g, 1), :, :].rearrange("o p (k s) -> (o p) k s", k=2)).then_inc(rare_in, 16)
                        sp.reg_add(rare_r, rare_r, 16)
                        sp.wait_ge(rare_in, sp.snap(rare_r, min_val=16, max_val=1 << 24))
                        sp.sem_inc(passed, 1)
                    sp.sem_inc(cols_ready, 1)

                rare_r = sp.alloc_register(f"{tag}_rare_loads")
                sp.reg_mov(rare_r, 0)
                over_rest(sp, "sp", load_columns, lambda t, m: None)

            @block.vector
            def _(dve):
                v = nc.vector
                wreg = dve.alloc_register(f"{tag}_window")
                dve.reg_mov(wreg, 0)
                dve.wait_ge(grid_ready, 1)

                def start(g, number, m):
                    dve.reg_mov(wreg, dve.value_load(meta[0:1, 0, 2:3], min_val=0, max_val=NW - 1))
                    dve.wait_ge(cols_ready, number)
                    dve.sem_inc(passed, 1)

                def add_block(t, m):
                    w = dve.snap(wreg, min_val=0, max_val=NW - 1)
                    v.tensor_tensor(hot[:, :, :, :], grid4[:, None, :, :].broadcast_to([P, 2, P, 4]),
                                    cols[:, :, None, bass.ds(t * 4, 4)].broadcast_to([P, 2, P, 4]),
                                    ALU.is_equal).then_inc(hot_ready, 1)
                    dve.wait_ge(block_out, m)
                    v.tensor_reduce(total[:, :], ps_out[:, :, :].rearrange("p t f -> p f t"), AX.X,
                                    ALU.add).then_inc(totalled, 1)
                    dve.wait_ge(totalled, m)
                    to = acc[:, bass.ds(w, 1), :].rearrange("p o f -> p (o f)")
                    v.tensor_tensor(to, to, total[:, :], ALU.add).then_inc(added, 1)
                    dve.wait_ge(added, m + 1)
                    dve.sem_inc(passed, 1)

                over_rest(dve, "dve", start, add_block)

            @block.scalar
            def _(act):
                def copy_counts(t, m):
                    act.wait_ge(cnt_ready, m)
                    nc.scalar.activation(cnts[:, :, :], ps_cnts[:, :, :], ACT.Identity).then_inc(cnt_copied, 1)

                over_rest(act, "act", lambda g, number, m: None, copy_counts)

            @block.tensor
            def _(pe):
                def use(t, m):
                    pe.wait_ge(hot_ready, m)
                    for c in range(4):
                        last = nc.tensor.matmul(ps_cnts[:, c, :], hot[:, 0, :, c], hot[:, 1, :, c], start=True, stop=True)
                    last.then_inc(cnt_ready, 1)
                    tiles = []
                    for c in range(4):
                        a = pe.value_load(meta[0:1, bass.ds(t * 4 + c, 1), 0:1].rearrange("o s k -> o (s k)"),
                                          min_val=0, max_val=NW - 1)
                        tiles.append(parts[:, bass.ds(a, 1), :, :].rearrange("p o t f -> p (o t) f"))
                    pe.wait_ge(cnt_copied, m)
                    for c in range(4):
                        last = nc.tensor.matmul(ps_out[:, :, :], cnts[:, c, :], tiles[c], start=(c == 0), stop=(c == 3))
                    last.then_inc(block_out, 1)

                over_rest(pe, "pe", lambda g, number, m: None, use)


def normalize(nc, tag, x, out, scratch):
    with Phase(nc, tag) as ph:
        stats = ph.sb("stats", [P, 4, NWP])
        eps = ph.sb(f"eps", [P, 1])
        step = ph.sem(f"normalize_steps")
        rooted = ph.sem(f"rooted")
        with nc.Block() as block:
            @block.vector
            def _(dve):
                v = nc.vector
                done = [0]

                def link(ins):
                    done[0] += 1
                    ins.then_inc(step, 1)
                    dve.wait_ge(step, done[0])

                shape = [P, NWP, F]
                v.memset(eps[:, :], 1e-5)
                link(v.tensor_reduce(stats[:, 0, :], x, AX.X, ALU.add))
                link(v.tensor_scalar(stats[:, 1, :], stats[:, 0, :], 1.0 / F, None, ALU.mult))
                link(v.tensor_tensor(out, x, stats[:, 1, :, None].broadcast_to(shape), ALU.subtract))
                link(v.tensor_tensor(scratch, out, out, ALU.mult))
                link(v.tensor_reduce(stats[:, 2, :], scratch, AX.X, ALU.add))
                dve.wait_ge(rooted, 1)
                link(v.reciprocal(stats[:, 0, :], stats[:, 3, :]))
                link(v.scalar_tensor_tensor(out, out, 0.0, stats[:, 0, :, None].broadcast_to(shape), ALU.max, ALU.mult))

            @block.scalar
            def _(act):
                act.wait_ge(step, 5)
                nc.scalar.activation(stats[:, 3, :], stats[:, 2, :], ACT.Sqrt, bias=eps[:, 0:1], scale=1.0 / F).then_inc(rooted, 1)


def split_parts(nc, tag, x, parts, scratch):
    with Phase(nc, tag) as ph:
        half = [ph.sem(f"split{i}") for i in range(4)]
        with nc.Block() as block:
            @block.scalar
            def _(act):
                nc.scalar.activation(parts[:, :, 0, :], x, ACT.Copy).then_inc(half[0], 1)
                act.wait_ge(half[1], 1)
                nc.scalar.activation(parts[:, :, 1, :], scratch, ACT.Copy).then_inc(half[2], 1)

            @block.vector
            def _(dve):
                v = nc.vector
                dve.wait_ge(half[0], 1)
                v.tensor_tensor(scratch, x, parts[:, :, 0, :], ALU.subtract).then_inc(half[1], 1)
                dve.wait_ge(half[2], 1)
                dve.wait_ge(half[1], 1)
                v.tensor_tensor(parts[:, :, 2, :], scratch, parts[:, :, 1, :], ALU.subtract).then_inc(half[3], 1)
                dve.wait_ge(half[3], 1)


def perceptron(nc, tag, ident, x, hidden, last, width, finish):
    with Phase(nc, tag) as ph:
        k = x.shape[2]
        xt = [ph.sb(f"xt{i}", [k, 4 * P]) for i in range(2)]
        hid = [[ph.sb(f"hid{i}_{n}", [P, 4 * P]) for n in range(len(hidden))]
               for i in range(2)]
        ps_t = [ph.ps(f"ps_t{i}", [k, 4, P]) for i in range(2)]
        ps_h = [ph.ps(f"ps_h{i}", [P, 4 * P]) for i in range(2)]
        ps_f = [ph.ps(f"ps_f{i}", [P, 4, width]) for i in range(2)]
        xs = [ph.sb(f"xs{i}", [P, 4, k]) for i in range(2)]
        fetched = ph.sem(f"fetched")
        seen = ph.sem(f"fetched_seen")
        turned = ph.sem(f"turned")
        copied = ph.sem(f"turned_copied")
        product = [ph.sem(f"product{n}") for n in range(len(hidden))]
        relued = [ph.sem(f"relued{n}") for n in range(len(hidden))]
        last_product = ph.sem(f"last_product")
        finished = ph.sem(f"finished")
        finishing = ph.sem(f"finishing")

        def over_batches(eng, stages):
            with eng.Fori(0, NB4 // 2) as i:
                for s in stages:
                    for b in range(2):
                        s(i * 2 + b, b)
            if NB4 % 2:
                for s in stages:
                    s(NB4 - 1, 0)

        with nc.Block() as block:
            @block.tensor
            def _(pe):
                def turn(n, b):
                    pe.wait_ge(fetched, n + 1)
                    pe.sem_inc(seen, 1)
                    for c in range(4):
                        last_ = nc.tensor.transpose(ps_t[b][:, c, :], xs[b][:, c, :], ident[:, :])
                    last_.then_inc(turned, 1)

                def layer(m):
                    def run(n, b):
                        if m:
                            pe.wait_ge(relued[m - 1], n + 1)
                        else:
                            pe.wait_ge(copied, n + 3)
                        nc.tensor.matmul(ps_h[b][:, :], hidden[m][0], (hid[b][m - 1] if m else xt[b])[:, :],
                                         start=True, stop=True).then_inc(product[m], 1)
                    return run

                def back(n, b):
                    pe.wait_ge(relued[-1], n + 1)
                    pe.wait_ge(finished, n + 1)
                    for c in range(4):
                        last_ = nc.tensor.matmul(ps_f[b][:, c, :], hid[b][-1][:, c * P:(c + 1) * P], last,
                                                 start=True, stop=True)
                    last_.then_inc(last_product, 1)

                over_batches(pe, [turn] + [layer(m) for m in range(len(hidden))] + [back])

            @block.gpsimd
            def _(pool):
                pool.sem_inc(copied, 2)

                def fetch(n, b):
                    pool.wait_ge(copied, n + 1)
                    nc.gpsimd.tensor_copy(xs[b][:, :, :], x[:, bass.ds(n * 4, 4), :]).then_inc(fetched, 1)

                over_batches(pool, [fetch])

            @block.scalar
            def _(act):
                def relu(m):
                    def run(n, b):
                        act.wait_ge(product[m], n + 1)
                        nc.scalar.activation(hid[b][m][:, :], ps_h[b][:, :], ACT.Relu, bias=hidden[m][1]).then_inc(relued[m], 1)
                    return run

                over_batches(act, [relu(m) for m in range(len(hidden))])

            @block.vector
            def _(dve):
                dve.sem_inc(finished, 2)

                def copy(n, b):
                    dve.wait_ge(turned, n + 1)
                    nc.vector.tensor_copy(xt[b][:, :].rearrange("p (c e) -> p c e", c=4), ps_t[b][:, :, :]).then_inc(copied, 1)

                def end(n, b):
                    dve.wait_ge(last_product, n + 1)
                    finish(dve, n, ps_f[b], finishing).then_inc(finished, 1)

                over_batches(dve, [copy, end])


_INS = ["x", "src", "dst",
        "L0_gnn_W1", "L0_gnn_b1", "L0_gnn_W2", "L0_gnn_b2", "L0_gnn_W3", "L0_gnn_b3", "L0_gnn_W4", "L0_gnn_b4",
        "L1_gnn_WM1", "L1_gnn_bM1", "L1_gnn_WM2", "L1_gnn_bM2", "L1_gnn_WM3", "L1_gnn_bM3",
        "L1_gnn_WU1", "L1_gnn_bU1", "L1_gnn_WU2", "L1_gnn_bU2", "L1_gnn_WU3", "L1_gnn_bU3"]


def gnn(nc, a, out):
    with ExitStack() as ctx:
        def sb(name, shape, dt=FP32):
            return ctx.enter_context(nc.sbuf_tensor(name, shape, dt))

        MAIN = 4 * MAIN_BLOCKS
        dram = {
            "main": nc.dram_tensor("main_columns", [GMAX, P, 2 * MAIN], BF16).ap(),
            "rare": nc.dram_tensor("rare_columns", [GMAX, P, 2 * (SLOTS - MAIN)], BF16).ap(),
            "meta": nc.dram_tensor("group_tables", [GMAX, P, 4], I32).ap(),
            "window": nc.dram_tensor("window_table", [2 * NW], I32).ap(),
            "counts": nc.dram_tensor("edge_counts", [KEPT, P, MAIN * P], BF16).ap(),
        }

        row = sb("row", [1, 2 * NW + 3], I32)
        left = sb("left", [1, 1], I32)
        ident = sb("identity", [P, P])
        xres = sb("xres", [P, NWP, F])
        feat = sb("feat", [P, NWP, H])

        weight, bias = {}, {}
        LAST = ("L0_gnn_b2", "L0_gnn_b4", "L1_gnn_bM3", "L1_gnn_bU3")
        for name in _INS[3:]:
            if a[name].shape.__len__() == 2:
                weight[name] = sb("w_" + name, list(a[name].shape))
            elif name in LAST:
                bias[name] = sb("b_" + name, [P, a[name].shape[0]])
            else:
                bias[name] = sb("b_" + name, [a[name].shape[0], 1])

        whole = N // P
        loaded = ctx.enter_context(nc.semaphore("inputs_loaded"))
        zeroed = ctx.enter_context(nc.semaphore("padding_zeroed"))
        idx = ctx.enter_context(nc.semaphore("index_ready"))
        with nc.sbuf_tensor("ramp", [P, P], FP32) as ramp, nc.sbuf_tensor("lane", [P, 1], FP32) as lane, nc.Block() as block:
            @block.sync
            def _(sp):
                loads = 0
                for name in _INS[3:]:
                    if name in weight:
                        sp.dma_start(weight[name][:, :], a[name]).then_inc(loaded, 16)
                    elif name in LAST:
                        w = a[name].shape[0]
                        sp.dma_start(bias[name][:, :], a[name].rearrange("(o f) -> o f", o=1).broadcast_to([P, w])
                                     ).then_inc(loaded, 16)
                    else:
                        sp.dma_start(bias[name][:, :], a[name].rearrange("(f o) -> f o", o=1)).then_inc(loaded, 16)
                    loads += 1
                sp.wait_ge(zeroed, 1)
                sp.dma_start(xres[:, 0:whole, :], a["x"][0:whole * P, :].rearrange("(w p) f -> p w f", p=P)).then_inc(loaded, 16)
                sp.dma_start(xres[0:N - whole * P, whole, :], a["x"][whole * P:N, :]).then_inc(loaded, 16)
                sp.wait_ge(loaded, 16 * (loads + 2))

            @block.gpsimd
            def _(pool):
                nc.gpsimd.memset(xres[:, whole:NWP, :], 0.0).then_inc(zeroed, 1)
                kw = dict(allow_small_or_imprecise_dtypes=True)
                nc.gpsimd.iota(ramp[:, :], [[1, P]], 0, 0, **kw).then_inc(idx, 1)
                nc.gpsimd.iota(lane[:, :], [[0, 1]], 0, 1, **kw).then_inc(idx, 1)

            @block.vector
            def _(dve):
                dve.wait_ge(idx, 2)
                nc.vector.tensor_scalar(ident[:, :], ramp[:, :], lane[:, 0:1], None, ALU.is_equal).then_inc(idx, 1)
                dve.wait_ge(idx, 3)

        sort_edges(nc, "sort", a["src"], a["dst"], dram, row, left)

        parts = sb("parts", [P, NWP, 3, H], BF16)
        parts64 = parts[:, :, :, :].rearrange("p w t f -> p (w t f)")[:, 0:NWP * 3 * F].rearrange(
            "p (w t f) -> p w t f", t=3, f=F)
        scratch = sb("scratch", [P, NWP, H])
        h64, z64 = feat[:, :, 0:F], feat[:, :, F:H]
        W, Bc = weight, bias

        def biased(name, out_of, width, relu=False):
            def finish(dve, n, ps, sem):
                v = nc.vector
                to = out_of[:, bass.ds(n * 4, 4), :]
                ins = v.tensor_tensor(to, ps[:, :, :], Bc[name][:, None, :].broadcast_to([P, 4, width]), ALU.add)
                if not relu:
                    return ins
                ins.then_inc(sem, 1)
                dve.wait_ge(sem, n + 1)
                return v.tensor_scalar(to, to, 0.0, None, ALU.max)
            return finish

        normalize(nc, "norm0", xres[:, :, :], h64, scratch[:, :, 0:F])
        split_parts(nc, "split0", h64, parts64, scratch[:, :, 0:F])
        aggregate(nc, "sum0", dram, row, parts64, F, h64, build=True)
        aggregate_rest(nc, "sum0r", dram, row, left, parts64, F, h64)
        perceptron(nc, "mlp0", ident, h64, [(W["L0_gnn_W1"][:, :], Bc["L0_gnn_b1"][:, 0:1])], W["L0_gnn_W2"][:, :], H,
                   biased("L0_gnn_b2", feat[:, :, :], H, relu=True))
        split_parts(nc, "split1", feat[:, :, :], parts[:, :, :, :], scratch[:, :, :])
        aggregate(nc, "sum1", dram, row, parts[:, :, :, :], H, feat[:, :, :], build=False)
        aggregate_rest(nc, "sum1r", dram, row, left, parts[:, :, :, :], H, feat[:, :, :])
        perceptron(nc, "mlp1", ident, feat[:, :, :], [(W["L0_gnn_W3"][:, :], Bc["L0_gnn_b3"][:, 0:1])], W["L0_gnn_W4"][:, :], F,
                   residual(nc, Bc["L0_gnn_b4"], xres[:, :, :], xres[:, :, :], scratch[:, :, 0:F]))
        normalize(nc, "norm1", xres[:, :, :], h64, scratch[:, :, 0:F])
        perceptron(nc, "mlp2", ident, h64, [(W["L1_gnn_WM1"][:, :], Bc["L1_gnn_bM1"][:, 0:1]),
                                    (W["L1_gnn_WM2"][:, :], Bc["L1_gnn_bM2"][:, 0:1])], W["L1_gnn_WM3"][:, :], F,
                   biased("L1_gnn_bM3", z64, F))
        split_parts(nc, "split2", z64, parts64, scratch[:, :, 0:F])
        clear(nc, z64)
        aggregate(nc, "sum2", dram, row, parts64, F, z64, build=False)
        aggregate_rest(nc, "sum2r", dram, row, left, parts64, F, z64)
        perceptron(nc, "mlp3", ident, feat[:, :, :], [(W["L1_gnn_WU1"][:, :], Bc["L1_gnn_bU1"][:, 0:1]),
                                              (W["L1_gnn_WU2"][:, :], Bc["L1_gnn_bU2"][:, 0:1])], W["L1_gnn_WU3"][:, :], F,
                   residual(nc, Bc["L1_gnn_bU3"], xres[:, :, :], xres[:, :, :], scratch[:, :, 0:F]))

        stored = ctx.enter_context(nc.semaphore("result_stored"))
        with nc.Block() as block:
            @block.sync
            def _(sp):
                sp.dma_start(out[0:whole * P, :].rearrange("(w p) f -> p w f", p=P), xres[:, 0:whole, :]).then_inc(stored, 16)
                sp.dma_start(out[whole * P:N, :], xres[0:N - whole * P, whole, :]).then_inc(stored, 16)
                sp.wait_ge(stored, 32)


def residual(nc, bias, x, to, scratch):
    def finish(dve, n, ps, sem):
        v = nc.vector
        mid = scratch[:, bass.ds(n * 4, 4), :]
        v.tensor_tensor(mid, ps[:, :, :], bias[:, None, :].broadcast_to([P, 4, F]), ALU.add).then_inc(sem, 1)
        dve.wait_ge(sem, n + 1)
        return v.tensor_tensor(to[:, bass.ds(n * 4, 4), :], mid, x[:, bass.ds(n * 4, 4), :], ALU.add)
    return finish


def clear(nc, x):
    with nc.Block() as block:
        @block.vector
        def _(dve):
            nc.vector.memset(x, 0.0)


def kernel(**inputs):
    import concourse.bacc as bacc
    from concourse.bass_utils import run_bass_kernel_spmd

    nc = bacc.Bacc("TRN2", target_bir_lowering=False, num_devices=1)
    arrays, aps = {}, {}
    for name in _INS:
        arr = np.ascontiguousarray(inputs[name])
        arrays[f"in_{name}"] = arr
        aps[name] = nc.dram_tensor(f"in_{name}", arr.shape, mybir.dt.from_np(arr.dtype), kind="ExternalInput").ap()
    out = nc.dram_tensor("out", (N, F), FP32, kind="ExternalOutput").ap()
    gnn(nc, aps, out)
    r = run_bass_kernel_spmd(nc, [arrays], core_ids=[0])
    return r.results[0]["out"]
```

```python
import numpy as np
import concourse.bass as bass
from concourse import mybir
from contextlib import ExitStack

FP32 = mybir.dt.float32
BF16 = mybir.dt.bfloat16
I32 = mybir.dt.int32
ALU = mybir.AluOpType
ACT = mybir.ActivationFunctionType
AX = mybir.AxisListType

P = 128
N = 6250
E = 206250
F = 64
H = 128
NW = -(-N // P)
NWP = -(-NW // 4) * 4
NB4 = NWP // 4
NT = -(-E // (P * P))
NCH = -(-E // P)
J = -(-(E // NW) // P) + 3
COLS = NT * P + 40
XM = J - 1
MAIN_X = 1
MAIN = NW + MAIN_X
MAIN_BLOCKS = -(-MAIN // 4)
RARE_BLOCKS = -(-(XM - MAIN_X) // 4)
SLOTS = 4 * (MAIN_BLOCKS + RARE_BLOCKS)
COUNT_STEPS = 7
RANK_STEPS = 8
ROWS_DONE = 10
ENDS_DONE = 15
GMAX = NW * -(-NCH // J) + 3
RB = 8192
FAR = 64 * P
SKIP = NT * P
KEPT = 64
PICK = NW // 7 // 2 * 7 + 7
assert J * P < RB and NW <= 64


class Phase:

    def __init__(self, nc, tag):
        self.nc, self.tag, self.ctx, self.sems = nc, tag, ExitStack(), []

    def sb(self, name, shape, dt=FP32):
        return self.ctx.enter_context(self.nc.sbuf_tensor(f"{self.tag}_{name}", shape, dt))

    def ps(self, name, shape, dt=FP32):
        return self.ctx.enter_context(self.nc.psum_tensor(f"{self.tag}_{name}", shape, dt))

    def sem(self, name):
        self.sems.append(self.ctx.enter_context(self.nc.semaphore(f"{self.tag}_{name}")))
        return self.sems[-1]

    def __enter__(self):
        return self

    def __exit__(self, *error):
        if error[0] is None:
            with self.nc.Block() as block:
                @block.gpsimd
                def _(pool):
                    for s in self.sems:
                        pool.sem_clear(s)
        return self.ctx.__exit__(*error)


def group_pairs(eng, row):
    return eng.value_load(row[0:1, 2 * NW:2 * NW + 1], min_val=NW // 2 - 2, max_val=GMAX // 2 - 2) + 2


def sort_edges(nc, tag, src, dst, dram, row, left, load_rest):
    with ExitStack() as ctx:
        def sb(name, shape, dt):
            return ctx.enter_context(nc.sbuf_tensor(name, shape, dt))

        key = sb("key", [P, COLS], FP32)
        tile_of = sb("tile_of", [P, COLS], BF16)
        low = sb("low", [P, 2, COLS], BF16)
        ident = sb("ident", [P, P], FP32)
        tri = sb("tri", [P, P], BF16)
        ones = sb("ones", [P, P], BF16)
        free = sb("free", [P, P], FP32)
        part = sb("part", [P, 1], FP32)
        part_k = sb("part_k", [P, 1], FP32)
        window_no = sb("window_no", [P, NW], FP32)
        minus64w = sb("minus64w", [P, NW], FP32)
        grid_k = sb("grid_k", [P, P, J], BF16)
        grid_a = sb("grid_a", [P, NW, J], BF16)
        grid_x = sb("grid_x", [P, MAIN_X, J], FP32)
        grid_r = sb("grid_r", [P, SLOTS - MAIN], FP32)
        tile_rb = sb("tile_rb", [P, NW], FP32)
        lane_x = sb("lane_x", [P, 3], FP32)
        sort_phase = ctx.enter_context(Phase(nc, "sort"))
        grids = sort_phase.sem("grids_ready")

        with Phase(nc, "columns") as ph:
            tmp = ph.sb

            srow = tmp("srow", [P, NT, P], I32)
            drow = tmp("drow", [P, NT, P], I32)
            bits = tmp("bits", [P, NT, P], I32)
            hi = tmp("hi", [P, NT, P], I32)
            rows = [tmp(n, [P, NT, P], FP32) for n in ("key_row", "tile_row", "slow_row", "dlow_row")]
            dhi = tmp("dhi", [P, NT, P], FP32)
            dmax = tmp("dmax", [P, NT], FP32)
            dmin = tmp("dmin", [P, NT], FP32)
            cid1 = tmp("cid1", [P, NT], FP32)
            wgrid = tmp("wgrid", [P, NW, NT], FP32)
            hit = tmp("hit", [P, 2, NW, NT], FP32)
            ends = tmp("ends", [P, 2, NW], FP32)
            span = tmp("span", [NW, 4], FP32)
            span_i = tmp("span_i", [NW, 2], I32)
            steps = tmp("steps", [NW, NCH // J + 1], FP32)
            stepped = tmp("stepped", [NW, NCH // J + 1], FP32)
            onesf = tmp("onesf", [NW, P], FP32)
            pairs_i = tmp("pairs_i", [1, 2], I32)
            pairs_f = tmp("pairs_f", [1, 1], FP32)
            pt = [ph.ps(f"pt{i}", [P, 4, P]) for i in range(4)]
            pe_ends = ph.ps("pe_ends", [NW, 2, P])
            pe_tot = ph.ps("pe_tot", [P, 1])

            loaded = ph.sem("edges_loaded")
            padded = ph.sem("padding_set")
            consts = ph.sem("constants_ready")
            step = ph.sem("vector_steps")
            turned = ph.sem("columns_turned")
            copied = [ph.sem(f"columns_copied{i}") for i in range(2)]
            ends_turned = ph.sem("ends_turned")
            counted = ph.sem("groups_counted")
            summed = ph.sem("groups_summed")
            table_out = ph.sem("table_written")
            table_in = ph.sem("table_read")
            table_done = ph.sem("table_ready")

            full = E // P
            in_last = full - (NT - 1) * P
            rest = E - full * P

            with nc.Block() as block:
                @block.sync
                def _(sp):
                    sp.wait_ge(padded, 2)
                    for edges, to in ((dst, drow), (src, srow)):
                        sp.dma_start(to[:, 0:NT - 1, :],
                                     edges[0:(NT - 1) * P * P].rearrange("(t c e) -> c t e", c=P, e=P)
                                     ).then_inc(loaded, 16)
                        sp.dma_start(to[0:in_last, NT - 1, :],
                                     edges[(NT - 1) * P * P:full * P].rearrange("(c e) -> c e", e=P)
                                     ).then_inc(loaded, 16)
                        if rest:
                            sp.dma_start(to[in_last:in_last + 1, NT - 1, 0:rest],
                                         edges[full * P:E].rearrange("(c e) -> c e", c=1)
                                         ).then_inc(loaded, 16)
                    load_rest(sp)
                    sp.wait_ge(table_done, 1)
                    sp.dma_start(dram["window"][:].rearrange("(w k) -> w k", k=2),
                                 span_i[:, :]).then_inc(table_out, 16)
                    sp.wait_ge(table_out, 16)
                    sp.dma_start(row[:, 0:2 * NW], dram["window"][:].rearrange("(o k) -> o k", o=1)
                                 ).then_inc(table_in, 16)
                    sp.wait_ge(table_in, 16)

                @block.gpsimd
                def _(pool):
                    nc.gpsimd.memset(drow[:, NT - 1, :], FAR).then_inc(padded, 1)
                    nc.gpsimd.memset(srow[:, NT - 1, :], 0).then_inc(padded, 1)
                    kw = dict(allow_small_or_imprecise_dtypes=True)
                    nc.gpsimd.iota(free[:, :], [[1, P]], 0, 0, **kw).then_inc(consts, 1)
                    nc.gpsimd.iota(part[:, :], [[0, 1]], 0, 1, **kw).then_inc(consts, 1)
                    nc.gpsimd.iota(window_no[:, :], [[1, NW]], 0, 0, **kw).then_inc(consts, 1)
                    nc.gpsimd.iota(minus64w[:, :], [[-64, NW]], 0, 0, **kw).then_inc(consts, 1)
                    nc.gpsimd.iota(cid1[:, :], [[P, NT]], 1, 1, **kw).then_inc(consts, 1)
                    nc.gpsimd.iota(wgrid[:, :, :], [[1, NW], [0, NT]], 0, 0, **kw).then_inc(consts, 1)
                    nc.gpsimd.iota(steps[:, :], [[J, NCH // J + 1]], 0, 0, **kw).then_inc(consts, 1)
                    nc.gpsimd.memset(ones[:, :], 1.0)
                    nc.gpsimd.memset(onesf[:, :], 1.0)
                    nc.gpsimd.memset(key[:, NT * P:COLS], float(FAR))
                    nc.gpsimd.memset(tile_of[:, NT * P:COLS], 0.0)
                    nc.gpsimd.memset(low[:, :, NT * P:COLS], 0.0).then_inc(consts, 1)
                    nc.gpsimd.iota(grid_a[:, :, :], [[1, NW], [0, J]], 0, 0, **kw)
                    nc.gpsimd.iota(tile_rb[:, :], [[RB, NW]], 0, 0, **kw)
                    nc.gpsimd.iota(lane_x[:, 0:1], [[0, 1]], -NW, 1, **kw)
                    nc.gpsimd.iota(grid_k[:, :, :], [[1, P], [0, J]], 0, 0, **kw)
                    nc.gpsimd.iota(grid_x[:, :, :], [[1, MAIN_X], [0, J]], 1, 0, **kw)
                    nc.gpsimd.iota(grid_r[:, :], [[1, SLOTS - MAIN]], MAIN_X + 1, 0, **kw).then_inc(grids, 1)

                @block.vector
                def _(dve):
                    done = [0]

                    def link(ins):
                        done[0] += 1
                        ins.then_inc(step, 1)
                        dve.wait_ge(step, done[0])

                    v = nc.vector
                    dve.wait_ge(consts, 8)
                    v.tensor_scalar(ident[:, :], free[:, :], part[:, 0:1], None, ALU.is_equal)
                    link(v.tensor_scalar(tri[:, :], free[:, :], part[:, 0:1], None, ALU.is_gt))
                    key_row, tile_row, slow_row, dlow_row = rows
                    dve.wait_ge(loaded, 96 if rest else 64)
                    link(v.tensor_scalar(hi[:, :, :], drow[:, :, :], 7, 6, ALU.logical_shift_right, ALU.logical_shift_left))
                    v.tensor_scalar(key_row[:, :, :], hi[:, :, :], 1.0, None, ALU.mult)
                    link(v.tensor_scalar(bits[:, :, :], srow[:, :, :], 7, None, ALU.logical_shift_right))
                    link(v.tensor_copy(tile_row[:, :, :], bits[:, :, :]))
                    link(v.tensor_scalar(dhi[:, :, :], hi[:, :, :], 1.0 / 64, None, ALU.mult))
                    link(v.tensor_tensor(key_row[:, :, :], key_row[:, :, :], tile_row[:, :, :], ALU.add))
                    link(v.tensor_scalar(bits[:, :, :], srow[:, :, :], 127, None, ALU.bitwise_and))
                    link(v.tensor_scalar(slow_row[:, :, :], bits[:, :, :], 1.0, None, ALU.add))
                    link(v.tensor_scalar(hi[:, :, :], drow[:, :, :], 127, None, ALU.bitwise_and))
                    link(v.tensor_scalar(dlow_row[:, :, :], hi[:, :, :], 1.0, None, ALU.add))
                    rows_done = done[0]
                    assert rows_done == ROWS_DONE
                    v.tensor_reduce(dmax[:, :], dhi[:, :, :], AX.X, ALU.max)
                    link(v.tensor_reduce(dmin[:, :], dhi[:, :, :], AX.X, ALU.min))
                    wide = [P, NW, NT]
                    v.tensor_tensor(hit[:, 0, :, :], dmax[:, None, :].broadcast_to(wide), wgrid[:, :, :], ALU.is_ge)
                    link(v.tensor_tensor(hit[:, 1, :, :], dmin[:, None, :].broadcast_to(wide), wgrid[:, :, :], ALU.is_le))
                    link(v.tensor_scalar(dmax[:, :], cid1[:, :], float(-1 - NT * P), None, ALU.add))
                    v.tensor_tensor(hit[:, 0, :, :], hit[:, 0, :, :], dmax[:, None, :].broadcast_to(wide), ALU.mult)
                    link(v.tensor_tensor(hit[:, 1, :, :], hit[:, 1, :, :], cid1[:, None, :].broadcast_to(wide), ALU.mult))
                    v.tensor_reduce(ends[:, 0, :], hit[:, 0, :, :], AX.X, ALU.min)
                    link(v.tensor_reduce(ends[:, 1, :], hit[:, 1, :, :], AX.X, ALU.max))
                    assert done[0] == ENDS_DONE
                    for t in range(0, NT, 2):
                        dve.wait_ge(turned, t + 1)
                        c = slice(t * P, (t + 1) * P)
                        b = pt[t % 4]
                        v.tensor_copy(key[:, c], b[:, 0, :])
                        v.tensor_copy(tile_of[:, c], b[:, 1, :])
                        v.tensor_copy(low[:, :, c], b[:, 2:4, :]).then_inc(copied[0], 1)
                    dve.wait_ge(ends_turned, 2)
                    v.tensor_reduce(span[:, 0:1], pe_ends[:, 0, :], AX.X, ALU.min)
                    link(v.tensor_reduce(span[:, 1:2], pe_ends[:, 1, :], AX.X, ALU.max))
                    link(v.tensor_scalar(span[:, 0:1], span[:, 0:1], float(NT * P), None, ALU.add))
                    link(v.tensor_tensor(span[:, 2:3], span[:, 1:2], span[:, 0:1], ALU.subtract))
                    link(v.tensor_scalar(stepped[:, :], steps[:, :], span[:, 2:3], None, ALU.is_lt))
                    link(v.tensor_reduce(span[:, 3:4], stepped[:, :], AX.X, ALU.add))
                    link(v.tensor_scalar(span[:, 3:4], span[:, 3:4], 1.0, None, ALU.max))
                    v.tensor_copy(span_i[:, 0:1], span[:, 0:1])
                    v.tensor_copy(span_i[:, 1:2], span[:, 3:4]).then_inc(table_done, 1)
                    v.engine_nop().then_inc(counted, 1)
                    dve.wait_ge(summed, 1)
                    link(v.tensor_scalar(pairs_i[:, 0:1], pe_tot[0:1, :], -3.0, None, ALU.add))
                    link(v.tensor_scalar(pairs_i[:, 1:2], pairs_i[:, 0:1], 1, None, ALU.logical_shift_right))
                    link(v.tensor_copy(pairs_f[:, 0:1], pairs_i[:, 1:2]))
                    v.tensor_copy(row[:, 2 * NW:2 * NW + 1], pairs_f[:, 0:1])
                    v.tensor_scalar(row[:, 2 * NW + 1:2 * NW + 2], pairs_f[:, 0:1], float(KEPT // 2 - 2), None, ALU.min)
                    v.tensor_scalar(row[:, 2 * NW + 2:2 * NW + 3], pairs_f[:, 0:1], 2.0, 4.0, ALU.mult, ALU.add).then_inc(table_done, 1)

                @block.scalar
                def _(act):
                    for t in range(1, NT, 2):
                        act.wait_ge(turned, t + 1)
                        c = slice(t * P, (t + 1) * P)
                        b = pt[t % 4]
                        nc.scalar.activation(key[:, c], b[:, 0, :], ACT.Identity)
                        nc.scalar.activation(tile_of[:, c], b[:, 1, :], ACT.Identity)
                        nc.scalar.activation(low[:, :, c], b[:, 2:4, :], ACT.Identity).then_inc(copied[1], 1)

                @block.tensor
                def _(pe):
                    pe.wait_ge(step, ROWS_DONE)
                    for t in range(NT):
                        if t >= 4:
                            pe.wait_ge(copied[t % 2], (t - 4) // 2 + 1)
                        for k in range(4):
                            last = nc.tensor.transpose(pt[t % 4][:, k, :], rows[k][:, t, :], ident[:, :])
                        last.then_inc(turned, 1)
                    pe.wait_ge(step, ENDS_DONE)
                    for k in range(2):
                        nc.tensor.transpose(pe_ends[:, k, :], ends[:, k, :], ident[:, :]).then_inc(ends_turned, 1)
                    pe.wait_ge(counted, 1)
                    nc.tensor.matmul(pe_tot[:, :], onesf[:, :], span[:, 3:4], start=True, stop=True).then_inc(summed, 1)

        ph = sort_phase
        sb = ph.sb

        def pair(name, shape, dt):
            return [ph.sb(f"{name}{i}", shape, dt) for i in range(2)]

        stage_key = sb("stage_key", [P, 2, J], BF16)
        stage_tile = sb("stage_tile", [P, 2, J], BF16)
        stage_low = sb("stage_low", [P, 2, 2, J], BF16)
        stage_win = sb("stage_win", [P, 2, 1], FP32)
        bucket = sb("bucket", [P, 2, NW, J], BF16)
        bucket_kept = sb("bucket_kept", [P, 2, NW, J], BF16)
        place = pair("place", [P, P, J], BF16)
        cargo = pair("cargo", [P, 2, SLOTS, J], BF16)
        extra = pair("extra", [P, MAIN_X, J], BF16)
        low_main = pair("low_main", [P, 2, J], BF16)
        low_f = sb("low_f", [P, 2, J])
        resets = sb("resets", [P, NW, J])
        ranks = sb("ranks", [P, NW, J])
        picked = sb("picked", [P, NW, J])
        rank = sb("rank", [P, J])
        fields = sb("fields", [P, 5, J], I32)
        row_of = pair("row_of", [P, J], BF16)
        is_main = sb("is_main", [P, J], BF16)
        is_extra = sb("is_extra", [P, J], BF16)
        xslot = pair("xslot", [P, J], FP32)
        nx_i = sb("nx_i", [P, 2, NW], I32)
        nx = sb("nx", [P, 3, NW])
        nx_end = pair("nx_end", [P, NW], FP32)
        nx_all = sb("nx_all", [P, 1], I32)
        rare_max = sb("rare_max", [P, 1])
        left_f = sb("left_f", [1, 2])
        ones_f = sb("ones_f", [P, NW])
        ended = sb("ended", [P, NW - 1])
        ended_n = sb("ended_n", [P, 1])
        meta = pair("meta", [P, 4], I32)
        sorted_sb = pair("sorted_sb", [P, 2, SLOTS], BF16)
        ps_base = [ph.ps(f"ps_base{i}", [P, NW]) for i in range(2)]
        ps_cnt = [ph.ps(f"ps_cnt{i}", [P, NW]) for i in range(2)]
        ps_rank = ph.ps("ps_rank", [P, 7, J])
        ps_sorted = [ph.ps(f"ps_sorted{i}", [P, 2, SLOTS]) for i in range(2)]
        assert NW % 7 == 0

        sem = ph.sem
        lanes = sem("lanes_ready")
        zeroed = sem("rare_columns_zeroed")
        staged = sem("staged")
        key_staged = sem("key_staged")
        bucket_copied = sem("bucket_copied")
        stage_free_pool = sem("stage_free_pool")
        stage_free_dve = sem("stage_free_dve")
        bucketed = sem("bucketed")
        based = sem("based")
        count_steps = sem("count_steps")
        scanned = sem("scanned")
        steps = sem("rank_steps")
        meta_steps = sem("meta_steps")
        resets_set = sem("resets_set")
        rare_ready = sem("rare_ready")
        rare_seen = sem("rare_seen")
        picked_ready = sem("picked_ready")
        picked_by_pool = sem("picked_by_pool")
        summed = sem("ranks_summed")
        rare_scalars = sem("rare_scalars")
        extra_ready = sem("extra_ready")
        main_ready = sem("main_ready")
        placed = sem("placed")
        meta_ready = sem("meta_ready")
        cargoed = sem("cargoed")
        permuted = sem("permuted")
        sorted_out = sem("sorted_copied")
        stored = [sem(f"stored{i}") for i in range(2)]
        rare_stored = [sem(f"rare_stored{i}") for i in range(2)]
        meta_stored = [sem(f"meta_stored{i}") for i in range(2)]
        passed = sem("passed")

        def over_groups(eng, body):
            n = group_pairs(eng, row)
            body(0, 0, 0, 2)
            body(1, 1, 1, 2)
            with eng.Fori(1, n - 1) as i:
                body(i * 2, 0, 2, 2)
                body(i * 2 + 1, 1, 2, 2)
            body(n * 2 - 2, 0, 2, 1)
            body(n * 2 - 1, 1, 2, 0)
            return n

        with nc.Block() as block:
            @block.scalar
            def _(act):
                registers = {n: act.alloc_register(f"act_{n}") for n in ("number", "column", "column_before", "window_before")}

                def value(name, least, most):
                    return act.snap(registers[name], min_val=least, max_val=most)

                def stage_key_of(col, w):
                    m = value("number", 1, GMAX)
                    act.wait_ge(bucketed, m)
                    nc.scalar.activation(stage_key[:, bass.ds((m + 1) & 1, 1), :].rearrange("p o j -> p (o j)"),
                                         key[:, bass.ds(col, J)], ACT.Identity,
                                         bias=minus64w[:, bass.ds(w, 1)]).then_inc(key_staged, 1)

                def stage_rest(m, col, w):
                    b = (m + 1) & 1

                    def of(t):
                        return t[:, bass.ds(b, 1), :].rearrange("p o j -> p (o j)")

                    act.wait_ge(stage_free_pool, m)
                    act.wait_ge(stage_free_dve, m)
                    nc.scalar.activation(of(stage_tile), tile_of[:, bass.ds(col, J)], ACT.Identity)
                    nc.scalar.activation(of(stage_win), window_no[:, bass.ds(w, 1)], ACT.Identity)
                    nc.scalar.activation(stage_low[:, bass.ds(b, 1), :, :].rearrange("p o k j -> p (o k) j"), low[:, :, bass.ds(col, J)],
                                         ACT.Identity).then_inc(staged, 1)
                    act.wait_ge(bucketed, m + 2)
                    act.wait_ge(cargoed, m)
                    nc.scalar.activation(bucket_kept[:, bass.ds(b, 1), :, :].rearrange("p o a j -> p (o a j)"),
                                         bucket[:, bass.ds(b, 1), :, :].rearrange("p o a j -> p (o a j)"),
                                         ACT.Identity).then_inc(bucket_copied, 1)

                def stage_before():
                    stage_rest(value("number", 2, GMAX) - 1, value("column_before", 0, SKIP), value("window_before", 0, NW - 1))

                act.reg_mov(registers["number"], 1)
                act.reg_mov(registers["column_before"], 0)
                act.reg_mov(registers["window_before"], 0)
                with act.Fori(0, NW) as w:
                    act.reg_mov(registers["column"], act.value_load(row[0:1, bass.ds(w * 2, 1)], min_val=0, max_val=NT * P))
                    n = act.value_load(row[0:1, bass.ds(w * 2 + 1, 1)], min_val=1, max_val=NCH // J + 1)
                    with act.Fori(0, n):
                        stage_key_of(value("column", 0, SKIP), w)
                        with act.If(value("number", 1, GMAX) > 1):
                            stage_before()
                        act.reg_mov(registers["column_before"], registers["column"])
                        act.reg_mov(registers["window_before"], w)
                        act.reg_add(registers["column"], registers["column"], J)
                        act.reg_add(registers["number"], registers["number"], 1)
                lone = act.snap((value("number", 1, GMAX) + 1) & 1, min_val=0, max_val=1)
                with act.If(lone > 0):
                    stage_key_of(SKIP, NW - 1)
                stage_before()
                with act.If(lone > 0):
                    stage_rest(value("number", 1, GMAX), SKIP, NW - 1)

            @block.gpsimd
            def _(pool):
                pool.sem_inc(stage_free_pool, 2)
                pool.sem_inc(cargoed, 2)
                for b in range(2):
                    nc.gpsimd.memset(cargo[b][:, :, MAIN:SLOTS, :], 0.0).then_inc(zeroed, 1)
                dirty = [pool.alloc_register(f"pool_dirty{b}") for b in range(2)]
                for b in range(2):
                    pool.reg_mov(dirty[b], 0)
                copies = pool.alloc_register("pool_rare_groups")
                pool.reg_mov(copies, 1)

                def pick(g, b):
                    pool.wait_ge(scanned, g + 1)
                    nc.gpsimd.tensor_tensor(picked[:, PICK:NW, :], ranks[:, PICK:NW, :], bucket[:, b, PICK:NW, :],
                                            ALU.mult).then_inc(picked_by_pool, 1)

                def cargo_of(g, b, before, behind):
                    pool.wait_ge(rare_ready, g + 1)
                    pool.sem_inc(passed, 1)
                    rare = pool.value_load(meta[b][0:1, 1:2], min_val=0, max_val=RARE_BLOCKS)
                    pool.sem_inc(rare_seen, 1)
                    pool.wait_ge(extra_ready, g + 1)
                    pool.wait_ge(permuted, g + 1)
                    pool.sem_inc(passed, 1)
                    with pool.If(pool.snap(dirty[b], min_val=0, max_val=1) > 0):
                        nc.gpsimd.memset(cargo[b][:, :, MAIN:SLOTS, :], 0.0).then_inc(zeroed, 1)
                        pool.reg_mov(dirty[b], 0)
                    with pool.If(rare > 0):
                        done = pool.snap(copies, min_val=1, max_val=1 << 20)
                        nc.gpsimd.tensor_copy(low_f[:, :, :], stage_low[:, b, :, :]).then_inc(rare_scalars, 1)
                        pool.wait_ge(rare_scalars, done)
                        pool.sem_inc(passed, 1)
                        for k in range(2):
                            for j in range(J):
                                nc.gpsimd.tensor_scalar(cargo[b][:, k, MAIN:SLOTS, j], grid_r[:, :], xslot[b][:, j:j + 1],
                                                        low_f[:, k, j:j + 1], ALU.is_equal, ALU.mult)
                        pool.reg_mov(dirty[b], 1)
                        pool.reg_add(copies, copies, 1)
                    for k in range(2):
                        last = nc.gpsimd.tensor_tensor(cargo[b][:, k, NW:MAIN, :], extra[b][:, :, :],
                                                       stage_low[:, b, k, None, :].broadcast_to([P, MAIN_X, J]), ALU.mult)
                    last.then_inc(stage_free_pool, 1)
                    if behind:
                        pick(g + 1, 1 - b)
                    pool.wait_ge(main_ready, g + 1)
                    pool.wait_ge(bucket_copied, g + 1)
                    for k in range(2):
                        last = nc.gpsimd.tensor_tensor(cargo[b][:, k, 0:NW, :], bucket_kept[:, b, :, :],
                                                       low_main[b][:, k, None, :].broadcast_to([P, NW, J]), ALU.mult)
                    last.then_inc(cargoed, 1)

                pick(0, 0)
                over_groups(pool, cargo_of)

            @block.vector
            def _(dve):
                v = nc.vector
                dve.sem_inc(stage_free_dve, 2)
                dve.sem_inc(bucketed, 2)
                dve.sem_inc(sorted_out, 2)
                v.memset(resets[:, :, :], 0.0)
                v.memset(rare_max[:, :], 0.0)
                v.memset(ones_f[:, :], 1.0)
                dve.wait_ge(grids, 1)
                v.tensor_scalar(lane_x[:, 1:2], lane_x[:, 0:1], 0.0, None, ALU.is_ge).then_inc(lanes, 1)
                v.tensor_scalar(lane_x[:, 2:3], lane_x[:, 0:1], 0.0, None, ALU.is_lt).then_inc(lanes, 1)
                dve.wait_ge(lanes, 2)
                v.tensor_tensor(lane_x[:, 2:3], lane_x[:, 2:3], part[:, :], ALU.mult).then_inc(lanes, 1)
                dve.wait_ge(lanes, 3)

                def to_bucket(g, b):
                    dve.wait_ge(key_staged, g + 1)
                    if not (isinstance(g, int) and g < 2):
                        dve.wait_ge(bucket_copied, g - 1)
                        dve.wait_ge(summed, g - 1)
                    v.tensor_tensor(bucket[:, b, :, :], grid_a[:, :, :],
                                    stage_key[:, b, None, :].broadcast_to([P, NW, J]), ALU.is_equal).then_inc(bucketed, 1)

                def place_rows(g, b):
                    dve.wait_ge(permuted, g + 1)
                    v.tensor_tensor(place[b][:, :, :], grid_k[:, :, :],
                                    row_of[b][:, None, :].broadcast_to([P, P, J]), ALU.is_equal).then_inc(placed, 1)

                def copy_out(g, b):
                    dve.wait_ge(permuted, g + 3)
                    dve.wait_ge(stored[b], (g - b) * 8 + 16)
                    dve.wait_ge(rare_stored[b], (g - b) * 8 + 16)
                    v.tensor_copy(sorted_sb[b][:, :, :], ps_sorted[b][:, :, :]).then_inc(sorted_out, 1)

                def ended_before(g, b):
                    v.tensor_scalar(ended[:, :], nx_end[b][:, 0:NW - 1], lane_x[:, 0:1], None, ALU.is_le).then_inc(meta_steps, 1)

                def count_ended(g, b):
                    dve.wait_ge(meta_steps, g * 2 + 1)
                    v.tensor_reduce(ended_n[:, :], ended[:, :], AX.X, ALU.add).then_inc(meta_steps, 1)

                def column_tile(g, b):
                    dve.wait_ge(meta_steps, g * 2 + 2)
                    v.tensor_scalar(meta[b][:, 0:1], ended_n[:, :], lane_x[:, 1:2], lane_x[:, 2:3], ALU.mult, ALU.add).then_inc(meta_ready, 1)

                def table_of(g, b):
                    def window():
                        dve.wait_ge(staged, g + 1)
                        v.tensor_copy(meta[b][:, 2:4], stage_win[:, b, :].broadcast_to([P, 2]))
                    return [window, lambda: ended_before(g, b), lambda: count_ended(g, b), lambda: column_tile(g, b)]

                def counts(g, b, first, between):
                    done = [0]
                    between = list(between)

                    def step(ins):
                        ins.then_inc(count_steps, 1)
                        done[0] += 1
                        if between:
                            between.pop(0)()
                        dve.wait_ge(count_steps, g * COUNT_STEPS + done[0])

                    dve.wait_ge(based, g + 1)
                    step(v.tensor_scalar(nx_i[:, 0, :], ps_cnt[b][:, :], 128.0, -1.0, ALU.max, ALU.add))
                    step(v.tensor_scalar(nx_i[:, 1, :], nx_i[:, 0, :], 7, None, ALU.logical_shift_right))
                    step(v.tensor_copy(nx[:, 0, :], nx_i[:, 1, :]))
                    step(v.tensor_tensor_scan(nx_end[b][:, :], ones_f[:, :], nx[:, 0, :], 0.0, ALU.mult, ALU.add))
                    v.tensor_scalar(nx_all[:, :], nx_end[b][:, NW - 1:NW], float(3 - MAIN_X), None, ALU.add)
                    step(v.tensor_tensor(nx[:, 1, :], nx_end[b][:, :], nx[:, 0, :], ALU.subtract))
                    step(v.scalar_tensor_tensor(nx[:, 2, :], nx[:, 1, :], float(RB), tile_rb[:, :], ALU.mult, ALU.add))
                    if not first:
                        dve.wait_ge(meta_stored[b], (g - b) * 8)
                        dve.wait_ge(rare_seen, g - 1)
                    v.tensor_scalar(meta[b][:, 1:2], nx_all[:, :], 2, None, ALU.logical_shift_right).then_inc(rare_ready, 1)
                    v.tensor_tensor(resets[:, :, 0], nx[:, 2, :], ps_base[b][:, :], ALU.add).then_inc(resets_set, 1)
                    dve.wait_ge(rare_ready, g + 1)
                    step(v.tensor_tensor(rare_max[:, :], rare_max[:, :], meta[b][:, 1:2], ALU.max))
                    for f in between:
                        f()
                    assert done[0] == COUNT_STEPS

                def scan(g, b):
                    dve.wait_ge(resets_set, g + 1)
                    v.tensor_tensor_scan(ranks[:, :, :].rearrange("p a j -> p (a j)"),
                                         resets[:, :, :].rearrange("p a j -> p (a j)"),
                                         bucket[:, b, :, :].rearrange("p a j -> p (a j)"),
                                         0.0, ALU.max, ALU.add).then_inc(scanned, 1)
                    dve.wait_ge(scanned, g + 1)
                    v.tensor_tensor(picked[:, 0:PICK, :], ranks[:, 0:PICK, :], bucket[:, b, 0:PICK, :], ALU.mult).then_inc(picked_ready, 1)

                def rows_and_slots(g, b, waited):
                    done = [0]

                    def step(ins):
                        ins.then_inc(steps, 1)
                        done[0] += 1
                        return done[0]

                    def after(number):
                        dve.wait_ge(steps, g * RANK_STEPS + number)

                    if not waited:
                        dve.wait_ge(summed, g + 1)
                    a = step(v.tensor_reduce(rank[:, :], ps_rank[:, :, :].rearrange("p a j -> p j a"), AX.X, ALU.add))
                    after(a)
                    a = step(v.tensor_scalar(fields[:, 0, :], rank[:, :], -1.0, None, ALU.add))
                    after(a)
                    v.tensor_scalar(fields[:, 1, :], fields[:, 0, :], 127, None, ALU.bitwise_and)
                    q = step(v.tensor_scalar(fields[:, 4, :], fields[:, 0, :], RB - 1, None, ALU.bitwise_and))
                    v.tensor_scalar(fields[:, 2, :], fields[:, 0, :], 13, None, ALU.arith_shift_right)
                    after(q)
                    q = step(v.tensor_scalar(fields[:, 3, :], fields[:, 4, :], 7, None, ALU.arith_shift_right))
                    v.tensor_copy(row_of[b][:, :], fields[:, 1, :])
                    after(q)
                    m = step(v.tensor_scalar(is_main[:, :], fields[:, 3, :], 0.0, None, ALU.is_equal))
                    x = step(v.tensor_tensor(xslot[b][:, :], fields[:, 2, :], fields[:, 3, :], ALU.add))
                    dve.wait_ge(staged, g + 1)
                    after(m)
                    v.tensor_tensor(low_main[b][:, :, :], stage_low[:, b, :, :],
                                    is_main[:, None, :].broadcast_to([P, 2, J]), ALU.mult).then_inc(main_ready, 1)
                    e = step(v.scalar_tensor_tensor(is_extra[:, :], rank[:, :], 0.0, is_main[:, :], ALU.is_gt, ALU.is_gt))
                    after(x)
                    v.tensor_tensor(xslot[b][:, :], xslot[b][:, :], stage_tile[:, b, :], ALU.subtract).then_inc(stage_free_dve, 1)
                    after(e)
                    dve.wait_ge(stage_free_dve, g + 3)
                    x = step(v.tensor_tensor(xslot[b][:, :], xslot[b][:, :], is_extra[:, :], ALU.mult))
                    after(x)
                    v.tensor_tensor(extra[b][:, :, :], grid_x[:, :, :],
                                    xslot[b][:, None, :].broadcast_to([P, MAIN_X, J]), ALU.is_equal).then_inc(extra_ready, 1)
                    dve.sem_inc(passed, 1)
                    assert done[0] == RANK_STEPS

                def group(g, b, before, behind):
                    scan(g, b)
                    if before:
                        place_rows(g - 1, 1 - b)
                    others = table_of(g, b)
                    if before == 2:
                        others.append(lambda: copy_out(g - 2, b))
                    if behind:
                        counts(g + 1, 1 - b, before == 0, others)
                    else:
                        for f in others:
                            f()
                    if behind == 2:
                        to_bucket(g + 2, b)
                    rows_and_slots(g, b, behind == 2)

                for b in range(2):
                    to_bucket(b, b)
                counts(0, 0, True, [])
                n = over_groups(dve, group)
                place_rows(n * 2 - 1, 1)
                copy_out(n * 2 - 2, 0)
                copy_out(n * 2 - 1, 1)
                v.tensor_scalar(left_f[:, 0:1], rare_max[0:1, :], 0.0, None, ALU.is_gt)
                v.tensor_scalar(left_f[:, 1:2], row[0:1, 2 * NW + 2:2 * NW + 3], float(KEPT), None, ALU.is_gt).then_inc(lanes, 1)
                dve.wait_ge(lanes, 4)
                v.tensor_tensor(left[:, :], left_f[:, 0:1], left_f[:, 1:2], ALU.max)

            @block.tensor
            def _(pe):
                def base(g, b):
                    pe.wait_ge(bucketed, g + 3)
                    if not (isinstance(g, int) and g < 2):
                        pe.wait_ge(resets_set, g - 1)
                    for j in range(J):
                        nc.tensor.matmul(ps_base[b][:, :], tri[:, :], bucket[:, b, :, j],
                                         start=(j == 0), stop=(j == J - 1))
                    for j in range(J):
                        last = nc.tensor.matmul(ps_cnt[b][:, :], ones[:, :], bucket[:, b, :, j],
                                                start=(j == 0), stop=(j == J - 1))
                    last.then_inc(based, 1)

                def permute(g, b):
                    pe.wait_ge(placed, g + 1)
                    pe.wait_ge(cargoed, g + 3)
                    pe.wait_ge(stage_free_pool, g + 3)
                    pe.wait_ge(sorted_out, g + 1)
                    for j in range(J):
                        last = nc.tensor.matmul(ps_sorted[b][:, :, :], place[b][:, :, j], cargo[b][:, :, :, j],
                                                start=(j == 0), stop=(j == J - 1))
                    last.then_inc(permuted, 1)

                def group(g, b, before, behind):
                    pe.wait_ge(picked_ready, g + 1)
                    pe.wait_ge(picked_by_pool, g + 1)
                    for i in range(NW // 7):
                        end = nc.tensor.matmul(ps_rank[:, :, :], ident[:, :], picked[:, 7 * i:7 * i + 7, :],
                                               start=(i == 0), stop=(i == NW // 7 - 1))
                    end.then_inc(summed, 1)
                    if behind == 2:
                        base(g + 2, b)
                    if before:
                        permute(g - 1, 1 - b)

                pe.sem_inc(permuted, 2)
                for b in range(2):
                    base(b, b)
                n = over_groups(pe, group)
                permute(n * 2 - 1, 1)

            @block.sync
            def _(sp):
                def store_columns(g, b):
                    sp.wait_ge(sorted_out, g + 3)
                    sp.dma_start(dram["main"][bass.ds(g, 1), :, :].rearrange("o p (k s) -> (o p) k s", k=2),
                                 sorted_sb[b][:, :, 0:MAIN]).then_inc(stored[b], 16)
                    sp.dma_start(dram["rare"][bass.ds(g, 1), :, :].rearrange("o p (k s) -> (o p) k s", k=2),
                                 sorted_sb[b][:, :, MAIN:SLOTS]).then_inc(rare_stored[b], 16)

                def store(g, b, before, behind):
                    sp.wait_ge(meta_ready, g + 1)
                    sp.dma_start(dram["meta"][bass.ds(g, 1), :, :].rearrange("o p k -> (o p) k"),
                                 meta[b][:, :]).then_inc(meta_stored[b], 16)
                    if before == 2:
                        store_columns(g - 2, b)

                for b in range(2):
                    sp.sem_inc(stored[b], 16)
                    sp.sem_inc(rare_stored[b], 16)
                n = over_groups(sp, store)
                for b in range(2):
                    store_columns(n * 2 - 2 + b, b)
                for b in range(2):
                    sp.wait_ge(stored[b], n * 16 + 16)
                    sp.wait_ge(rare_stored[b], n * 16 + 16)
                    sp.wait_ge(meta_stored[b], n * 16)
                sp.sem_inc(passed, 1)


def known_pairs(eng, row):
    return eng.value_load(row[0:1, 2 * NW + 1:2 * NW + 2], min_val=NW // 2 - 2, max_val=KEPT // 2 - 2) + 2


def over_pairs(eng, row, body):
    n = known_pairs(eng, row)
    for b in range(2):
        body(b, b)
    with eng.Fori(1, n) as i:
        for b in range(2):
            body(i * 2 + b, b)
    return n


def aggregate(nc, tag, dram, row, parts, width, acc, build):
    with Phase(nc, tag) as ph:
        B = MAIN_BLOCKS
        RING = 4
        LAG = 3
        PIECE = 4
        PIECES = -(-B // PIECE)
        BY_POOL = B // 2
        assert (B - 1) % RING == 0
        metas = [ph.sb(f"metas{i}", [1, P, 4], I32) for i in range(2)]
        cnts = [ph.sb(f"cnts{i}", [P, MAIN, P], BF16) for i in range(2)]
        xtiles = [ph.sb(f"xtiles{i}", [P, MAIN_X, 3 * width], BF16) for i in range(2)]
        total = [ph.sb(f"total{i}", [P, width]) for i in range(2)]
        ps_out = [ph.ps(f"ps_out{i}", [P, 3, width]) for i in range(2)]
        meta_in = [ph.sem(f"meta_in{i}") for i in range(2)]
        meta_seen = ph.sem("meta_seen")
        tiles_ready = ph.sem("tiles_ready")
        group_out = ph.sem("group_out")
        totalled = ph.sem("totalled")
        added = ph.sem("added")
        if build:
            grid4 = ph.sb("grid4", [P, P, 4], BF16)
            lists = [ph.sb(f"lists{i}", [P, 2, MAIN], BF16) for i in range(2)]
            hot = [ph.sb(f"hot{i}", [P, 2, P, 4], BF16) for i in range(RING + 1)]
            ps_cnts = [ph.ps(f"ps_cnts{i}", [P, 4, P]) for i in range(RING + 1)]
            ramp = ph.sb("ramp", [P, P], BF16)
            pool_hot = ph.sb("pool_hot", [P, 2, 4, P], BF16)
            pool_list = ph.sb("pool_list", [P, 2, 4])
            pool_list_ready = ph.sem("pool_list_ready")
            pool_hot_ready = ph.sem("pool_hot_ready")
            grid_ready = ph.sem("grid_ready")
            list_in = [ph.sem(f"list_in{i}") for i in range(2)]
            hot_ready = ph.sem("hot_ready")
            cnt_ready = ph.sem("cnt_ready")
            cnt_copied = ph.sem("cnt_copied")
            kept = [ph.sem(f"kept{i}") for i in range(2)]
        else:
            piece_in = [[ph.sem(f"piece_in{i}_{p}") for p in range(PIECES)] for i in range(2)]
            piece_used = ph.sem("piece_used")

        def at_start(g, upto):
            return isinstance(g, int) and g < upto

        def slot(k):
            return k % RING if k < B - 1 else RING

        def earlier(g, k):
            if k == B - 1:
                return g * B
            return g * B + k - RING + (1 if k >= RING else 0)

        def unused(g, k):
            return at_start(g, 1) and (k < RING or k == B - 1)

        def by_vector(g, k):
            return g * (B - 1) + k + (0 if k > BY_POOL else 1)

        def columns(k):
            return range(4 * k, min(4 * k + 4, MAIN))

        def tile(b, c):
            return parts[:, c, :, :] if c < NW else xtiles[b][:, c - NW, :]

        with nc.Block() as block:
            @block.sync
            def _(sp):
                def load(g, b):
                    if build:
                        if not at_start(g, 2):
                            sp.wait_ge(hot_ready, (g - 1) * (B - 1))
                            sp.wait_ge(pool_list_ready, g - 1)
                        sp.dma_start(lists[b][:, :, :].rearrange("p k s -> p (k s)"),
                                     dram["main"][bass.ds(g, 1), :, :].rearrange("o p k -> (o p) k")).then_inc(list_in[b], 16)
                    if not at_start(g, 2):
                        sp.wait_ge(added, g - 1)
                    sp.dma_start(metas[b][:, :, :].rearrange("o p k -> o (p k)"),
                                 dram["meta"][bass.ds(g, 1), :, :].rearrange("o p k -> o (p k)")).then_inc(meta_in[b], 16)

                def load_counts(g, b):
                    for p in range(PIECES):
                        cs = slice(p * PIECE * 4, min(MAIN, (p + 1) * PIECE * 4))
                        if not at_start(g, 2):
                            if p < PIECES - 1:
                                sp.wait_ge(piece_used, (g - 2) * (PIECES - 1) + p + 1)
                            else:
                                sp.wait_ge(group_out, g - 1)
                        sp.dma_start(cnts[b][:, cs, :].rearrange("p c d -> p (c d)"),
                                     dram["counts"][bass.ds(g, 1), :, cs.start * P:cs.stop * P].rearrange("o p k -> (o p) k")
                                     ).then_inc(piece_in[b][p], 16)

                def both(g, b):
                    load_counts(g, b)
                    load(g, b)

                over_pairs(sp, row, load if build else both)

            @block.gpsimd
            def _(pool):
                if build:
                    kw = dict(allow_small_or_imprecise_dtypes=True)
                    nc.gpsimd.iota(grid4[:, :, :], [[1, P], [0, 4]], 1, 0, **kw).then_inc(grid_ready, 1)
                    nc.gpsimd.iota(ramp[:, :], [[1, P]], 1, 0, **kw).then_inc(grid_ready, 1)
                    pool.wait_ge(grid_ready, 2)

                def one_hots(g, b):
                    pool.wait_ge(list_in[b], (g - b) * 8 + 16)
                    if not at_start(g, 1):
                        pool.wait_ge(cnt_ready, (g - 1) * B + BY_POOL + 1)
                    pool.sem_inc(meta_seen, 1)
                    nc.gpsimd.tensor_copy(pool_list[:, :, :], lists[b][:, :, 4 * BY_POOL:4 * BY_POOL + 4]).then_inc(pool_list_ready, 1)
                    pool.wait_ge(pool_list_ready, g + 1)
                    pool.sem_inc(meta_seen, 1)
                    for side in range(2):
                        for c in range(4):
                            last = nc.gpsimd.tensor_scalar(pool_hot[:, side, c, :], ramp[:, :],
                                                           pool_list[:, side, c:c + 1], None, ALU.is_equal)
                    last.then_inc(pool_hot_ready, 1)

                def fetch_tiles(g, b):
                    pool.wait_ge(meta_in[b], (g - b) * 8 + 16)
                    pool.sem_inc(meta_seen, 1)
                    a = [pool.value_load(metas[b][0:1, NW + x, 0:1], min_val=0, max_val=NW - 1) for x in range(MAIN_X)]
                    if not at_start(g, 2):
                        pool.wait_ge(group_out, g - 1)
                    for x in range(MAIN_X):
                        last = nc.gpsimd.tensor_copy(
                            xtiles[b][:, x, :].bitcast(I32),
                            parts[:, bass.ds(a[x], 1), :, :].rearrange("p o t f -> p (o t f)").bitcast(I32))
                    last.then_inc(tiles_ready, 1)

                def hots_and_tiles(g, b):
                    one_hots(g, b)
                    fetch_tiles(g, b)

                over_pairs(pool, row, hots_and_tiles if build else fetch_tiles)

            @block.vector
            def _(dve):
                v = nc.vector
                wreg = dve.alloc_register(f"{tag}_window")

                def load_window(g, b):
                    dve.wait_ge(meta_in[b], (g - b) * 8 + 16)
                    dve.sem_inc(meta_seen, 1)
                    dve.reg_mov(wreg, dve.value_load(metas[b][0:1, 0, 2:3], min_val=0, max_val=NW - 1))

                def total_group(g, b):
                    dve.wait_ge(group_out, g + 1)
                    v.tensor_reduce(total[b][:, :], ps_out[b][:, :, :].rearrange("p t f -> p f t"), AX.X,
                                    ALU.add).then_inc(totalled, 1)

                def add_group(g, b):
                    w = dve.snap(wreg, min_val=0, max_val=NW - 1)
                    dve.wait_ge(totalled, g + 1)
                    to = acc[:, bass.ds(w, 1), :].rearrange("p o f -> p (o f)")
                    v.tensor_tensor(to, to, total[b][:, :], ALU.add).then_inc(added, 1)

                def one_hots(g, b):
                    dve.wait_ge(list_in[b], (g - b) * 8 + 16)
                    for k in range(B):
                        if k != BY_POOL:
                            if not unused(g, k):
                                dve.wait_ge(cnt_ready, earlier(g, k))
                            c = columns(k)
                            shape = [P, 2, P, len(c)]
                            v.tensor_tensor(hot[slot(k)][:, :, :, 0:len(c)], grid4[:, None, :, 0:len(c)].broadcast_to(shape),
                                            lists[b][:, :, None, c.start:c.stop].broadcast_to(shape),
                                            ALU.is_equal).then_inc(hot_ready, 1)
                        if k == LAG + 3 and not at_start(g, 1):
                            total_group(g - 1, 1 - b)
                        if k == LAG + 4 and not at_start(g, 1):
                            add_group(g - 1, 1 - b)
                        if k == LAG + 5:
                            load_window(g, b)

                def add_only(g, b):
                    load_window(g, b)
                    total_group(g, b)
                    add_group(g, b)

                if build:
                    dve.wait_ge(grid_ready, 1)
                    n = over_pairs(dve, row, one_hots)
                    total_group(n * 2 - 1, 1)
                    add_group(n * 2 - 1, 1)
                else:
                    over_pairs(dve, row, add_only)

            @block.tensor
            def _(pe):
                def use(g, b, k):
                    if build:
                        pe.wait_ge(cnt_copied, g * B + k + 1)
                    elif k % PIECE == 0:
                        pe.wait_ge(piece_in[b][k // PIECE], (g - b) * 8 + 16)
                    if k == 0 and not at_start(g, 2):
                        pe.wait_ge(added, g - 1)
                    if k == B - 1:
                        pe.wait_ge(tiles_ready, g + 1)
                    for c in columns(k):
                        last = nc.tensor.matmul(ps_out[b][:, :, :], cnts[b][:, c, :], tile(b, c),
                                                start=(c == 0), stop=(c == MAIN - 1))
                    if k == B - 1:
                        last.then_inc(group_out, 1)
                    elif not build and k % PIECE == PIECE - 1:
                        last.then_inc(piece_used, 1)

                def count_and_use(g, b):
                    for k in range(B):
                        if k == BY_POOL:
                            pe.wait_ge(pool_hot_ready, g + 1)
                            hots = [pool_hot[:, side, :, :].rearrange("p c d -> p d c") for side in range(2)]
                        else:
                            pe.wait_ge(hot_ready, by_vector(g, k))
                            hots = [hot[slot(k)][:, side, :, :] for side in range(2)]
                        if not unused(g, k):
                            pe.wait_ge(cnt_copied, earlier(g, k))
                        for c in range(len(columns(k))):
                            last = nc.tensor.matmul(ps_cnts[slot(k)][:, c, :], hots[0][:, :, c], hots[1][:, :, c],
                                                    start=True, stop=True)
                        last.then_inc(cnt_ready, 1)
                        if k >= LAG:
                            use(g, b, k - LAG)
                        elif not at_start(g, 1):
                            use(g - 1, 1 - b, B - LAG + k)

                def use_all(g, b):
                    for k in range(B):
                        use(g, b, k)

                if build:
                    n = over_pairs(pe, row, count_and_use)
                    for k in range(B - LAG, B):
                        use(n * 2 - 1, 1, k)
                else:
                    over_pairs(pe, row, use_all)

            if build:
                @block.scalar
                def _(act):
                    def copy_counts(g, b):
                        if not at_start(g, 2):
                            act.wait_ge(group_out, g - 1)
                            act.wait_ge(kept[b], (g - b) * 8)
                        for k in range(B):
                            act.wait_ge(cnt_ready, g * B + k + 1)
                            c = columns(k)
                            nc.scalar.activation(cnts[b][:, c.start:c.stop, :], ps_cnts[slot(k)][:, 0:len(c), :],
                                                 ACT.Identity).then_inc(cnt_copied, 1)
                        act.wait_ge(cnt_copied, g * B + B)
                        act.dma_start(dram["counts"][bass.ds(g, 1), :, :].rearrange("o p k -> (o p) k"),
                                      cnts[b][:, :, :].rearrange("p c d -> p (c d)")).then_inc(kept[b], 16)

                    n = over_pairs(act, row, copy_counts)
                    for b in range(2):
                        act.wait_ge(kept[b], n * 16)
                    act.sem_inc(meta_seen, 1)


def aggregate_rest(nc, tag, dram, row, left, parts, width, acc):
    with Phase(nc, tag) as ph:
        meta = ph.sb("meta", [1, P, 4], I32)
        grid4 = ph.sb("grid4", [P, P, 4], BF16)
        cols = ph.sb("cols", [P, 2, SLOTS], BF16)
        hot = ph.sb("hot", [P, 2, P, 4], BF16)
        cnts = ph.sb("cnts", [P, 4, P], BF16)
        total = ph.sb("total", [P, width])
        ps_cnts = ph.ps("ps_cnts", [P, 4, P])
        ps_out = ph.ps("ps_out", [P, 3, width])
        grid_ready = ph.sem("grid_ready")
        meta_in = ph.sem("meta_in")
        cols_in = ph.sem("cols_in")
        passed = ph.sem("passed")
        hot_ready = ph.sem("hot_ready")
        cnt_ready = ph.sem("cnt_ready")
        cnt_copied = ph.sem("cnt_copied")
        block_out = ph.sem("block_out")
        totalled = ph.sem("totalled")
        added = ph.sem("added")
        seen = {e: ph.sem(f"{e}_seen") for e in ("sp", "dve", "act", "pe")}

        def over_rest(eng, name, of_group, of_block):
            def registers(what):
                r = eng.alloc_register(f"{tag}_{name}_{what}")
                eng.reg_mov(r, 1)
                return r, lambda: eng.snap(r, min_val=1, max_val=1 << 24)

            (block_r, block_no), (group_r, group_no) = registers("blocks"), registers("groups")
            any_left = eng.value_load(left[0:1, 0:1], min_val=0, max_val=1)

            def groups(lo, hi, first_column, main_blocks):
                with eng.Fori(lo, hi) as g:
                    if name == "sp":
                        for s in seen.values():
                            eng.wait_ge(s, g + 1)
                        eng.dma_start(meta[:, :, :].rearrange("o p k -> o (p k)"),
                                      dram["meta"][bass.ds(g, 1), :, :].rearrange("o p k -> o (p k)")).then_inc(meta_in, 16)
                    eng.wait_ge(meta_in, g * 16 + 16)
                    eng.sem_inc(passed, 1)
                    blocks = eng.value_load(meta[0:1, 0, 1:2], min_val=0, max_val=RARE_BLOCKS) + main_blocks
                    with eng.If(blocks > 0):
                        of_group(g, group_no(), block_no())
                        eng.reg_add(group_r, group_r, 1)
                        with eng.Fori(0, blocks) as t:
                            of_block(t * 4 + first_column, block_no())
                            eng.reg_add(block_r, block_r, 1)
                    eng.sem_inc(seen[name], 1)

            with eng.If(any_left > 0):
                n = known_pairs(eng, row)
                groups(0, n * 2, MAIN, 0)
                more = eng.value_load(row[0:1, 2 * NW + 2:2 * NW + 3], min_val=0, max_val=GMAX)
                with eng.If(more > KEPT):
                    groups(KEPT, more, 0, MAIN_BLOCKS)

        with nc.Block() as block:
            @block.gpsimd
            def _(pool):
                any_left = pool.value_load(left[0:1, 0:1], min_val=0, max_val=1)
                with pool.If(any_left > 0):
                    nc.gpsimd.iota(grid4[:, :, :], [[1, P], [0, 4]], 1, 0,
                                   allow_small_or_imprecise_dtypes=True).then_inc(grid_ready, 1)
                for s in seen.values():
                    pool.sem_inc(s, 1)
                pool.sem_inc(added, 1)

            @block.sync
            def _(sp):
                def load_columns(g, number, m):
                    sp.wait_ge(added, m)
                    sp.dma_start(cols[:, :, 0:MAIN],
                                 dram["main"][bass.ds(g, 1), :, :].rearrange("o p (k s) -> (o p) k s", k=2)).then_inc(cols_in, 16)
                    sp.dma_start(cols[:, :, MAIN:SLOTS],
                                 dram["rare"][bass.ds(g, 1), :, :].rearrange("o p (k s) -> (o p) k s", k=2)).then_inc(cols_in, 16)

                over_rest(sp, "sp", load_columns, lambda column, m: None)

            @block.vector
            def _(dve):
                v = nc.vector
                wreg = dve.alloc_register(f"{tag}_window")
                dve.reg_mov(wreg, 0)

                def start(g, number, m):
                    dve.reg_mov(wreg, dve.value_load(meta[0:1, 0, 2:3], min_val=0, max_val=NW - 1))
                    dve.wait_ge(grid_ready, 1)
                    dve.wait_ge(cols_in, number * 32)
                    dve.sem_inc(passed, 1)

                def add_block(column, m):
                    w = dve.snap(wreg, min_val=0, max_val=NW - 1)
                    v.tensor_tensor(hot[:, :, :, :], grid4[:, None, :, :].broadcast_to([P, 2, P, 4]),
                                    cols[:, :, None, bass.ds(column, 4)].broadcast_to([P, 2, P, 4]),
                                    ALU.is_equal).then_inc(hot_ready, 1)
                    dve.wait_ge(block_out, m)
                    v.tensor_reduce(total[:, :], ps_out[:, :, :].rearrange("p t f -> p f t"), AX.X,
                                    ALU.add).then_inc(totalled, 1)
                    dve.wait_ge(totalled, m)
                    to = acc[:, bass.ds(w, 1), :].rearrange("p o f -> p (o f)")
                    v.tensor_tensor(to, to, total[:, :], ALU.add).then_inc(added, 1)
                    dve.wait_ge(added, m + 1)
                    dve.sem_inc(passed, 1)

                over_rest(dve, "dve", start, add_block)

            @block.scalar
            def _(act):
                def copy_counts(column, m):
                    act.wait_ge(cnt_ready, m)
                    nc.scalar.activation(cnts[:, :, :], ps_cnts[:, :, :], ACT.Identity).then_inc(cnt_copied, 1)

                over_rest(act, "act", lambda g, number, m: None, copy_counts)

            @block.tensor
            def _(pe):
                def use(column, m):
                    pe.wait_ge(hot_ready, m)
                    for c in range(4):
                        last = nc.tensor.matmul(ps_cnts[:, c, :], hot[:, 0, :, c], hot[:, 1, :, c], start=True, stop=True)
                    last.then_inc(cnt_ready, 1)
                    tiles = []
                    for c in range(4):
                        a = pe.value_load(meta[0:1, bass.ds(column + c, 1), 0:1].rearrange("o s k -> o (s k)"),
                                          min_val=0, max_val=NW - 1)
                        tiles.append(parts[:, bass.ds(a, 1), :, :].rearrange("p o t f -> p (o t) f"))
                    pe.wait_ge(cnt_copied, m)
                    for c in range(4):
                        last = nc.tensor.matmul(ps_out[:, :, :], cnts[:, c, :], tiles[c], start=(c == 0), stop=(c == 3))
                    last.then_inc(block_out, 1)

                over_rest(pe, "pe", lambda g, number, m: None, use)


SHARES = [slice(NWP * i // 4, NWP * (i + 1) // 4) for i in range(4)]


def in_turn(stages):
    for t in range(len(SHARES) + len(stages) - 1):
        for s in reversed(range(len(stages))):
            if 0 <= t - s < len(SHARES):
                stages[s](t - s, SHARES[t - s])


class Splitter:

    def __init__(self, nc, ph, x, parts, scratch):
        self.nc, self.x, self.parts, self.scratch = nc, x, parts, scratch
        self.first, self.rest, self.second, self.third = (
            ph.sem(n) for n in ("part0_ready", "rest_ready", "part1_ready", "part2_ready"))

    def part0(self, act, q, w):
        self.nc.scalar.activation(self.parts[:, w, 0, :], self.x[:, w, :], ACT.Identity).then_inc(self.first, 1)

    def subtract0(self, dve, q, w):
        dve.wait_ge(self.first, q + 1)
        self.nc.vector.tensor_tensor(self.scratch[:, w, :], self.x[:, w, :], self.parts[:, w, 0, :],
                                     ALU.subtract).then_inc(self.rest, 1)

    def part1(self, act, q, w):
        act.wait_ge(self.rest, q + 1)
        self.nc.scalar.activation(self.parts[:, w, 1, :], self.scratch[:, w, :], ACT.Identity).then_inc(self.second, 1)

    def part2(self, pool, q, w):
        pool.wait_ge(self.second, q + 1)
        self.nc.gpsimd.tensor_tensor(self.parts[:, w, 2, :], self.scratch[:, w, :], self.parts[:, w, 1, :],
                                     ALU.subtract).then_inc(self.third, 1)


def normalize(nc, tag, x, out, scratch, parts=None):
    with Phase(nc, tag) as ph:
        stats = ph.sb("stats", [P, 5, NWP])
        eps = ph.sb("eps", [P, 1])
        eps_set = ph.sem("eps_set")
        summed = ph.sem("summed")
        averaged = ph.sem("averaged")
        centred = ph.sem("centred")
        squared = ph.sem("squared")
        squares_summed = ph.sem("squares_summed")
        rooted = ph.sem("rooted")
        inverted = ph.sem("inverted")
        normalized = ph.sem("normalized")
        split = Splitter(nc, ph, out, parts, scratch) if parts is not None else None

        def wide(row, w):
            return stats[:, row, w, None].broadcast_to([P, w.stop - w.start, F])

        with nc.Block() as block:
            @block.vector
            def _(dve):
                v = nc.vector

                def total(q, w):
                    v.tensor_reduce(stats[:, 0, w], x[:, w, :], AX.X, ALU.add).then_inc(summed, 1)

                def mean(q, w):
                    dve.wait_ge(summed, q + 1)
                    v.tensor_scalar(stats[:, 1, w], stats[:, 0, w], 1.0 / F, None, ALU.mult).then_inc(averaged, 1)

                def centre(q, w):
                    dve.wait_ge(averaged, q + 1)
                    v.tensor_tensor(out[:, w, :], x[:, w, :], wide(1, w), ALU.subtract).then_inc(centred, 1)

                def squares(q, w):
                    dve.wait_ge(squared, q + 1)
                    v.tensor_reduce(stats[:, 2, w], scratch[:, w, :], AX.X, ALU.add).then_inc(squares_summed, 1)

                def invert(q, w):
                    dve.wait_ge(rooted, q + 1)
                    v.reciprocal(stats[:, 4, w], stats[:, 3, w]).then_inc(inverted, 1)

                def scale(q, w):
                    dve.wait_ge(inverted, q + 1)
                    v.scalar_tensor_tensor(out[:, w, :], out[:, w, :], 0.0, wide(4, w), ALU.max, ALU.mult).then_inc(normalized, 1)

                v.memset(eps[:, :], 1e-5).then_inc(eps_set, 1)
                in_turn([total, mean, centre, squares, invert, scale] +
                        ([lambda q, w: split.subtract0(dve, q, w)] if split else []))

            @block.gpsimd
            def _(pool):
                def square(q, w):
                    pool.wait_ge(centred, q + 1)
                    nc.gpsimd.tensor_tensor(scratch[:, w, :], out[:, w, :], out[:, w, :], ALU.mult).then_inc(squared, 1)

                in_turn([square])
                if split:
                    in_turn([lambda q, w: split.part2(pool, q, w)])

            @block.scalar
            def _(act):
                def root(q, w):
                    act.wait_ge(squares_summed, q + 1)
                    nc.scalar.activation(stats[:, 3, w], stats[:, 2, w], ACT.Sqrt, bias=eps[:, 0:1], scale=1.0 / F).then_inc(rooted, 1)

                def part0(q, w):
                    act.wait_ge(normalized, q + 1)
                    split.part0(act, q, w)

                act.wait_ge(eps_set, 1)
                in_turn([root] + ([part0, lambda q, w: split.part1(act, q, w)] if split else []))


def split_parts(nc, tag, x, parts, scratch):
    with Phase(nc, tag) as ph:
        split = Splitter(nc, ph, x, parts, scratch)
        with nc.Block() as block:
            @block.scalar
            def _(act):
                in_turn([lambda q, w: split.part0(act, q, w), lambda q, w: split.part1(act, q, w)])

            @block.vector
            def _(dve):
                in_turn([lambda q, w: split.subtract0(dve, q, w)])

            @block.gpsimd
            def _(pool):
                in_turn([lambda q, w: split.part2(pool, q, w)])


def perceptron(nc, tag, ident, x, hidden, last, width, finish):
    with Phase(nc, tag) as ph:
        k = x.shape[2]
        xt = [ph.sb(f"xt{i}", [k, 4 * P]) for i in range(2)]
        hid = [[ph.sb(f"hid{i}_{n}", [P, 4 * P]) for n in range(len(hidden))]
               for i in range(2)]
        ps_t = [ph.ps(f"ps_t{i}", [k, 4, P]) for i in range(2)]
        ps_h = [ph.ps(f"ps_h{i}", [P, 4 * P]) for i in range(2)]
        ps_f = [ph.ps(f"ps_f{i}", [P, 4, width]) for i in range(2)]
        xs = [ph.sb(f"xs{i}", [P, 4, k]) for i in range(2)]
        fetched = ph.sem("fetched")
        seen = ph.sem("fetched_seen")
        turned = ph.sem("turned")
        copied = ph.sem("turned_copied")
        product = [ph.sem(f"product{n}") for n in range(len(hidden))]
        relued = [ph.sem(f"relued{n}") for n in range(len(hidden))]
        last_product = ph.sem("last_product")
        finished = ph.sem("finished")
        finishing = ph.sem("finishing")

        def over_batches(eng, stages, ahead=()):
            def pair(n, now, next_):
                for s in stages:
                    for b in range(next_ if s in ahead else now):
                        s(n + (2 if s in ahead else 0) + b, b)

            full = NB4 // 2
            for s in ahead:
                for b in range(2):
                    s(b, b)
            with eng.Fori(0, full - 1) as i:
                pair(i * 2, 2, 2)
            pair(full * 2 - 2, 2, NB4 % 2)
            if NB4 % 2:
                pair(NB4 - 1, 1, 0)

        with nc.Block() as block:
            @block.tensor
            def _(pe):
                def turn(n, b):
                    pe.wait_ge(fetched, n + 1)
                    pe.sem_inc(seen, 1)
                    for c in range(4):
                        last_ = nc.tensor.transpose(ps_t[b][:, c, :], xs[b][:, c, :], ident[:, :])
                    last_.then_inc(turned, 1)

                def layer(m):
                    def run(n, b):
                        if m:
                            pe.wait_ge(relued[m - 1], n + 1)
                        else:
                            pe.wait_ge(copied, n + 3)
                        nc.tensor.matmul(ps_h[b][:, :], hidden[m][0], (hid[b][m - 1] if m else xt[b])[:, :],
                                         start=True, stop=True).then_inc(product[m], 1)
                    return run

                def back(n, b):
                    pe.wait_ge(relued[-1], n + 1)
                    pe.wait_ge(finished, n + 1)
                    for c in range(4):
                        last_ = nc.tensor.matmul(ps_f[b][:, c, :], hid[b][-1][:, c * P:(c + 1) * P], last,
                                                 start=True, stop=True)
                    last_.then_inc(last_product, 1)

                over_batches(pe, [layer(0), turn] + [layer(m) for m in range(1, len(hidden))] + [back], (turn,))

            @block.gpsimd
            def _(pool):
                pool.sem_inc(copied, 2)

                def fetch(n, b):
                    pool.wait_ge(copied, n + 1)
                    nc.gpsimd.tensor_copy(xs[b][:, :, :], x[:, bass.ds(n * 4, 4), :]).then_inc(fetched, 1)

                over_batches(pool, [fetch])

            @block.scalar
            def _(act):
                def relu(m):
                    def run(n, b):
                        act.wait_ge(product[m], n + 1)
                        nc.scalar.activation(hid[b][m][:, :], ps_h[b][:, :], ACT.Relu, bias=hidden[m][1]).then_inc(relued[m], 1)
                    return run

                over_batches(act, [relu(m) for m in range(len(hidden))])

            @block.vector
            def _(dve):
                dve.sem_inc(finished, 2)

                def copy(n, b):
                    dve.wait_ge(turned, n + 1)
                    nc.vector.tensor_copy(xt[b][:, :].rearrange("p (c e) -> p c e", c=4), ps_t[b][:, :, :]).then_inc(copied, 1)

                def end(n, b):
                    dve.wait_ge(last_product, n + 1)
                    finish(dve, n, ps_f[b], finishing).then_inc(finished, 1)

                over_batches(dve, [copy, end], (copy,))


_INS = ["x", "src", "dst",
        "L0_gnn_W1", "L0_gnn_b1", "L0_gnn_W2", "L0_gnn_b2", "L0_gnn_W3", "L0_gnn_b3", "L0_gnn_W4", "L0_gnn_b4",
        "L1_gnn_WM1", "L1_gnn_bM1", "L1_gnn_WM2", "L1_gnn_bM2", "L1_gnn_WM3", "L1_gnn_bM3",
        "L1_gnn_WU1", "L1_gnn_bU1", "L1_gnn_WU2", "L1_gnn_bU2", "L1_gnn_WU3", "L1_gnn_bU3"]


def gnn(nc, a, out):
    with ExitStack() as ctx:
        def sb(name, shape, dt=FP32):
            return ctx.enter_context(nc.sbuf_tensor(name, shape, dt))

        dram = {
            "main": nc.dram_tensor("main_columns", [GMAX, P, 2 * MAIN], BF16).ap(),
            "rare": nc.dram_tensor("rare_columns", [GMAX, P, 2 * (SLOTS - MAIN)], BF16).ap(),
            "meta": nc.dram_tensor("group_tables", [GMAX, P, 4], I32).ap(),
            "window": nc.dram_tensor("window_table", [2 * NW], I32).ap(),
            "counts": nc.dram_tensor("edge_counts", [KEPT, P, MAIN * P], BF16).ap(),
        }

        row = sb("row", [1, 2 * NW + 3], I32)
        left = sb("left", [1, 1], I32)
        ident = sb("identity", [P, P])
        xres = sb("xres", [P, NWP, F])
        feat = sb("feat", [P, NWP, H])

        weight, bias = {}, {}
        LAST = ("L0_gnn_b2", "L0_gnn_b4", "L1_gnn_bM3", "L1_gnn_bU3")
        for name in _INS[3:]:
            if a[name].shape.__len__() == 2:
                weight[name] = sb("w_" + name, list(a[name].shape))
            elif name in LAST:
                bias[name] = sb("b_" + name, [P, a[name].shape[0]])
            else:
                bias[name] = sb("b_" + name, [a[name].shape[0], 1])

        whole = N // P
        loaded = ctx.enter_context(nc.semaphore("inputs_loaded"))
        loads = len(_INS) - 3 + 2
        zeroed = ctx.enter_context(nc.semaphore("padding_zeroed"))
        idx = ctx.enter_context(nc.semaphore("index_ready"))
        with nc.sbuf_tensor("ramp", [P, P], FP32) as ramp, nc.sbuf_tensor("lane", [P, 1], FP32) as lane, nc.Block() as block:
            @block.gpsimd
            def _(pool):
                nc.gpsimd.memset(xres[:, whole:NWP, :], 0.0).then_inc(zeroed, 1)
                kw = dict(allow_small_or_imprecise_dtypes=True)
                nc.gpsimd.iota(ramp[:, :], [[1, P]], 0, 0, **kw).then_inc(idx, 1)
                nc.gpsimd.iota(lane[:, :], [[0, 1]], 0, 1, **kw).then_inc(idx, 1)

            @block.vector
            def _(dve):
                dve.wait_ge(idx, 2)
                nc.vector.tensor_scalar(ident[:, :], ramp[:, :], lane[:, 0:1], None, ALU.is_equal).then_inc(idx, 1)
                dve.wait_ge(idx, 3)

        def load_rest(sp):
            sp.wait_ge(zeroed, 1)
            sp.dma_start(xres[:, 0:whole, :], a["x"][0:whole * P, :].rearrange("(w p) f -> p w f", p=P)).then_inc(loaded, 16)
            sp.dma_start(xres[0:N - whole * P, whole, :], a["x"][whole * P:N, :]).then_inc(loaded, 16)
            for name in _INS[3:]:
                if name in weight:
                    sp.dma_start(weight[name][:, :], a[name]).then_inc(loaded, 16)
                elif name in LAST:
                    w = a[name].shape[0]
                    sp.dma_start(bias[name][:, :], a[name].rearrange("(o f) -> o f", o=1).broadcast_to([P, w])
                                 ).then_inc(loaded, 16)
                else:
                    sp.dma_start(bias[name][:, :], a[name].rearrange("(f o) -> f o", o=1)).then_inc(loaded, 16)

        sort_edges(nc, "sort", a["src"], a["dst"], dram, row, left, load_rest)

        parts = sb("parts", [P, NWP, 3, H], BF16)
        parts64 = parts[:, :, :, :].rearrange("p w t f -> p (w t f)")[:, 0:NWP * 3 * F].rearrange(
            "p (w t f) -> p w t f", t=3, f=F)
        scratch = sb("scratch", [P, NWP, H])
        h64, z64 = feat[:, :, 0:F], feat[:, :, F:H]
        W, Bc = weight, bias

        def biased(name, out_of, width, relu=False):
            def finish(dve, n, ps, sem):
                v = nc.vector
                to = out_of[:, bass.ds(n * 4, 4), :]
                ins = v.tensor_tensor(to, ps[:, :, :], Bc[name][:, None, :].broadcast_to([P, 4, width]), ALU.add)
                if not relu:
                    return ins
                ins.then_inc(sem, 1)
                dve.wait_ge(sem, n + 1)
                return v.tensor_scalar(to, to, 0.0, None, ALU.max)
            return finish

        with nc.Block() as block:
            @block.sync
            def _(sp):
                sp.wait_ge(loaded, 16 * loads)

        normalize(nc, "norm0", xres[:, :, :], h64, scratch[:, :, 0:F], parts64)
        aggregate(nc, "sum0", dram, row, parts64, F, h64, build=True)
        aggregate_rest(nc, "sum0r", dram, row, left, parts64, F, h64)
        perceptron(nc, "mlp0", ident, h64, [(W["L0_gnn_W1"][:, :], Bc["L0_gnn_b1"][:, 0:1])], W["L0_gnn_W2"][:, :], H,
                   biased("L0_gnn_b2", feat[:, :, :], H, relu=True))
        split_parts(nc, "split1", feat[:, :, :], parts[:, :, :, :], scratch[:, :, :])
        aggregate(nc, "sum1", dram, row, parts[:, :, :, :], H, feat[:, :, :], build=False)
        aggregate_rest(nc, "sum1r", dram, row, left, parts[:, :, :, :], H, feat[:, :, :])
        perceptron(nc, "mlp1", ident, feat[:, :, :], [(W["L0_gnn_W3"][:, :], Bc["L0_gnn_b3"][:, 0:1])], W["L0_gnn_W4"][:, :], F,
                   residual(nc, Bc["L0_gnn_b4"], xres[:, :, :], xres[:, :, :], scratch[:, :, 0:F]))
        normalize(nc, "norm1", xres[:, :, :], h64, scratch[:, :, 0:F])
        perceptron(nc, "mlp2", ident, h64, [(W["L1_gnn_WM1"][:, :], Bc["L1_gnn_bM1"][:, 0:1]),
                                    (W["L1_gnn_WM2"][:, :], Bc["L1_gnn_bM2"][:, 0:1])], W["L1_gnn_WM3"][:, :], F,
                   biased("L1_gnn_bM3", z64, F))
        split_parts(nc, "split2", z64, parts64, scratch[:, :, 0:F])
        clear(nc, z64)
        aggregate(nc, "sum2", dram, row, parts64, F, z64, build=False)
        aggregate_rest(nc, "sum2r", dram, row, left, parts64, F, z64)
        perceptron(nc, "mlp3", ident, feat[:, :, :], [(W["L1_gnn_WU1"][:, :], Bc["L1_gnn_bU1"][:, 0:1]),
                                              (W["L1_gnn_WU2"][:, :], Bc["L1_gnn_bU2"][:, 0:1])], W["L1_gnn_WU3"][:, :], F,
                   residual(nc, Bc["L1_gnn_bU3"], xres[:, :, :], xres[:, :, :], scratch[:, :, 0:F]))

        stored = ctx.enter_context(nc.semaphore("result_stored"))
        with nc.Block() as block:
            @block.sync
            def _(sp):
                sp.dma_start(out[0:whole * P, :].rearrange("(w p) f -> p w f", p=P), xres[:, 0:whole, :]).then_inc(stored, 16)
                sp.dma_start(out[whole * P:N, :], xres[0:N - whole * P, whole, :]).then_inc(stored, 16)
                sp.wait_ge(stored, 32)


def residual(nc, bias, x, to, scratch):
    def finish(dve, n, ps, sem):
        v = nc.vector
        mid = scratch[:, bass.ds(n * 4, 4), :]
        v.tensor_tensor(mid, ps[:, :, :], bias[:, None, :].broadcast_to([P, 4, F]), ALU.add).then_inc(sem, 1)
        dve.wait_ge(sem, n + 1)
        return v.tensor_tensor(to[:, bass.ds(n * 4, 4), :], mid, x[:, bass.ds(n * 4, 4), :], ALU.add)
    return finish


def clear(nc, x):
    with nc.Block() as block:
        @block.vector
        def _(dve):
            nc.vector.memset(x, 0.0)


def kernel(**inputs):
    import concourse.bacc as bacc
    from concourse.bass_utils import run_bass_kernel_spmd

    nc = bacc.Bacc("TRN2", target_bir_lowering=False, num_devices=1)
    arrays, aps = {}, {}
    for name in _INS:
        arr = np.ascontiguousarray(inputs[name])
        arrays[f"in_{name}"] = arr
        aps[name] = nc.dram_tensor(f"in_{name}", arr.shape, mybir.dt.from_np(arr.dtype), kind="ExternalInput").ap()
    out = nc.dram_tensor("out", (N, F), FP32, kind="ExternalOutput").ap()
    gnn(nc, aps, out)
    r = run_bass_kernel_spmd(nc, [arrays], core_ids=[0])
    return r.results[0]["out"]
```
